# Optimizing a Trainium2 kernel written in Bass

```python
import numpy as np
import jax
import jax.numpy as jnp

def _softmax(x, axis=-1):
    return jax.nn.softmax(x, axis=axis)

def _gelu(x):
    return jax.nn.gelu(x, approximate=True)

def _silu(x):
    return jax.nn.silu(x)

def _sigmoid(x):
    return jax.nn.sigmoid(x)

def _layernorm(x, axis=-1, eps=1e-05):
    m = jnp.mean(x, axis=axis, keepdims=True)
    v = jnp.var(x, axis=axis, keepdims=True)
    return (x - m) / jnp.sqrt(v + eps)

def _scatter_add(tgt, idx, src, axis=0):
    return tgt.at[idx].add(src)

def _segment_sum(src, seg, n):
    return jax.ops.segment_sum(src, seg, n)
kernel_name = 'mk_early_fusion_embed_d4_tok_img256_r4_832a5e'

def setup_inputs(seed: int=0):
    np.random.seed(seed)
    _w = jnp.asarray

    def _rec_inputs():
        import jax
        import jax.numpy as jnp
        _rk = jax.random.key(seed)
        x = -0.000348152 + 1.00002 * jax.random.normal(jax.random.fold_in(_rk, 1), (8, 64, 96, 96), jnp.float32)
        x_txt = jax.random.randint(jax.random.fold_in(_rk, 51), (8, 128), 0, 24991, jnp.int32)
        return (x, x_txt)
    x, x_txt = _rec_inputs()

    def _L0_tok_setup():
        import jax, jax.numpy as jnp
        import numpy as np
        N_BATCH, CH, HW, KERNEL, STRIDE, VC = (8, 64, 96, 8, 3, 128)

        def _unfold(x, k, s):
            n, c, h, w = x.shape
            oh = (h - k) // s + 1
            ow = (w - k) // s + 1
            ih = (jnp.arange(oh) * s)[:, None] + jnp.arange(k)[None, :]
            iw = (jnp.arange(ow) * s)[:, None] + jnp.arange(k)[None, :]
            p = x[:, :, ih, :]
            p = p[:, :, :, :, iw]
            p = p.transpose(0, 2, 4, 1, 3, 5)
            return (p.reshape(n, oh * ow, c, k, k), oh * ow)
        key = jax.random.key(seed)
        k0, k1, k2, k3 = jax.random.split(key, 4)
        kk = KERNEL * KERNEL
        x = jax.random.normal(k0, (N_BATCH, CH, HW, HW), dtype=jnp.float32)
        conv_w = jax.random.normal(k1, (VC, CH), dtype=jnp.float32) * 0.05
        W1 = jax.random.normal(k2, (3 * CH, CH + kk), dtype=jnp.float32) * 0.02
        b1 = jnp.zeros((3 * CH,), dtype=jnp.float32)
        W2 = jax.random.normal(k3, (CH, 3 * CH), dtype=jnp.float32) * 0.02
        b2 = jnp.zeros((CH,), dtype=jnp.float32)
        return {'x': x, 'conv_w': conv_w, 'W1': W1, 'b1': b1, 'W2': W2, 'b2': b2}
    _L0_tok_all = _L0_tok_setup()
    _L0_tok_in = {k: v for k, v in _L0_tok_all.items() if k in ('conv_w', 'W1', 'b1', 'W2', 'b2')}
    del _L0_tok_all

    def _L0_txt_setup():
        import jax, jax.numpy as jnp
        import numpy as np
        VOCAB = 25000
        EMB_DIM = 75
        OUT_DIM = 64
        B, T = (32, 128)
        key = jax.random.key(seed)
        ks = jax.random.split(key, 8)
        scale = 0.02
        return {'tokens': jax.random.randint(ks[0], (B, T), 0, VOCAB, dtype=jnp.int32), 'E0': jax.random.normal(ks[1], (VOCAB, EMB_DIM), dtype=jnp.float32) * scale, 'E1': jax.random.normal(ks[2], (VOCAB, EMB_DIM), dtype=jnp.float32) * scale, 'W0': jax.random.normal(ks[3], (EMB_DIM, OUT_DIM), dtype=jnp.float32) * scale, 'b0': jnp.zeros((OUT_DIM,), dtype=jnp.float32), 'W1': jax.random.normal(ks[4], (EMB_DIM, OUT_DIM), dtype=jnp.float32) * scale, 'b1': jnp.zeros((OUT_DIM,), dtype=jnp.float32), 'Wa': jax.random.normal(ks[5], (OUT_DIM, 1), dtype=jnp.float32) * scale, 'ba': jnp.zeros((1,), dtype=jnp.float32)}
    _L0_txt_all = _L0_txt_setup()
    _L0_txt_in = {k: v for k, v in _L0_txt_all.items() if k in ('E0', 'E1', 'W0', 'b0', 'W1', 'b1', 'Wa', 'ba')}
    del _L0_txt_all

    def _L0_attn_setup():
        import jax, jax.numpy as jnp
        import numpy as np
        EPS = 1e-06

        def _rmsnorm(x, w):
            xf = x.astype(jnp.float32)
            y = xf * jax.lax.rsqrt(jnp.mean(xf * xf, axis=-1, keepdims=True) + EPS)
            return y.astype(x.dtype) * w
        key = jax.random.key(seed)
        k0, k1, k2 = jax.random.split(key, 3)
        B, T, C = (2, 256, 64)
        x = jax.random.normal(k0, (B, T, C), jnp.float32)
        w_qkv = jax.random.normal(k1, (3 * C, C), jnp.float32) / np.float32(np.sqrt(C))
        w_proj = jax.random.normal(k2, (C, C), jnp.float32) / np.float32(np.sqrt(C))
        qn_w = jnp.ones((2,), jnp.float32)
        kn_w = jnp.ones((2,), jnp.float32)
        return {'x': x, 'w_qkv': w_qkv, 'w_proj': w_proj, 'qn_w': qn_w, 'kn_w': kn_w}
    _L0_attn_all = _L0_attn_setup()
    _L0_attn_in = {k: v for k, v in _L0_attn_all.items() if k in ('w_qkv', 'w_proj', 'qn_w', 'kn_w')}
    del _L0_attn_all

    def _L0_ffn_setup():
        import jax, jax.numpy as jnp
        import numpy as np
        NUM_EXPERTS = 8
        TOP_K = 2
        B, S, D = (8, 2048, 64)

        def _moe(tokens, router_w, w1, b1, w2, b2):
            N = tokens.shape[0]
            E = router_w.shape[0]
            logits = tokens.astype(jnp.float32) @ router_w.astype(jnp.float32).T
            probs = jax.nn.softmax(logits, axis=-1)
            rw, re = jax.lax.top_k(probs, TOP_K)
            if TOP_K > 1:
                rw = rw / jnp.maximum(rw.sum(-1, keepdims=True), 1e-12)
            rw = rw.astype(tokens.dtype)
            combine = jnp.zeros((N, E), tokens.dtype).at[jnp.arange(N)[:, None], re].set(rw)
            out = tokens
            for e in range(E):
                h = jax.nn.gelu(tokens @ w1[e] + b1[e], approximate=False)
                y = h @ w2[e] + b2[e]
                out = out + combine[:, e:e + 1] * y
            return out
        key = jax.random.key(seed)
        ks = jax.random.split(key, 4)
        scale = 1.0 / np.sqrt(D).astype(np.float32)
        return {'input_embeddings': jax.random.normal(ks[0], (B, S, D), jnp.float32), 'router_w': jax.random.normal(ks[1], (NUM_EXPERTS, D), jnp.float32) * scale, 'w1': jax.random.normal(ks[2], (NUM_EXPERTS, D, D), jnp.float32) * scale, 'b1': jnp.zeros((NUM_EXPERTS, D), jnp.float32), 'w2': jax.random.normal(ks[3], (NUM_EXPERTS, D, D), jnp.float32) * scale, 'b2': jnp.zeros((NUM_EXPERTS, D), jnp.float32)}
    _L0_ffn_all = _L0_ffn_setup()
    _L0_ffn_in = {k: v for k, v in _L0_ffn_all.items() if k in ('router_w', 'w1', 'b1', 'w2', 'b2')}
    del _L0_ffn_all

    def _L1_attn_setup():
        import jax, jax.numpy as jnp
        import numpy as np
        key = jax.random.key(seed)
        ks = jax.random.split(key, 4)
        B, S, D = (4, 1024, 64)
        x = jax.random.normal(ks[0], (B, S, D), dtype=jnp.float32)
        Wq = jax.random.normal(ks[1], (D, D), dtype=jnp.float32) * 0.02
        Wk = jax.random.normal(ks[2], (D, D), dtype=jnp.float32) * 0.02
        Wv = jax.random.normal(ks[3], (D, D), dtype=jnp.float32) * 0.02
        bq = jnp.zeros((D,), dtype=jnp.float32)
        bk = jnp.zeros((D,), dtype=jnp.float32)
        bv = jnp.zeros((D,), dtype=jnp.float32)
        return {'x': x, 'Wq': Wq, 'bq': bq, 'Wk': Wk, 'bk': bk, 'Wv': Wv, 'bv': bv}
    _L1_attn_all = _L1_attn_setup()
    _L1_attn_in = {k: v for k, v in _L1_attn_all.items() if k in ('Wq', 'bq', 'Wk', 'bk', 'Wv', 'bv')}
    del _L1_attn_all

    def _L1_ffn_setup():
        import jax, jax.numpy as jnp
        import numpy as np
        B, S, H, F, E, K = (8, 1024, 64, 128, 16, 2)
        EPS = 1e-05
        key = jax.random.key(seed)
        ks = jax.random.split(key, 9)
        sc = 0.02
        return {'x': jax.random.normal(ks[0], (B, S, H), dtype=jnp.float32), 'gate_w': jax.random.normal(ks[1], (H, E), dtype=jnp.float32) * sc, 'gate_b': jnp.zeros((E,), dtype=jnp.float32), 'w1': jax.random.normal(ks[2], (E, H, F), dtype=jnp.float32) * sc, 'b1': jnp.zeros((E, F), dtype=jnp.float32), 'w2': jax.random.normal(ks[3], (E, F, H), dtype=jnp.float32) * sc, 'b2': jnp.zeros((E, H), dtype=jnp.float32), 'gamma': jnp.ones((H,), dtype=jnp.float32), 'beta': jnp.zeros((H,), dtype=jnp.float32)}
    _L1_ffn_all = _L1_ffn_setup()
    _L1_ffn_in = {k: v for k, v in _L1_ffn_all.items() if k in ('gate_w', 'gate_b', 'w1', 'b1', 'w2', 'b2', 'gamma', 'beta')}
    del _L1_ffn_all

    def _L2_attn_setup():
        import jax, jax.numpy as jnp
        import numpy as np
        WS = 7
        CT = 2
        H = 8
        C = 64
        B = 1024
        WS2 = WS * WS
        N = WS2 + CT * CT
        HD = C // H

        def _relative_position_index():
            coords = np.arange(WS)
            cc = np.stack(np.meshgrid(coords, coords, indexing='ij'))
            cc = cc.reshape(2, -1)
            rel = cc[:, :, None] - cc[:, None, :]
            rel = rel.transpose(1, 2, 0).copy()
            rel[:, :, 0] += WS - 1
            rel[:, :, 1] += WS - 1
            rel[:, :, 0] *= 2 * WS - 1
            return jnp.asarray(rel.sum(-1).reshape(-1), dtype=jnp.int32)
        key = jax.random.key(seed)
        k1, k2, k3, k4, k5 = jax.random.split(key, 5)
        s = 0.02
        return {'x': jax.random.normal(k1, (B, N, C), dtype=jnp.float32), 'w_qkv': jax.random.normal(k2, (3 * C, C), dtype=jnp.float32) * s, 'w_proj': jax.random.normal(k3, (C, C), dtype=jnp.float32) * s, 'b_proj': jax.random.normal(k4, (C,), dtype=jnp.float32) * s, 'rel_table': jax.random.normal(k5, ((2 * WS - 1) ** 2, H), dtype=jnp.float32) * s, 'rel_index': _relative_position_index()}
    _L2_attn_all = _L2_attn_setup()
    _L2_attn_in = {k: v for k, v in _L2_attn_all.items() if k in ('w_qkv', 'w_proj', 'b_proj', 'rel_table', 'rel_index')}
    del _L2_attn_all

    def _L2_ffn_setup():
        import jax, jax.numpy as jnp
        import numpy as np
        B, T, C = (64, 96, 64)
        NH, NKV = (4, 2)
        HD = C // NH
        NREP = NH // NKV
        NE, TOPK = (8, 2)
        HID = int(8 / 3 * C)
        EPS_RMS = 1e-06

        def _rope_tables(t_len):
            inv_freq = 1.0 / 10000.0 ** (np.arange(0, HD, 2, dtype=np.float32) / HD)
            t = np.arange(t_len, dtype=np.float32)
            freqs = np.outer(t, inv_freq)
            emb = np.concatenate([freqs, freqs], axis=-1)
            return (jnp.asarray(np.cos(emb)), jnp.asarray(np.sin(emb)))

        def _rotate_half(x):
            h = x.shape[-1] // 2
            return jnp.concatenate([-x[..., h:], x[..., :h]], axis=-1)

        def _rmsnorm(v, w):
            return v * jax.lax.rsqrt(jnp.mean(v * v, axis=-1, keepdims=True) + EPS_RMS) * w
        key = jax.random.key(seed)
        ks = jax.random.split(key, 10)
        s = lambda k, shape: jax.random.normal(k, shape, jnp.float32) * 0.02
        return {'x': jax.random.normal(ks[0], (B, T, C), jnp.float32), 'ln1_w': jnp.ones((C,), jnp.float32), 'ln2_w': jnp.ones((C,), jnp.float32), 'wq': s(ks[1], (NH * HD, C)), 'wk': s(ks[2], (NKV * HD, C)), 'wv': s(ks[3], (NKV * HD, C)), 'wo': s(ks[4], (C, C)), 'router_w': s(ks[5], (NE, C)), 'w1': s(ks[6], (NE, HID, C)), 'w2': s(ks[7], (NE, C, HID)), 'w3': s(ks[8], (NE, HID, C))}
    _L2_ffn_all = _L2_ffn_setup()
    _L2_ffn_in = {k: v for k, v in _L2_ffn_all.items() if k in ('ln1_w', 'ln2_w', 'wq', 'wk', 'wv', 'wo', 'router_w', 'w1', 'w2', 'w3')}
    del _L2_ffn_all

    def _L3_attn_setup():
        import jax, jax.numpy as jnp
        import numpy as np
        HEADS = 8
        EPS = 1e-05

        def _ln(t, w, b, headc):
            m = jnp.mean(t, axis=-1, keepdims=True)
            d = t - m
            std = jnp.sqrt(jnp.sum(d * d, axis=-1, keepdims=True) / (headc - 1))
            return w * (d / (std + EPS)) + b
        key = jax.random.key(seed)
        B, N, C = (32, 1024, 64)
        headc = C // HEADS
        x = jax.random.normal(key, (B, N, C), dtype=jnp.float32)
        return {'x': x, 'kln_weight': jnp.ones((HEADS, 1, headc), dtype=jnp.float32), 'kln_bias': jnp.zeros((HEADS, 1, headc), dtype=jnp.float32), 'vln_weight': jnp.ones((HEADS, 1, headc), dtype=jnp.float32), 'vln_bias': jnp.zeros((HEADS, 1, headc), dtype=jnp.float32)}
    _L3_attn_all = _L3_attn_setup()
    _L3_attn_in = {k: v for k, v in _L3_attn_all.items() if k in ('kln_weight', 'kln_bias', 'vln_weight', 'vln_bias')}
    del _L3_attn_all

    def _L3_ffn_setup():
        import jax, jax.numpy as jnp
        import numpy as np
        E, D, H, TOP_K = (6, 64, 64, 2)
        ROUTER_H = D // 2
        key = jax.random.key(seed)
        ks = jax.random.split(key, 12)
        s = 1.0 / np.sqrt(D)
        sh = 1.0 / np.sqrt(H)
        sr = 1.0 / np.sqrt(ROUTER_H)
        return {'features': jax.random.normal(ks[0], (8, 1024, D), dtype=jnp.float32), 'router_w1': jax.random.uniform(ks[1], (D, ROUTER_H), jnp.float32, -s, s), 'router_b1': jnp.zeros((ROUTER_H,), jnp.float32), 'router_w2': jax.random.uniform(ks[2], (ROUTER_H, E), jnp.float32, -sr, sr), 'router_b2': jnp.zeros((E,), jnp.float32), 'expert_w1': jax.random.uniform(ks[3], (E, D, H), jnp.float32, -s, s), 'expert_b1': jnp.zeros((E, H), jnp.float32), 'expert_w2': jax.random.uniform(ks[4], (E, H, H), jnp.float32, -sh, sh), 'expert_b2': jnp.zeros((E, H), jnp.float32), 'expert_w3': jax.random.uniform(ks[5], (E, H, D), jnp.float32, -sh, sh), 'expert_b3': jnp.zeros((E, D), jnp.float32)}
    _L3_ffn_all = _L3_ffn_setup()
    _L3_ffn_in = {k: v for k, v in _L3_ffn_all.items() if k in ('router_w1', 'router_b1', 'router_w2', 'router_b2', 'expert_w1', 'expert_b1', 'expert_w2', 'expert_b2', 'expert_w3', 'expert_b3')}
    del _L3_ffn_all
    return {'x': x, 'x_txt': x_txt, 'L0_tok_conv_w': _L0_tok_in['conv_w'], 'L0_tok_W1': _L0_tok_in['W1'], 'L0_tok_b1': _L0_tok_in['b1'], 'L0_tok_W2': _L0_tok_in['W2'], 'L0_tok_b2': _L0_tok_in['b2'], 'L0_txt_E0': _L0_txt_in['E0'], 'L0_txt_E1': _L0_txt_in['E1'], 'L0_txt_W0': _L0_txt_in['W0'], 'L0_txt_b0': _L0_txt_in['b0'], 'L0_txt_W1': _L0_txt_in['W1'], 'L0_txt_b1': _L0_txt_in['b1'], 'L0_txt_Wa': _L0_txt_in['Wa'], 'L0_txt_ba': _L0_txt_in['ba'], 'L0_attn_w_qkv': _L0_attn_in['w_qkv'], 'L0_attn_w_proj': _L0_attn_in['w_proj'], 'L0_attn_qn_w': _L0_attn_in['qn_w'], 'L0_attn_kn_w': _L0_attn_in['kn_w'], 'L0_ffn_router_w': _L0_ffn_in['router_w'], 'L0_ffn_w1': _L0_ffn_in['w1'], 'L0_ffn_b1': _L0_ffn_in['b1'], 'L0_ffn_w2': _L0_ffn_in['w2'], 'L0_ffn_b2': _L0_ffn_in['b2'], 'L1_attn_Wq': _L1_attn_in['Wq'], 'L1_attn_bq': _L1_attn_in['bq'], 'L1_attn_Wk': _L1_attn_in['Wk'], 'L1_attn_bk': _L1_attn_in['bk'], 'L1_attn_Wv': _L1_attn_in['Wv'], 'L1_attn_bv': _L1_attn_in['bv'], 'L1_ffn_gate_w': _L1_ffn_in['gate_w'], 'L1_ffn_gate_b': _L1_ffn_in['gate_b'], 'L1_ffn_w1': _L1_ffn_in['w1'], 'L1_ffn_b1': _L1_ffn_in['b1'], 'L1_ffn_w2': _L1_ffn_in['w2'], 'L1_ffn_b2': _L1_ffn_in['b2'], 'L1_ffn_gamma': _L1_ffn_in['gamma'], 'L1_ffn_beta': _L1_ffn_in['beta'], 'L2_attn_w_qkv': _L2_attn_in['w_qkv'], 'L2_attn_w_proj': _L2_attn_in['w_proj'], 'L2_attn_b_proj': _L2_attn_in['b_proj'], 'L2_attn_rel_table': _L2_attn_in['rel_table'], 'L2_attn_rel_index': _L2_attn_in['rel_index'], 'L2_ffn_ln1_w': _L2_ffn_in['ln1_w'], 'L2_ffn_ln2_w': _L2_ffn_in['ln2_w'], 'L2_ffn_wq': _L2_ffn_in['wq'], 'L2_ffn_wk': _L2_ffn_in['wk'], 'L2_ffn_wv': _L2_ffn_in['wv'], 'L2_ffn_wo': _L2_ffn_in['wo'], 'L2_ffn_router_w': _L2_ffn_in['router_w'], 'L2_ffn_w1': _L2_ffn_in['w1'], 'L2_ffn_w2': _L2_ffn_in['w2'], 'L2_ffn_w3': _L2_ffn_in['w3'], 'L3_attn_kln_weight': _L3_attn_in['kln_weight'], 'L3_attn_kln_bias': _L3_attn_in['kln_bias'], 'L3_attn_vln_weight': _L3_attn_in['vln_weight'], 'L3_attn_vln_bias': _L3_attn_in['vln_bias'], 'L3_ffn_router_w1': _L3_ffn_in['router_w1'], 'L3_ffn_router_b1': _L3_ffn_in['router_b1'], 'L3_ffn_router_w2': _L3_ffn_in['router_w2'], 'L3_ffn_router_b2': _L3_ffn_in['router_b2'], 'L3_ffn_expert_w1': _L3_ffn_in['expert_w1'], 'L3_ffn_expert_b1': _L3_ffn_in['expert_b1'], 'L3_ffn_expert_w2': _L3_ffn_in['expert_w2'], 'L3_ffn_expert_b2': _L3_ffn_in['expert_b2'], 'L3_ffn_expert_w3': _L3_ffn_in['expert_w3'], 'L3_ffn_expert_b3': _L3_ffn_in['expert_b3']}

def reference(x, x_txt, L0_tok_conv_w, L0_tok_W1, L0_tok_b1, L0_tok_W2, L0_tok_b2, L0_txt_E0, L0_txt_E1, L0_txt_W0, L0_txt_b0, L0_txt_W1, L0_txt_b1, L0_txt_Wa, L0_txt_ba, L0_attn_w_qkv, L0_attn_w_proj, L0_attn_qn_w, L0_attn_kn_w, L0_ffn_router_w, L0_ffn_w1, L0_ffn_b1, L0_ffn_w2, L0_ffn_b2, L1_attn_Wq, L1_attn_bq, L1_attn_Wk, L1_attn_bk, L1_attn_Wv, L1_attn_bv, L1_ffn_gate_w, L1_ffn_gate_b, L1_ffn_w1, L1_ffn_b1, L1_ffn_w2, L1_ffn_b2, L1_ffn_gamma, L1_ffn_beta, L2_attn_w_qkv, L2_attn_w_proj, L2_attn_b_proj, L2_attn_rel_table, L2_attn_rel_index, L2_ffn_ln1_w, L2_ffn_ln2_w, L2_ffn_wq, L2_ffn_wk, L2_ffn_wv, L2_ffn_wo, L2_ffn_router_w, L2_ffn_w1, L2_ffn_w2, L2_ffn_w3, L3_attn_kln_weight, L3_attn_kln_bias, L3_attn_vln_weight, L3_attn_vln_bias, L3_ffn_router_w1, L3_ffn_router_b1, L3_ffn_router_w2, L3_ffn_router_b2, L3_ffn_expert_w1, L3_ffn_expert_b1, L3_ffn_expert_w2, L3_ffn_expert_b2, L3_ffn_expert_w3, L3_ffn_expert_b3):
    import jax
    import jax.numpy as jnp

    def _L0_tok_ref(x, conv_w, W1, b1, W2, b2):
        import jax, jax.numpy as jnp
        import numpy as np
        N_BATCH, CH, HW, KERNEL, STRIDE, VC = (8, 64, 96, 8, 3, 128)

        def _unfold(x, k, s):
            n, c, h, w = x.shape
            oh = (h - k) // s + 1
            ow = (w - k) // s + 1
            ih = (jnp.arange(oh) * s)[:, None] + jnp.arange(k)[None, :]
            iw = (jnp.arange(ow) * s)[:, None] + jnp.arange(k)[None, :]
            p = x[:, :, ih, :]
            p = p[:, :, :, :, iw]
            p = p.transpose(0, 2, 4, 1, 3, 5)
            return (p.reshape(n, oh * ow, c, k, k), oh * ow)
        k = KERNEL
        kk = k * k
        n, c, h, w = x.shape
        patches, L = _unfold(x, k, STRIDE)
        N = n * L
        p = patches.reshape(N, c, k, k)
        x_norm = jnp.sqrt((p ** 2).sum(1))
        w_norm = jnp.sqrt((conv_w ** 2).sum(1))
        y = jnp.einsum('nchw,vc->nvhw', p, conv_w)
        y = y / (x_norm[:, None, :, :] * w_norm[None, :, None, None])
        vc = conv_w.shape[0]
        y_flat = y.reshape(N, vc * kk)
        idx = jnp.argmax(y_flat, axis=1)
        max_sim = jnp.take_along_axis(y_flat, idx[:, None], axis=1)
        max_ch = idx // kk
        col = idx % kk
        rows = jnp.arange(N)
        sim_map_max = y.reshape(N, vc, kk)[rows, max_ch]
        max_act = p.reshape(N, c, kk)[rows, :, col]
        vc_vec = conv_w[max_ch]
        integ = max_act * max_sim + vc_vec * (1.0 - max_sim)
        inp = jnp.concatenate([integ, sim_map_max], axis=1)
        h1 = inp @ W1.T + b1
        h1 = jnp.where(h1 > 0, h1, 0.2 * h1)
        out = jnp.tanh(h1 @ W2.T + b2)
        return out.reshape(n, L, c)

    def _L0_txt_ref(tokens, E0, E1, W0, b0, W1, b1, Wa, ba):
        import jax, jax.numpy as jnp
        import numpy as np
        VOCAB = 25000
        EMB_DIM = 75
        OUT_DIM = 64
        B, T = (32, 128)
        e0 = E0[tokens]
        e1 = E1[tokens]
        p0 = jnp.einsum('bte,eo->bto', e0, W0) + b0
        p1 = jnp.einsum('bte,eo->bto', e1, W1) + b1
        projected = jnp.stack([p0, p1], axis=2)
        logits = jnp.einsum('btno,oi->btni', projected, Wa) + ba
        alphas = jax.nn.softmax(logits, axis=-2)
        out = jnp.sum(projected * alphas, axis=2)
        return out

    def _L0_attn_ref(x, w_qkv, w_proj, qn_w, kn_w):
        import jax, jax.numpy as jnp
        import numpy as np
        EPS = 1e-06

        def _rmsnorm(x, w):
            xf = x.astype(jnp.float32)
            y = xf * jax.lax.rsqrt(jnp.mean(xf * xf, axis=-1, keepdims=True) + EPS)
            return y.astype(x.dtype) * w
        B, T, C = x.shape
        HD = 2
        H = C // HD
        qkv = x @ w_qkv.T
        q, k, v = jnp.split(qkv, 3, axis=-1)
        heads = lambda t: t.reshape(B, T, H, HD).transpose(0, 2, 1, 3)
        q = _rmsnorm(heads(q), qn_w)
        k = _rmsnorm(heads(k), kn_w)
        v = heads(v)
        scale = np.float32(1.0 / np.sqrt(HD))
        att = jnp.einsum('bhtd,bhsd->bhts', q, k) * scale
        causal = jnp.tril(jnp.ones((T, T), bool))
        att = jnp.where(causal, att, jnp.float32(-1e+30))
        att = jax.nn.softmax(att, axis=-1)
        y = jnp.einsum('bhts,bhsd->bhtd', att, v)
        y = y.transpose(0, 2, 1, 3).reshape(B, T, C)
        return y @ w_proj.T

    def _L0_ffn_ref(input_embeddings, router_w, w1, b1, w2, b2):
        import jax, jax.numpy as jnp
        import numpy as np
        NUM_EXPERTS = 8
        TOP_K = 2
        B, S, D = (8, 2048, 64)

        def _moe(tokens, router_w, w1, b1, w2, b2):
            N = tokens.shape[0]
            E = router_w.shape[0]
            logits = tokens.astype(jnp.float32) @ router_w.astype(jnp.float32).T
            probs = jax.nn.softmax(logits, axis=-1)
            rw, re = jax.lax.top_k(probs, TOP_K)
            if TOP_K > 1:
                rw = rw / jnp.maximum(rw.sum(-1, keepdims=True), 1e-12)
            rw = rw.astype(tokens.dtype)
            combine = jnp.zeros((N, E), tokens.dtype).at[jnp.arange(N)[:, None], re].set(rw)
            out = tokens
            for e in range(E):
                h = jax.nn.gelu(tokens @ w1[e] + b1[e], approximate=False)
                y = h @ w2[e] + b2[e]
                out = out + combine[:, e:e + 1] * y
            return out
        b, s, d = input_embeddings.shape
        tokens = input_embeddings.reshape(b * s, d)
        return _moe(tokens, router_w, w1, b1, w2, b2).reshape(b, s, d)

    def _L1_attn_ref(x, Wq, bq, Wk, bk, Wv, bv):
        import jax, jax.numpy as jnp
        import numpy as np
        Q = jnp.einsum('bsd,de->bse', x, Wq) + bq
        K = jnp.einsum('bsd,de,->bse'.replace(',->', '->'), x, Wk) + bk
        V = jnp.einsum('bsd,de->bse', x, Wv) + bv
        scale = 1.0 / jnp.sqrt(jnp.asarray(Q.shape[-1], dtype=jnp.float32))
        scores = jnp.einsum('bqd,bkd->bqk', Q, K) * scale
        weights = jax.nn.softmax(scores, axis=-1)
        return jnp.einsum('bqk,bkd->bqd', weights, V)

    def _L1_ffn_ref(x, gate_w, gate_b, w1, b1, w2, b2, gamma, beta):
        import jax, jax.numpy as jnp
        import numpy as np
        B, S, H, F, E, K = (8, 1024, 64, 128, 16, 2)
        EPS = 1e-05
        gate_logits = x @ gate_w + gate_b
        topk_vals, topk_idx = jax.lax.top_k(gate_logits, K)
        topk_w = jax.nn.softmax(topk_vals, axis=-1)
        h = jax.nn.relu(jnp.einsum('bsh,ehf->bsef', x, w1) + b1)
        expert_out = jnp.einsum('bsef,efh->bseh', h, w2) + b2
        sel = jnp.take_along_axis(expert_out, topk_idx[:, :, :, None], axis=2)
        moe = jnp.sum(topk_w[..., None] * sel, axis=2)
        y = x + moe
        mu = jnp.mean(y, axis=-1, keepdims=True)
        var = jnp.var(y, axis=-1, keepdims=True)
        return (y - mu) / jnp.sqrt(var + EPS) * gamma + beta

    def _L2_attn_ref(x, w_qkv, w_proj, b_proj, rel_table, rel_index):
        import jax, jax.numpy as jnp
        import numpy as np
        WS = 7
        CT = 2
        H = 8
        C = 64
        B = 1024
        WS2 = WS * WS
        N = WS2 + CT * CT
        HD = C // H

        def _relative_position_index():
            coords = np.arange(WS)
            cc = np.stack(np.meshgrid(coords, coords, indexing='ij'))
            cc = cc.reshape(2, -1)
            rel = cc[:, :, None] - cc[:, None, :]
            rel = rel.transpose(1, 2, 0).copy()
            rel[:, :, 0] += WS - 1
            rel[:, :, 1] += WS - 1
            rel[:, :, 0] *= 2 * WS - 1
            return jnp.asarray(rel.sum(-1).reshape(-1), dtype=jnp.int32)
        b, n, c = x.shape
        scale = HD ** (-0.5)
        qkv = jnp.einsum('bnc,dc->bnd', x, w_qkv).reshape(b, n, 3, H, HD)
        qkv = jnp.moveaxis(qkv, 2, 0)
        q, k, v = (qkv[0], qkv[1], qkv[2])
        attn = jnp.einsum('bnhd,bmhd->bhnm', q, k) * scale
        bias = rel_table[rel_index].reshape(WS2, WS2, H).transpose(2, 0, 1)
        pad = n - WS2
        bias = jnp.pad(bias, ((0, 0), (pad, 0), (pad, 0)))
        attn = jax.nn.softmax(attn + bias[None], axis=-1)
        out = jnp.einsum('bhnm,bmhd->bnhd', attn, v).reshape(b, n, c)
        return jnp.einsum('bnc,dc->bnd', out, w_proj) + b_proj

    def _L2_ffn_ref(x, ln1_w, ln2_w, wq, wk, wv, wo, router_w, w1, w2, w3):
        import jax, jax.numpy as jnp
        import numpy as np
        B, T, C = (64, 96, 64)
        NH, NKV = (4, 2)
        HD = C // NH
        NREP = NH // NKV
        NE, TOPK = (8, 2)
        HID = int(8 / 3 * C)
        EPS_RMS = 1e-06

        def _rope_tables(t_len):
            inv_freq = 1.0 / 10000.0 ** (np.arange(0, HD, 2, dtype=np.float32) / HD)
            t = np.arange(t_len, dtype=np.float32)
            freqs = np.outer(t, inv_freq)
            emb = np.concatenate([freqs, freqs], axis=-1)
            return (jnp.asarray(np.cos(emb)), jnp.asarray(np.sin(emb)))

        def _rotate_half(x):
            h = x.shape[-1] // 2
            return jnp.concatenate([-x[..., h:], x[..., :h]], axis=-1)

        def _rmsnorm(v, w):
            return v * jax.lax.rsqrt(jnp.mean(v * v, axis=-1, keepdims=True) + EPS_RMS) * w
        Bx, Tx, Cx = x.shape
        h = _rmsnorm(x, ln1_w)
        q = (h @ wq.T).reshape(Bx, Tx, NH, HD).transpose(0, 2, 1, 3)
        k = (h @ wk.T).reshape(Bx, Tx, NKV, HD).transpose(0, 2, 1, 3)
        v = (h @ wv.T).reshape(Bx, Tx, NKV, HD).transpose(0, 2, 1, 3)
        cos, sin = _rope_tables(Tx)
        cos, sin = (cos[None, None], sin[None, None])
        q = q * cos + _rotate_half(q) * sin
        k = k * cos + _rotate_half(k) * sin
        k = jnp.repeat(k, NREP, axis=1)
        v = jnp.repeat(v, NREP, axis=1)
        scores = jnp.einsum('bhtd,bhsd->bhts', q, k) / jnp.sqrt(jnp.float32(HD))
        causal = jnp.tril(jnp.ones((Tx, Tx), dtype=bool))
        scores = jnp.where(causal[None, None], scores, jnp.float32(-1e+30))
        att = jax.nn.softmax(scores, axis=-1)
        y = jnp.einsum('bhts,bhsd->bhtd', att, v).transpose(0, 2, 1, 3).reshape(Bx, Tx, Cx)
        x = x + y @ wo.T
        flat = _rmsnorm(x, ln2_w).reshape(-1, Cx)
        probs = jax.nn.softmax(flat @ router_w.T, axis=-1)
        tp, ti = jax.lax.top_k(probs, TOPK)
        tp = tp / (jnp.sum(tp, axis=-1, keepdims=True) + 1e-09)
        weights = jnp.sum(tp[..., None] * jax.nn.one_hot(ti, NE, dtype=flat.dtype), axis=1)
        out = jnp.zeros_like(flat)
        for e in range(NE):
            hh = jax.nn.silu(flat @ w1[e].T) * (flat @ w3[e].T)
            out = out + weights[:, e:e + 1] * (hh @ w2[e].T)
        return x + out.reshape(Bx, Tx, Cx)

    def _L3_attn_ref(x, kln_weight, kln_bias, vln_weight, vln_bias):
        import jax, jax.numpy as jnp
        import numpy as np
        HEADS = 8
        EPS = 1e-05

        def _ln(t, w, b, headc):
            m = jnp.mean(t, axis=-1, keepdims=True)
            d = t - m
            std = jnp.sqrt(jnp.sum(d * d, axis=-1, keepdims=True) / (headc - 1))
            return w * (d / (std + EPS)) + b
        B, N, C = x.shape
        headc = C // HEADS
        qkv = x.reshape(B, N, HEADS, headc).transpose(0, 2, 1, 3)
        k = _ln(qkv, kln_weight, kln_bias, headc)
        v = _ln(qkv, vln_weight, vln_bias, headc)
        kv = jnp.einsum('bhnd,bhne->bhde', k, v) / N
        out = jnp.einsum('bhnd,bhde->bhne', qkv, kv)
        out = out.transpose(0, 2, 1, 3).reshape(B, N, C)
        return out + x

    def _L3_ffn_ref(features, router_w1, router_b1, router_w2, router_b2, expert_w1, expert_b1, expert_w2, expert_b2, expert_w3, expert_b3):
        import jax, jax.numpy as jnp
        import numpy as np
        E, D, H, TOP_K = (6, 64, 64, 2)
        ROUTER_H = D // 2
        rh = jax.nn.relu(features @ router_w1 + router_b1)
        expert_logits = jax.nn.softmax(rh @ router_w2 + router_b2, axis=-1)
        top_w, top_i = jax.lax.top_k(expert_logits, TOP_K)
        routing_weights = jax.nn.softmax(top_w, axis=-1)
        h1 = jax.nn.relu(jnp.einsum('bsd,edh->bseh', features, expert_w1) + expert_b1)
        h2 = jax.nn.relu(jnp.einsum('bseh,ehf->bsef', h1, expert_w2) + expert_b2)
        expert_out = jnp.einsum('bsef,efo->bseo', h2, expert_w3) + expert_b3
        sel = jnp.take_along_axis(expert_out, top_i[:, :, :, None], axis=2)
        combined = jnp.sum(sel * routing_weights[..., None], axis=2)
        return combined
    h = _L0_tok_ref(x, L0_tok_conv_w, L0_tok_W1, L0_tok_b1, L0_tok_W2, L0_tok_b2)
    h = jnp.concatenate([h, _L0_txt_ref(x_txt, L0_txt_E0, L0_txt_E1, L0_txt_W0, L0_txt_b0, L0_txt_W1, L0_txt_b1, L0_txt_Wa, L0_txt_ba)], axis=1)
    h = h + _L0_attn_ref(_layernorm(h, axis=-1), L0_attn_w_qkv, L0_attn_w_proj, L0_attn_qn_w, L0_attn_kn_w)
    h = h + _L0_ffn_ref(_layernorm(h, axis=-1), L0_ffn_router_w, L0_ffn_w1, L0_ffn_b1, L0_ffn_w2, L0_ffn_b2)
    h = h + _L1_attn_ref(_layernorm(h, axis=-1), L1_attn_Wq, L1_attn_bq, L1_attn_Wk, L1_attn_bk, L1_attn_Wv, L1_attn_bv)
    h = h + _L1_ffn_ref(_layernorm(h, axis=-1), L1_ffn_gate_w, L1_ffn_gate_b, L1_ffn_w1, L1_ffn_b1, L1_ffn_w2, L1_ffn_b2, L1_ffn_gamma, L1_ffn_beta)
    h = h + _L2_attn_ref(_layernorm(h, axis=-1), L2_attn_w_qkv, L2_attn_w_proj, L2_attn_b_proj, L2_attn_rel_table, L2_attn_rel_index)
    h = h + _L2_ffn_ref(_layernorm(h, axis=-1), L2_ffn_ln1_w, L2_ffn_ln2_w, L2_ffn_wq, L2_ffn_wk, L2_ffn_wv, L2_ffn_wo, L2_ffn_router_w, L2_ffn_w1, L2_ffn_w2, L2_ffn_w3)
    h = h + _L3_attn_ref(_layernorm(h, axis=-1), L3_attn_kln_weight, L3_attn_kln_bias, L3_attn_vln_weight, L3_attn_vln_bias)
    h = h + _L3_ffn_ref(_layernorm(h, axis=-1), L3_ffn_router_w1, L3_ffn_router_b1, L3_ffn_router_w2, L3_ffn_router_b2, L3_ffn_expert_w1, L3_ffn_expert_b1, L3_ffn_expert_w2, L3_ffn_expert_b2, L3_ffn_expert_w3, L3_ffn_expert_b3)
    return h

_drawn_inputs = setup_inputs


def setup_inputs(seed=0):
    import zlib

    import numpy as np

    out = dict(_drawn_inputs(seed))
    spreads = {'L0_tok_b1': (0.0, 0.1),
     'L0_tok_b2': (0.0, 0.1),
     'L0_txt_b0': (0.0, 0.1),
     'L0_txt_b1': (0.0, 0.1),
     'L0_attn_qn_w': (1.0, 0.6),
     'L0_attn_kn_w': (1.0, 0.6),
     'L0_ffn_b1': (0.0, 0.32),
     'L0_ffn_b2': (0.0, 0.1),
     'L1_attn_bq': (0.0, 2.0),
     'L1_attn_bk': (0.0, 2.0),
     'L1_attn_bv': (0.0, 0.1),
     'L1_ffn_gate_b': (0.0, 0.353),
     'L1_ffn_b1': (0.0, 0.8),
     'L1_ffn_b2': (0.0, 0.359),
     'L1_ffn_gamma': (1.0, 0.2),
     'L1_ffn_beta': (0.0, 0.279),
     'L2_ffn_ln1_w': (1.0, 0.6),
     'L2_ffn_ln2_w': (1.0, 0.6),
     'L3_attn_kln_weight': (1.0, 0.2),
     'L3_attn_kln_bias': (0.0, 0.1),
     'L3_attn_vln_weight': (1.0, 0.2),
     'L3_attn_vln_bias': (0.0, 0.1),
     'L3_ffn_router_b1': (0.0, 0.8),
     'L3_ffn_router_b2': (0.0, 0.8),
     'L3_ffn_expert_b1': (0.0, 0.8),
     'L3_ffn_expert_b2': (0.0, 0.8),
     'L3_ffn_expert_b3': (0.0, 2.0)}
    factors = {'x': 2.813,
     'L0_txt_E0': 8.0,
     'L0_txt_E1': 8.0,
     'L0_txt_W0': 8.0,
     'L0_txt_W1': 8.0,
     'L0_txt_Wa': 8.0,
     'L1_attn_Wq': 8.0,
     'L1_attn_Wk': 8.0,
     'L1_ffn_gate_w': 3.394,
     'L1_ffn_w1': 8.0,
     'L1_ffn_w2': 8.0,
     'L2_attn_w_qkv': 6.479,
     'L2_attn_w_proj': 6.949,
     'L2_attn_b_proj': 7.135,
     'L2_attn_rel_table': 200.0,
     'L2_ffn_wq': 8.0,
     'L2_ffn_wk': 8.0,
     'L2_ffn_wv': 8.0,
     'L2_ffn_wo': 8.0,
     'L2_ffn_router_w': 8.0,
     'L2_ffn_w1': 8.0,
     'L2_ffn_w2': 8.0,
     'L2_ffn_w3': 8.0,
     'L3_ffn_router_w1': 8.0,
     'L3_ffn_router_w2': 7.763,
     'L3_ffn_expert_w1': 8.0,
     'L3_ffn_expert_w2': 8.0,
     'L3_ffn_expert_w3': 8.0}
    for name, (base, spread) in spreads.items():
        noise = np.random.default_rng([zlib.crc32(name.encode()), seed]).standard_normal(out[name].shape)
        drawn = base * np.exp(spread * noise) if base else spread * noise
        out[name] = jnp.asarray(drawn.astype(out[name].dtype))
    for name, factor in factors.items():
        out[name] = (out[name] * factor).astype(out[name].dtype)
    return out
```

```python
from contextlib import ExitStack

import concourse.bass as bass
from concourse import mybir

ALU = mybir.AluOpType
ACT = mybir.ActivationFunctionType
F32 = mybir.dt.float32
BF16 = mybir.dt.bfloat16
U32 = mybir.dt.uint32
I32 = mybir.dt.int32
AX = mybir.AxisListType.X
ds = bass.ds

B = 8
D = 64
GRID = 30
VIS = GRID * GRID
TXT = 128
S = VIS + TXT
N_TOK = B * S
NT = -(-S // 128)
PAD_ROWS = (B - 1) * S + NT * 128 + 100
FT = 5
FTOK = FT * 128
F_TURNS = -(-N_TOK // FTOK)
PAD_ROWS = max(PAD_ROWS, F_TURNS * FTOK)
LN_EPS = 1e-5
RMS_EPS = 1e-6
WS2 = 49
NEG = -1e30
COMBOS = [(0, 0), (0, 1), (1, 0), (1, 1), (0, 2), (2, 0)]


class Signals:

    def __init__(self, nc, ctx, stage, names):
        self.nc = nc
        self.all = {n: ctx.enter_context(nc.semaphore(f"{stage}_{n}")) for n in names.split()}

    def __getitem__(self, name):
        return self.all[name]

    def end_turn(self):
        for s in self.all.values():
            self.nc.sync.sem_clear(s)
        self.nc.all_engine_barrier()


class Chain:

    def __init__(self, eng, sem):
        self.eng, self.sem, self.n = eng, sem, 0

    def __call__(self, ins):
        ins.then_inc(self.sem, 1)
        self.n += 1
        self.eng.wait_ge(self.sem, self.n)


def per_row(stat, shape):
    return stat.unsqueeze(len(shape) - 1).to_broadcast(shape)


def dve_center(nc, link, x, xc, sq, stat, shape):
    link(nc.vector.tensor_reduce(stat[:, 0], x, AX, ALU.add))
    link(nc.vector.tensor_scalar(stat[:, 0], stat[:, 0], -1.0 / D, None, ALU.mult))
    link(nc.vector.tensor_tensor(xc, x, per_row(stat[:, 0], shape), ALU.add))
    link(nc.vector.tensor_tensor(sq, xc, xc, ALU.mult))
    return nc.vector.tensor_reduce(stat[:, 1], sq, AX, ALU.add)


def dve_scale_rows(nc, link, out, xc, stat, shape):
    link(nc.vector.reciprocal(stat[:, 3], stat[:, 2]))
    return nc.vector.tensor_tensor(out, xc, per_row(stat[:, 3], shape), ALU.mult)


def act_std(nc, stat, eps, n=D):
    return nc.scalar.activation(stat[:, 2], stat[:, 1], ACT.Sqrt, bias=eps, scale=1.0 / n)



def load_constants(nc, ctx, c):
    k = {}

    def sb(name, shape, dt):
        k[name] = ctx.enter_context(nc.sbuf_tensor("k_" + name, shape, dt))
        return k[name]

    sg = Signals(nc, ctx, "k", "const_in const_set")
    ident = sb("ident", [128, 128], F32)
    identb = sb("identb", [128, 128], BF16)
    mask_st = sb("mask_st", [128, 128], BF16)
    mask_ts = sb("mask_ts", [128, 128], BF16)
    shift = sb("shift", [WS2, 132], F32)
    iota = sb("iota", [128, 16], F32)
    eps5 = sb("eps5", [128, 1], F32)
    eps6 = sb("eps6", [128, 1], F32)
    zero = sb("zero", [128, 1], F32)
    zrows = sb("zrows", [128, 128], F32)
    with nc.Block() as block:
        @block.sync
        def _(sp):
            for t, n in ((ident, "ident"), (identb, "identb"), (mask_st, "mask_st"), (mask_ts, "mask_ts"),
                         (shift, "shift"), (iota, "iota")):
                sp.dma_start(t[:], c[n]).then_inc(sg["const_in"], 16)
            sp.wait_ge(sg["const_in"], 6 * 16)
            sp.wait_ge(sg["const_set"], 4)
            for n, h in enumerate(c["pads"]):
                rows = PAD_ROWS - N_TOK
                half = rows // 2
                sp.dma_start(h[N_TOK:N_TOK + 2 * half, :].rearrange("(p a) d -> p (a d)", a=2),
                             zrows[0:half, :]).then_inc(sg["const_in"], 16)
                sp.wait_ge(sg["const_in"], (7 + n) * 16)

        @block.vector
        def _(dve):
            nc.vector.memset(eps5[:], LN_EPS).then_inc(sg["const_set"], 1)
            nc.vector.memset(eps6[:], RMS_EPS).then_inc(sg["const_set"], 1)
            nc.vector.memset(zero[:], 0.0).then_inc(sg["const_set"], 1)
            nc.vector.memset(zrows[:], 0.0).then_inc(sg["const_set"], 1)
    sg.end_turn()
    return k



def attention_project(nc, k, cfg, h_in, w, parts_d, v_d, x_d):
    hd, hq, hk = cfg["hd"], cfg["hq"], cfg["hk"]
    QK = D + hk * hd
    W = QK + hk * hd
    KR = D + 1 if cfg["bias"] else D
    SH = [128, NT, D]
    with ExitStack() as ctx:
        def sb(name, shape, dt=F32):
            return ctx.enter_context(nc.sbuf_tensor(f"{cfg['name']}_p_{name}", shape, dt))

        sg = Signals(nc, ctx, cfg["name"] + "_p", "w_in x_in ones_set dve_step act_step var_ready std_ready u_ready uT_done uT_copied "
                              "qkv_done v_copied qk_ready part_ready part_turned part_copied store_done")
        x, xc, sq, u = (sb(n, SH) for n in ("x", "xc", "sq", "u"))
        stat = sb("stat", [128, 4, NT])
        uT = sb("uT", [D + 1, NT * 128])
        wT = sb("wT", [KR, W])
        qk = sb("qk", [128, NT, QK])
        qk2 = sb("qk2", [128, NT, QK])
        part = sb("part", [128, 3, NT, QK], BF16)
        partT = sb("partT", [QK, 3, NT * 128], BF16)
        va = sb("va", [128, NT, hk, hd + 1])
        pstat = sb("pstat", [128, 4, NT * 64]) if cfg["kind"] == "rmspair" else None
        nw = sb("nw", [128, QK]) if cfg["kind"] == "rmspair" else None
        ln1 = sb("ln1", [128, D]) if cfg["kind"] == "rope" else None
        rope = sb("rope", [128, 2, NT, 16]) if cfg["kind"] == "rope" else None
        psT = ctx.enter_context(nc.psum_tensor(f"{cfg['name']}_p_psT", [128, 3 * 512], F32))
        psQ = ctx.enter_context(nc.psum_tensor(f"{cfg['name']}_p_psQ", [128, 5 * 512], F32))
        qkv = psQ[:, :].rearrange("p (n w) -> p n w", w=256)[:, 0:NT, :]
        turned = [psT[:, :].bitcast(BF16)[0:QK, 0:NT * 128], psQ[:, 0:1024].bitcast(BF16)[0:QK, 0:NT * 128],
                  psQ[:, 1024:2048].bitcast(BF16)[0:QK, 0:NT * 128]]
        n_w = 0
        with nc.Block() as block:
            @block.sync
            def _(sp):
                n = 0
                loads = [(wT[0:KR, :], w["wT"])]
                if nw is not None:
                    loads += [(nw[:, 0:D].rearrange("p (h d) -> p h d", d=2),
                               w["qn"].partition_broadcast(128).unsqueeze(1).to_broadcast([128, 32, 2])),
                              (nw[:, D:QK].rearrange("p (h d) -> p h d", d=2),
                               w["kn"].partition_broadcast(128).unsqueeze(1).to_broadcast([128, 32, 2]))]
                if ln1 is not None:
                    loads += [(ln1[:], w["ln1"].partition_broadcast(128)), (rope[:], w["rope"])]
                for dst, src in loads:
                    sp.dma_start(dst, src).then_inc(sg["w_in"], 16)
                    n += 16
                    sp.wait_ge(sg["w_in"], n)

            @block.vector
            def _(dve):
                nc.vector.memset(va[:], 1.0).then_inc(sg["ones_set"], 1)
                nc.vector.memset(uT[:], 1.0).then_inc(sg["ones_set"], 1)
                dve.wait_ge(sg["ones_set"], 2)
        sg.end_turn()
        with nc.Fori(0, B) as b:
            with nc.Block() as block:
                @block.sync
                def _(sp):
                    sp.dma_start(x[:], h_in[ds(b * S, NT * 128), :].rearrange("(n p) d -> p n d", p=128)) \
                        .then_inc(sg["x_in"], 16)
                    sp.wait_ge(sg["v_copied"], 1)
                    sp.dma_start(v_d[ds(b, 1)].rearrange("o p n v -> p (o n) v"),
                                 va[:].rearrange("p n h e -> p n (h e)")).then_inc(sg["store_done"], 16)
                    n = 16
                    if x_d is not None:
                        sp.wait_ge(sg["u_ready"], 1)
                        sp.dma_start(x_d[ds(b * NT * 128, NT * 128), :].rearrange("(n p) d -> p n d", p=128), u[:]) \
                            .then_inc(sg["store_done"], 16)
                        n += 16
                    for i in range(3):
                        sp.wait_ge(sg["part_copied"], i + 1)
                        sp.dma_start(parts_d[ds(b * 3 + i, 1)].rearrange("o r t -> (o r) t"), partT[:, i, 0:S]) \
                            .then_inc(sg["store_done"], 16)
                        n += 16
                    sp.wait_ge(sg["store_done"], n)

                @block.vector
                def _(dve):
                    link = Chain(dve, sg["dve_step"])
                    dve.wait_ge(sg["x_in"], 16)
                    dve_center(nc, link, x[:], xc[:], sq[:], stat, SH).then_inc(sg["var_ready"], 1)
                    dve.wait_ge(sg["std_ready"], 1)
                    ins = dve_scale_rows(nc, link, u[:], xc[:], stat, SH)
                    feed = u
                    if ln1 is not None:
                        ins.then_inc(sg["u_ready"], 1)
                        dve.wait_ge(sg["u_ready"], 1)
                        link(nc.vector.tensor_tensor(sq[:], u[:], u[:], ALU.mult))
                        nc.vector.tensor_reduce(stat[:, 1], sq[:], AX, ALU.add).then_inc(sg["var_ready"], 1)
                        dve.wait_ge(sg["std_ready"], 2)
                        link(dve_scale_rows(nc, link, xc[:], u[:], stat, SH))
                        ins = nc.vector.tensor_tensor(x[:], xc[:], ln1[:].unsqueeze(1).to_broadcast(SH), ALU.mult)
                        feed = x
                    ins.then_inc(sg["u_ready"], 1)
                    dve.wait_ge(sg["qkv_done"], 1)
                    nc.vector.tensor_copy(va[:, :, :, 0:hd], qkv[:, :, QK:W].rearrange("p n (h d) -> p n h d", d=hd)) \
                        .then_inc(sg["v_copied"], 1)
                    dve.wait_ge(sg["qk_ready"], 1)
                    src, oth = qk, qk2
                    if cfg["kind"] == "rmspair":
                        pairs = [128, NT * 64, 2]
                        v3 = lambda t: t[:].rearrange("p n (h d) -> p (n h) d", d=2)
                        link(nc.vector.tensor_tensor(oth[:], src[:], src[:], ALU.mult))
                        nc.vector.tensor_reduce(pstat[:, 1], v3(oth), AX, ALU.add).then_inc(sg["var_ready"], 1)
                        dve.wait_ge(sg["std_ready"], 2)
                        link(dve_scale_rows(nc, link, v3(oth), v3(src), pstat, pairs))
                        link(nc.vector.tensor_tensor(src[:], oth[:], nw[:].unsqueeze(1).to_broadcast([128, NT, QK]),
                                                     ALU.mult))
                    if cfg["kind"] == "rope":
                        H = QK // 16
                        for hh in range(H):
                            q_, o_ = src[:, :, 16 * hh:16 * hh + 16], oth[:, :, 16 * hh:16 * hh + 16]
                            nc.vector.tensor_tensor(o_[:, :, 0:8], q_[:, :, 8:16], rope[:, 1, :, 0:8], ALU.mult)
                            ins = nc.vector.tensor_tensor(o_[:, :, 8:16], q_[:, :, 0:8], rope[:, 1, :, 8:16], ALU.mult)
                        link(ins)
                        for hh in range(H):
                            q_ = src[:, :, 16 * hh:16 * hh + 16]
                            ins = nc.vector.tensor_tensor(q_, q_, rope[:, 0], ALU.mult)
                        link(ins)
                        link(nc.vector.tensor_tensor(src[:], src[:], oth[:], ALU.add))
                    link(nc.vector.tensor_scalar(src[:, :, 0:D], src[:, :, 0:D], float(hd) ** -0.5, None, ALU.mult))
                    nc.vector.tensor_copy(part[:, 0], src[:]).then_inc(sg["part_ready"], 1)
                    dve.wait_ge(sg["part_ready"], 1)
                    link(nc.vector.tensor_tensor(oth[:], src[:], part[:, 0], ALU.subtract))
                    nc.vector.tensor_copy(part[:, 1], oth[:]).then_inc(sg["part_ready"], 1)
                    dve.wait_ge(sg["part_ready"], 2)
                    link(nc.vector.tensor_tensor(src[:], oth[:], part[:, 1], ALU.subtract))
                    nc.vector.tensor_copy(part[:, 2], src[:]).then_inc(sg["part_ready"], 1)
                    for i in range(3):
                        dve.wait_ge(sg["part_turned"], i + 1)
                        nc.vector.tensor_copy(partT[:, i], turned[i]).then_inc(sg["part_copied"], 1)

                @block.scalar
                def _(act):
                    act.wait_ge(sg["var_ready"], 1)
                    act_std(nc, stat, k["eps5"][:]).then_inc(sg["std_ready"], 1)
                    if ln1 is not None:
                        act.wait_ge(sg["var_ready"], 2)
                        act_std(nc, stat, k["eps6"][:]).then_inc(sg["std_ready"], 1)
                    act.wait_ge(sg["uT_done"], 1)
                    nc.scalar.copy(uT[0:D, :], psT[0:D, 0:NT * 128]).then_inc(sg["uT_copied"], 1)
                    act.wait_ge(sg["v_copied"], 1)
                    nc.scalar.copy(qk[:], qkv[:, :, 0:QK]).then_inc(sg["qk_ready"], 1)
                    if cfg["kind"] == "rmspair":
                        act.wait_ge(sg["var_ready"], 2)
                        act_std(nc, pstat, k["eps6"][:], 2).then_inc(sg["std_ready"], 1)

                @block.tensor
                def _(pe):
                    feed = x if ln1 is not None else u
                    pe.wait_ge(sg["u_ready"], 2 if ln1 is not None else 1)
                    for n in range(NT):
                        ins = nc.tensor.transpose(psT[0:D, n * 128:n * 128 + 128], feed[:, n, :], k["ident"][:])
                    ins.then_inc(sg["uT_done"], 1)
                    pe.wait_ge(sg["uT_copied"], 1)
                    for n in range(NT):
                        ins = nc.tensor.matmul(qkv[:, n, 0:W], uT[0:KR, n * 128:n * 128 + 128], wT[0:KR, :],
                                               start=True, stop=True)
                    ins.then_inc(sg["qkv_done"], 1)
                    pe.wait_ge(sg["v_copied"], 1)
                    pe.wait_ge(sg["qk_ready"], 1)
                    for i in range(3):
                        pe.wait_ge(sg["part_ready"], i + 1)
                        for n in range(NT):
                            ins = nc.tensor.transpose(turned[i][:, n * 128:n * 128 + 128], part[:, i, n, :],
                                                      k["identb"][:])
                        ins.then_inc(sg["part_turned"], 1)
            sg.end_turn()


def gather_bias(nc, ctx, sg, table, index, tiles):
    idx = [ctx.enter_context(nc.sbuf_tensor(f"bias_idx{i}", [WS2, WS2], I32)) for i in range(2)]
    gathered = nc.alloc_semaphore("bias_gathered")
    with nc.Block() as block:
        @block.sync
        def _(sp):
            sp.dma_start(idx[0][:], index[0]).then_inc(sg["loaded"], 16)
            sp.dma_start(idx[1][:], index[1]).then_inc(sg["loaded"], 16)

        @block.gpsimd
        def _(pool):
            pool.wait_ge(sg["loaded"], 32)
            n = 0
            for i in range(2):
                for c in range(WS2):
                    pool.indirect_dma_start(
                        out=tiles[i][:, c, :], out_offset=None, in_=table,
                        in_offset=bass.IndirectOffsetOnAxis(ap=idx[i][:, c:c + 1].bitcast(U32), axis=0)) \
                        .then_inc(gathered, 16)
                    n += 16
            pool.wait_ge(gathered, n)
    sg.end_turn()


def attention_core(nc, k, cfg, parts_d, v_d, nm_d, o_d, w):
    hd, hk, rep = cfg["hd"], cfg["hk"], cfg["hq"] // cfg["hk"]
    HG = cfg["heads_turn"]
    KG = HG // rep
    G = cfg["hq"] // HG
    causal, window, shifted = cfg["causal"], cfg["window"], cfg["rowmax"]
    per = min(6, 128 // hd)
    NCH = 6 // per
    R0 = per * hd
    RX = 3 if (shifted and NCH == 1) else 0
    VW = hd + 1
    steps = [(h, j) for h in range(HG) for j in range(NT)]
    o_split = NT if NT * VW <= 512 else 512 // VW
    o_banks = 1 if o_split == NT else 2
    rows = lambda i: min(128, S - 128 * i)
    QKR = D + hk * hd
    with ExitStack() as ctx:
        def sb(name, shape, dt=F32):
            return ctx.enter_context(nc.sbuf_tensor(f"{cfg['name']}_c_{name}", shape, dt))

        sg = Signals(nc, ctx, cfg["name"] + "_c", "loaded dve_step logits_ready max_taken nm_ready nmT_done nmT_copied nm_stored negmax_in "
                              "scores_ready exp_done pv_done o_taken o_ready store_done bound_in bound_set")
        QA = sb("QA", [R0 + RX, NCH, HG, S], BF16)
        KA = sb("KA", [R0 + RX, NCH, KG, S], BF16)
        V = sb("V", [128, NT, KG * VW])
        P = sb("P", [128, 2, S])
        O = sb("O", [128, NT, HG * hd])
        rden = sb("rden", [128, NT])
        if shifted:
            NM = sb("NM", [128, HG * NT])
            nmp = sb("nmp", [128, 3, HG * NT], BF16)
            nmT = sb("nmT", [HG * NT, 3, 128], BF16)
            if NCH > 1:
                QM = sb("QM", [3, HG, S], BF16)
                KM = sb("KM", [3, S], BF16)
        if not shifted:
            wq = sb("wq", [128, 2])
            wk = sb("wk", [128, 2])
            bound = sb("bound", [128, 1])
        SC = ctx.enter_context(nc.psum_tensor(f"{cfg['name']}_c_SC", [128, 2, 3 * 512], F32))
        OP = ctx.enter_context(nc.psum_tensor(f"{cfg['name']}_c_OP", [128, 2 * 512], F32))

        def o_place(h, i):
            base = 512 * (h % 2) if o_banks == 1 else 0
            return base + i * VW if i < o_split else 512 + (i - o_split) * VW

        if window:
            biases = [sb("biasT", [WS2, WS2, 8]), sb("biasA", [WS2, WS2, 8])]
            gather_bias(nc, ctx, sg, w["table"], w["index"], biases)
        with nc.Block() as block:
            @block.sync
            def _(sp):
                if shifted:
                    dst = KA[R0:R0 + 3, 0, :, :] if NCH == 1 else KM[:].unsqueeze(1)
                    n = KG if NCH == 1 else 1
                    sp.dma_start(dst, w["ones"][:, 0:n * S].rearrange("r (h t) -> r h t", t=S)).then_inc(sg["loaded"], 16)
                    sp.wait_ge(sg["loaded"], 16)
                else:
                    sp.dma_start(wq[:], w["qn"].partition_broadcast(128)).then_inc(sg["bound_in"], 16)
                    sp.dma_start(wk[:], w["kn"].partition_broadcast(128)).then_inc(sg["bound_in"], 16)

            @block.vector
            def _(dve):
                nc.vector.memset(O[:], 0.0).then_inc(sg["bound_set"], 1)
                dve.wait_ge(sg["bound_set"], 1)
                if shifted:
                    nc.vector.memset(NM[:], 0.0).then_inc(sg["bound_set"], 1)
                    dve.wait_ge(sg["bound_set"], 2)
                else:
                    link = Chain(dve, sg["dve_step"])
                    dve.wait_ge(sg["bound_in"], 32)
                    link(nc.vector.tensor_tensor(wq[:], wq[:], wk[:], ALU.mult))
                    link(nc.vector.tensor_reduce(bound[:], wq[:], AX, ALU.max, apply_absolute_value=True))
                    link(nc.vector.tensor_scalar(bound[:], bound[:], -(float(hd) ** 0.5), None, ALU.mult))
        sg.end_turn()

        def turn(b, g):
            with nc.Block() as block:
                @block.sync
                def _(sp):
                    n = 0
                    for c, (pq, pk) in enumerate(COMBOS):
                        ch, r0 = c // per, (c % per) * hd
                        q = parts_d[ds(b * 3 + pq, 1), ds(g * (HG * hd), HG * hd), :]
                        kk = parts_d[ds(b * 3 + pk, 1), ds(g * (KG * hd) + D, KG * hd), :]
                        sp.dma_start(QA[r0:r0 + hd, ch, :, :], q.rearrange("o (h d) t -> d (o h) t", d=hd)) \
                            .then_inc(sg["loaded"], 16)
                        sp.dma_start(KA[r0:r0 + hd, ch, :, :], kk.rearrange("o (h d) t -> d (o h) t", d=hd)) \
                            .then_inc(sg["loaded"], 16)
                        n += 32
                    sp.dma_start(V[:], v_d[ds(b, 1), :, :, ds(g * (KG * VW), KG * VW)]
                                 .rearrange("o p n v -> p (o n) v")).then_inc(sg["loaded"], 16)
                    if shifted:
                        sp.wait_ge(sg["nmT_copied"], 1)
                        sp.dma_start(nm_d.rearrange("r m p -> m r p"), nmT[:]).then_inc(sg["nm_stored"], 16)
                        sp.wait_ge(sg["nm_stored"], 16)
                        dst = QA[R0:R0 + 3, 0, :, :] if NCH == 1 else QM[:]
                        sp.dma_start(dst, nm_d.rearrange("r (h i) p -> r h (i p)", i=NT)[:, :, 0:S]) \
                            .then_inc(sg["negmax_in"], 16)
                    sp.wait_ge(sg["o_ready"], HG)
                    sp.dma_start(o_d[ds(b, 1), :, :, ds(g * (HG * hd), HG * hd)].rearrange("o p n v -> p (o n) v"), O[:]) \
                        .then_inc(sg["store_done"], 16)
                    sp.wait_ge(sg["store_done"], 16)

                def logits(buf, ncols, m, lhs, rhs, extra):
                    for c0 in range(0, ncols, 512):
                        c1 = min(ncols, c0 + 512)
                        adds = [(max(a0, c0), min(a1, c1), a0, l, r) for a0, a1, l, r in extra
                                if max(a0, c0) < min(a1, c1)]
                        ops = [(c0, c1, l, r[..., c0:c1]) for l, r in zip(lhs, rhs)]
                        ops += [(x0, x1, l, r[:, x0 - a0:x1 - a0]) for x0, x1, a0, l, r in adds]
                        for z, (x0, x1, l, r) in enumerate(ops):
                            ins = nc.tensor.matmul(SC[0:m, buf, x0:x1], l, r, start=(z == 0), stop=(z == len(ops) - 1),
                                                   skip_group_check=True)
                    return ins

                @block.tensor
                def _(pe):
                    pe.wait_ge(sg["loaded"], 16 * 13)
                    if shifted:
                        for z, (h, i) in enumerate(steps):
                            m, ncols = rows(i), (min(S, 128 * i + 128) if causal else S)
                            if z >= 2:
                                pe.wait_ge(sg["max_taken"], z - 1)
                            t = slice(128 * i, 128 * i + m)
                            extra = []
                            if causal:
                                extra.append((128 * i, 128 * i + m, k["identb"][:, 0:m], k["mask_ts"][:, 0:m]))
                            if window and i >= NT - 2:
                                e0 = 0 if i == NT - 2 else 128
                                extra.append((S - WS2, S, k["shift"][:, e0:e0 + m], biases[1][:, :, h]))
                            logits(z % 2, ncols, m, [QA[0:R0, c, h, t] for c in range(NCH)],
                                   [KA[0:R0, c, h // rep, :] for c in range(NCH)], extra) \
                                .then_inc(sg["logits_ready"], 1)
                        pe.wait_ge(sg["nm_ready"], 1)
                        nt = SC[0:HG * NT, 0, 0:192].bitcast(BF16)
                        for r in range(3):
                            ins = nc.tensor.transpose(nt[:, 128 * r:128 * r + 128], nmp[:, r, :], k["identb"][:])
                        ins.then_inc(sg["nmT_done"], 1)
                        pe.wait_ge(sg["nmT_copied"], 1)
                        pe.wait_ge(sg["negmax_in"], 16)

                    def weigh(z):
                        h, j = steps[z]
                        m = rows(j)
                        pe.wait_ge(sg["exp_done"], z + 1)
                        if j == 0:
                            held = 2 if o_banks == 1 else 1
                            if h >= held:
                                pe.wait_ge(sg["o_taken"], h - held + 1)
                        i0 = j if causal else 0
                        for i in range(i0, NT):
                            c = 128 * (i - i0)
                            o = o_place(h, i)
                            ins = nc.tensor.matmul(OP[0:rows(i), o:o + VW], P[0:m, z % 2, c:c + rows(i)],
                                                   V[0:m, j, (h // rep) * VW:(h // rep) * VW + VW],
                                                   start=(j == 0 and i in (0, o_split)), stop=(j == NT - 1 or (causal and i == j)),
                                                   skip_group_check=True)
                        ins.then_inc(sg["pv_done"], 1)

                    for z, (h, j) in enumerate(steps):
                        m = rows(j)
                        t0 = 128 * j if causal else 0
                        if z >= 2:
                            pe.wait_ge(sg["exp_done"], z - 1)
                        s = slice(128 * j, 128 * j + m)
                        extra = []
                        if causal:
                            extra.append((0, m, k["identb"][:, 0:m], k["mask_st"][:, 0:m]))
                        if window and j >= NT - 2:
                            e0 = 0 if j == NT - 2 else 128
                            extra.append((S - WS2, S, k["shift"][:, e0:e0 + m], biases[0][:, :, h]))
                        lhs = [KA[0:R0 + RX, c, h // rep, s] for c in range(NCH)]
                        rhs = [QA[0:R0 + RX, c, h, t0:S] for c in range(NCH)]
                        if shifted and NCH > 1:
                            lhs.append(KM[:, s])
                            rhs.append(QM[:, h, t0:S])
                        logits(z % 2, S - t0, m, lhs, rhs, extra).then_inc(sg["scores_ready"], 1)
                        if z >= 1:
                            weigh(z - 1)
                    weigh(len(steps) - 1)

                @block.scalar
                def _(act):
                    for z, (h, j) in enumerate(steps):
                        m, n = rows(j), S - (128 * j if causal else 0)
                        act.wait_ge(sg["scores_ready"], z + 1)
                        if z >= 2:
                            act.wait_ge(sg["pv_done"], z - 1)
                        bias = k["zero"] if shifted else bound
                        nc.scalar.activation(P[0:m, z % 2, 0:n], SC[0:m, z % 2, 0:n], ACT.Exp, bias=bias[0:m, :]) \
                            .then_inc(sg["exp_done"], 1)

                @block.vector
                def _(dve):
                    link = Chain(dve, sg["dve_step"])
                    if shifted:
                        for z, (h, i) in enumerate(steps):
                            m, ncols = rows(i), (min(S, 128 * i + 128) if causal else S)
                            dve.wait_ge(sg["logits_ready"], z + 1)
                            nc.vector.tensor_reduce(NM[0:m, z:z + 1], SC[0:m, z % 2, 0:ncols], AX, ALU.max, negate=True) \
                                .then_inc(sg["max_taken"], 1)
                        dve.wait_ge(sg["max_taken"], len(steps))
                        for r in range(3):
                            ins = nc.vector.tensor_copy(nmp[:, r, :], NM[:])
                            if r < 2:
                                link(ins)
                                link(nc.vector.tensor_tensor(NM[:], NM[:], nmp[:, r, :], ALU.subtract))
                        ins.then_inc(sg["nm_ready"], 1)
                        dve.wait_ge(sg["nmT_done"], 1)
                        nc.vector.tensor_copy(nmT[:].rearrange("m r p -> m (r p)"),
                                              SC[0:HG * NT, 0, 0:192].bitcast(BF16)).then_inc(sg["nmT_copied"], 1)
                    for h in range(HG):
                        dve.wait_ge(sg["pv_done"], (h + 1) * NT)
                        for a, e, m in ((0, min(o_split, NT - 1), 128), (o_split, NT - 1, 128), (NT - 1, NT, rows(NT - 1))):
                            if a >= e:
                                continue
                            o = OP[0:m, o_place(h, a):o_place(h, a) + (e - a) * VW].rearrange("p (i v) -> p i v", v=VW)
                            link(nc.vector.reciprocal(rden[0:m, a:e], o[:, :, hd]))
                            ins = nc.vector.tensor_tensor(O[0:m, a:e, h * hd:h * hd + hd], o[:, :, 0:hd],
                                                          per_row(rden[0:m, a:e], [m, e - a, hd]), ALU.mult)
                            link(ins)
                        nc.vector.tensor_copy(rden[0:1, 0:1], k["zero"][0:1, :]).then_inc(sg["o_taken"], 1)
                        dve.wait_ge(sg["o_taken"], h + 1)
                        nc.vector.tensor_copy(rden[0:1, 0:1], k["zero"][0:1, :]).then_inc(sg["o_ready"], 1)
                        dve.wait_ge(sg["o_ready"], h + 1)
            sg.end_turn()

        with nc.Fori(0, B) as b:
            if G == 1:
                turn(b, 0)
            else:
                with nc.Fori(0, G) as g:
                    turn(b, g)


def attention_output(nc, k, cfg, h_in, h_out, o_d, x_d, x1_d, w):
    SH = [128, NT, D]
    proj = w is not None
    with ExitStack() as ctx:
        def sb(name, shape, dt=F32):
            return ctx.enter_context(nc.sbuf_tensor(f"{cfg['name']}_o_{name}", shape, dt))

        sg = Signals(nc, ctx, cfg["name"] + "_o", "w_in in_done oT_done oT_copied y_done out_ready store_done ones_set")
        O, x, y = (sb(n, SH) for n in ("O", "x", "y"))
        oT = sb("oT", [D + 1, NT * 128])
        wT = sb("wT", [D + 1, D])
        psT = ctx.enter_context(nc.psum_tensor(f"{cfg['name']}_o_psT", [128, 3 * 512], F32))
        psY = ctx.enter_context(nc.psum_tensor(f"{cfg['name']}_o_psY", [128, 2 * 512], F32))
        KR = D + 1 if cfg["out_bias"] else D
        if proj:
            with nc.Block() as block:
                @block.sync
                def _(sp):
                    sp.dma_start(wT[0:KR, :], w).then_inc(sg["w_in"], 16)
                    sp.wait_ge(sg["w_in"], 16)

                @block.vector
                def _(dve):
                    nc.vector.memset(oT[:], 1.0).then_inc(sg["ones_set"], 1)
                    dve.wait_ge(sg["ones_set"], 1)
            sg.end_turn()
        with nc.Fori(0, B) as b:
            with nc.Block() as block:
                @block.sync
                def _(sp):
                    sp.dma_start(O[:], o_d[ds(b, 1)].rearrange("o p n v -> p (o n) v")).then_inc(sg["in_done"], 16)
                    if x_d is None:
                        src = h_in[ds(b * S, NT * 128), :]
                    else:
                        src = x_d[ds(b * NT * 128, NT * 128), :]
                    sp.dma_start(x[:], src.rearrange("(n p) d -> p n d", p=128)).then_inc(sg["in_done"], 16)
                    sp.wait_ge(sg["out_ready"], 1)
                    out = h_out if x1_d is None else x1_d
                    sp.dma_start(out[ds(b * S, S // 128 * 128), :].rearrange("(n p) d -> p n d", p=128), y[:, 0:S // 128]) \
                        .then_inc(sg["store_done"], 16)
                    sp.dma_start(out[ds(b * S + S // 128 * 128, S % 128), :], y[0:S % 128, NT - 1]) \
                        .then_inc(sg["store_done"], 16)
                    sp.wait_ge(sg["store_done"], 32)

                @block.tensor
                def _(pe):
                    if proj:
                        pe.wait_ge(sg["in_done"], 32)
                        for n in range(NT):
                            ins = nc.tensor.transpose(psT[0:D, n * 128:n * 128 + 128], O[:, n, :], k["ident"][:])
                        ins.then_inc(sg["oT_done"], 1)
                        pe.wait_ge(sg["oT_copied"], 1)
                        for n in range(NT):
                            ins = nc.tensor.matmul(psY[:, n * D:n * D + D], oT[0:KR, n * 128:n * 128 + 128], wT[0:KR, :],
                                                   start=True, stop=True)
                        ins.then_inc(sg["y_done"], 1)

                @block.scalar
                def _(act):
                    if proj:
                        act.wait_ge(sg["oT_done"], 1)
                        nc.scalar.copy(oT[0:D, :], psT[0:D, 0:NT * 128]).then_inc(sg["oT_copied"], 1)

                @block.vector
                def _(dve):
                    dve.wait_ge(sg["in_done"], 32)
                    a = O[:]
                    if proj:
                        dve.wait_ge(sg["y_done"], 1)
                        a = psY[:, 0:NT * D].rearrange("p (n d) -> p n d", d=D)
                    nc.vector.tensor_tensor(y[:], a, x[:], ALU.add).then_inc(sg["out_ready"], 1)
            sg.end_turn()


def attention_stage(nc, k, cfg, h_in, h_out, w, x1_d=None):
    name = cfg["name"]
    hd, hk = cfg["hd"], cfg["hk"]
    parts_d = nc.dram_tensor(name + "_parts", [B * 3, D + hk * hd, S], BF16).ap()
    v_d = nc.dram_tensor(name + "_v", [B, 128, NT, hk * (hd + 1)], F32).ap()
    o_d = nc.dram_tensor(name + "_o", [B, 128, NT, D], F32).ap()
    nm_d = nc.dram_tensor(name + "_nm", [3, cfg["heads_turn"] * NT, 128], BF16).ap()
    x_d = nc.dram_tensor(name + "_x", [B * NT * 128, D], F32).ap() if x1_d is not None else None
    attention_project(nc, k, cfg, h_in, w, parts_d, v_d, x_d)
    attention_core(nc, k, cfg, parts_d, v_d, nm_d, o_d, w)
    attention_output(nc, k, cfg, h_in, h_out, o_d, x_d, x1_d, w.get("wo"))


ATT = {
    "L0": dict(name="att0", hd=2, hq=32, hk=32, heads_turn=8, causal=True, window=False, rowmax=False, bias=False, kind="rmspair",
               out_bias=False),
    "L1": dict(name="att1", hd=64, hq=1, hk=1, heads_turn=1, causal=False, window=False, rowmax=True, bias=True, kind="plain",
               out_bias=False),
    "L2": dict(name="att2", hd=8, hq=8, hk=8, heads_turn=8, causal=False, window=True, rowmax=True, bias=False, kind="plain",
               out_bias=True),
    "L2f": dict(name="att2f", hd=16, hq=4, hk=2, heads_turn=4, causal=True, window=False, rowmax=True, bias=False, kind="rope",
                out_bias=False),
}


def constants():
    import numpy as np
    from concourse import mybir as mb
    bf = mb.dt.np(mb.dt.bfloat16)
    r = np.arange(128)
    inv = 1.0 / 10000.0 ** (np.arange(0, 16, 2, dtype=np.float32) / 16)
    emb = np.outer(np.arange(NT * 128, dtype=np.float32), inv)
    emb = np.concatenate([emb, emb], -1)
    sin = np.sin(emb)
    sin[:, :8] *= -1
    rope = np.stack([np.cos(emb), sin]).reshape(2, NT, 128, 16).transpose(2, 0, 1, 3)
    return {
        "ident": np.eye(128, dtype=np.float32),
        "identb": np.eye(128, dtype=np.float32).astype(bf),
        "mask_st": np.where(r[:, None] > r[None, :], NEG, 0.0).astype(np.float32).astype(bf),
        "mask_ts": np.where(r[None, :] > r[:, None], NEG, 0.0).astype(np.float32).astype(bf),
        "shift": (np.arange(WS2)[:, None] == np.arange(132)[None, :] - (S - WS2) % 128).astype(np.float32),
        "iota": np.tile(np.arange(16, dtype=np.float32), (128, 1)),
        "rope": np.ascontiguousarray(rope.astype(np.float32)),
        "ones3": np.ones((3, 8 * S), np.float32).astype(bf),
    }



def ffn_stage(nc, k, cfg, h_in, h_out, w, x1_d=None):
    E, F, mode = cfg["E"], cfg["F"], cfg["mode"]
    EP = max(8, E)
    pair, glu, deep, biased = cfg["pair"], cfg["glu"], cfg["deep"], cfg["biased"]
    chunks = cfg["chunks"]
    UNITS = E // 2 if pair else E * chunks
    M = 2 * F if pair else F
    layers = 2 if deep else 1
    KR = D + 1 if biased else D
    SH = [128, FT, D]
    HALF = FTOK // 2
    FUNC = {"gelu": ACT.Gelu, "relu": ACT.Relu, "silu": ACT.Silu}[cfg["act"]]
    RH = 32
    experts_of = (lambda u: (2 * u, 2 * u + 1)) if pair else (lambda u: (u // chunks,))
    n_std = 2 if cfg["post"] else 1
    with ExitStack() as ctx:
        def sb(name, shape, dt=F32):
            return ctx.enter_context(nc.sbuf_tensor(f"{cfg['name']}_{name}", shape, dt))

        sg = Signals(nc, ctx, cfg["name"], "w_in x_in x1_in preset dve_step var_ready std_ready u_ready uT_done uT_copied rh_done "
                              "rh_copied logits_done shifted_ready exp_ready gap_ready gap_exp c_ready cT_done cT_copied "
                              "yb_done hid_done hid_used gate_used unit_done y_used out_ready store_done")
        x, xc, sq, u, y = (sb(n, SH) for n in ("x", "xc", "sq", "u", "y"))
        x1 = sb("x1", SH) if x1_d is not None else None
        stat = sb("stat", [128, 4, FT])
        uT = sb("uT", [D + 1, FTOK])
        w1 = sb("w1", [KR, UNITS, M])
        w3 = sb("w3", [KR, UNITS, M]) if glu else None
        wm = sb("wm", [128, UNITS, 128]) if deep else None
        bm = sb("bm", [128, UNITS]) if deep else None
        w2 = sb("w2", [128, UNITS, D])
        b2 = sb("b2", [E, D]) if biased else None
        rw = sb("rw", [D + 1, E])
        rw1 = sb("rw1", [D + 1, RH]) if deep else None
        rhT = sb("rhT", [RH + 1, FTOK]) if deep else None
        gb = sb("gb", [128, 2, D]) if cfg["post"] else None
        lnw = sb("lnw", [128, D]) if x1_d is not None else None
        hT = sb("hT", [128, 2, FTOK])
        gT = sb("gT", [128, 2, FTOK]) if (deep or glu) else None
        lg = sb("lg", [128, FT, EP])
        top = sb("top", [128, FT, 8])
        idx = sb("idx", [128, FT, 8], U32)
        idxf = sb("idxf", [128, FT, 8])
        rst = sb("rst", [128, 4, FT])
        wt = sb("wt", [128, FT, 2])
        c = sb("c", [128, FT, E])
        c2 = sb("c2", [128, FT, E])
        cT = sb("cT", [E, FTOK])
        acc = sb("acc", SH)
        HP = ctx.enter_context(nc.psum_tensor(f"{cfg['name']}_HP", [128, 4, 512], F32))
        YP = ctx.enter_context(nc.psum_tensor(f"{cfg['name']}_YP", [128, 2, 512], F32))
        MP = ctx.enter_context(nc.psum_tensor(f"{cfg['name']}_MP", [128, 2 * 512], F32))
        lgP = MP[:, 768:768 + FT * 16].rearrange("p (n e) -> p n e", e=16)
        REXT = D + 1 if cfg["router_bias"] else D
        with nc.Block() as block:
            @block.sync
            def _(sp):
                sp.wait_ge(sg["preset"], 4)
                loads = [(w1[:], w["w1"]), (rw[0:(RH + 1 if deep else REXT), :], w["rw"])]
                if chunks == 1:
                    loads.append((w2[0:M], w["w2"]))
                else:
                    loads.append((w2[0:F], w["w2"]))
                if glu:
                    loads.append((w3[:], w["w3"]))
                if biased:
                    loads.append((b2[:], w["b2"]))
                if deep:
                    loads += [(rw1[:], w["rw1"]), (bm[:], w["bm"]),
                              (wm[0:64, :, 0:64], w["wm"][0]), (wm[64:128, :, 64:128], w["wm"][1])]
                if cfg["post"]:
                    loads += [(gb[:, 0, :], w["gamma"].partition_broadcast(128)),
                              (gb[:, 1, :], w["beta"].partition_broadcast(128))]
                if lnw is not None:
                    loads.append((lnw[:], w["ln"].partition_broadcast(128)))
                for n, (dst, src) in enumerate(loads):
                    sp.dma_start(dst, src).then_inc(sg["w_in"], 16)
                    sp.wait_ge(sg["w_in"], 16 * (n + 1))

            @block.vector
            def _(dve):
                nc.vector.memset(uT[:], 1.0).then_inc(sg["preset"], 1)
                nc.vector.memset(lg[:], NEG).then_inc(sg["preset"], 1)
                nc.vector.memset((wm if deep else c)[:], 0.0).then_inc(sg["preset"], 1)
                nc.vector.memset((rhT if deep else c2)[:], 1.0).then_inc(sg["preset"], 1)
                dve.wait_ge(sg["preset"], 4)
        sg.end_turn()
        items = [(un, la, hf) for un in range(UNITS) for la in range(layers) for hf in range(2)]
        unit_items = 2 * layers
        with nc.Fori(0, F_TURNS) as it:
            with nc.Block() as block:
                @block.sync
                def _(sp):
                    tok = lambda t: t[ds(it * FTOK, FTOK), :].rearrange("(p n) d -> p n d", n=FT)
                    if x1 is not None:
                        sp.dma_start(x1[:], tok(x1_d)).then_inc(sg["x1_in"], 16)
                    sp.dma_start(x[:], tok(h_in)).then_inc(sg["x_in"], 16)
                    sp.wait_ge(sg["out_ready"], 1)
                    sp.dma_start(tok(h_out), y[:]).then_inc(sg["store_done"], 16)
                    sp.wait_ge(sg["store_done"], 16)

                @block.tensor
                def _(pe):
                    pe.wait_ge(sg["u_ready"], 1)
                    for n in range(FT):
                        ins = nc.tensor.transpose(MP[0:D, 128 * n:128 * n + 128], u[:, n, :], k["ident"][:])
                    ins.then_inc(sg["uT_done"], 1)
                    pe.wait_ge(sg["uT_copied"], 1)
                    if deep:
                        for hf in range(2):
                            ins = nc.tensor.matmul(MP[0:RH, 512 * hf:512 * hf + HALF], rw1[:],
                                                   uT[:, HALF * hf:HALF * hf + HALF], start=True, stop=True)
                        ins.then_inc(sg["rh_done"], 1)
                        pe.wait_ge(sg["rh_copied"], 2)
                    for n in range(FT):
                        src = rhT[0:RH + 1, 128 * n:128 * n + 128] if deep else uT[0:REXT, 128 * n:128 * n + 128]
                        ins = nc.tensor.matmul(lgP[:, n, 0:E], src, rw[0:(RH + 1 if deep else REXT), :],
                                               start=True, stop=True)
                    ins.then_inc(sg["logits_done"], 1)

                    def hidden(un):
                        for la in range(layers):
                            for hf in range(2):
                                z = items.index((un, la, hf))
                                cols = slice(HALF * hf, HALF * hf + HALF)
                                if glu:
                                    if z >= 2:
                                        pe.wait_ge(sg["hid_used"], z - 1)
                                    nc.tensor.matmul(HP[0:M, 2 * (z % 2), 0:HALF], w1[:, un, :], uT[0:KR, cols],
                                                     start=True, stop=True)
                                    nc.tensor.matmul(HP[0:M, 2 * (z % 2) + 1, 0:HALF], w3[:, un, :], uT[0:KR, cols],
                                                     start=True, stop=True).then_inc(sg["hid_done"], 1)
                                    continue
                                if z >= 4:
                                    pe.wait_ge(sg["hid_used"], z - 3)
                                if la == 0:
                                    ins = nc.tensor.matmul(HP[0:M, z % 4, 0:HALF], w1[:, un, :], uT[0:KR, cols],
                                                           start=True, stop=True)
                                else:
                                    pe.wait_ge(sg["hid_used"], z - 1)
                                    ins = nc.tensor.matmul(HP[0:M, z % 4, 0:HALF], wm[:, un, :], gT[:, un % 2, cols],
                                                           start=True, stop=True)
                                ins.then_inc(sg["hid_done"], 1)

                    def outputs(un):
                        pe.wait_ge(sg["hid_used"], (un + 1) * unit_items)
                        for e in experts_of(un):
                            ch = un % chunks
                            if ch == 0 and e >= 2:
                                pe.wait_ge(sg["y_used"], e - 1)
                            p0 = 64 * (e % 2) if pair else 0
                            r = slice(p0, p0 + F)
                            for n in range(FT):
                                ins = nc.tensor.matmul(YP[:, e % 2, D * n:D * n + D], hT[r, un % 2, 128 * n:128 * n + 128],
                                                       w2[r, un, :], start=(ch == 0 and n == 0), stop=(ch == chunks - 1),
                                                       skip_group_check=True)
                        ins.then_inc(sg["unit_done"], 1)

                    for un in range(UNITS):
                        hidden(un)
                        if un >= 1:
                            outputs(un - 1)
                    outputs(UNITS - 1)
                    if biased:
                        pe.wait_ge(sg["c_ready"], 1)
                        for n in range(FT):
                            ins = nc.tensor.transpose(MP[0:E, 128 * n:128 * n + 128], c[:, n, :], k["ident"][:])
                        ins.then_inc(sg["cT_done"], 1)
                        pe.wait_ge(sg["cT_copied"], 1)
                        for n in range(FT):
                            ins = nc.tensor.matmul(MP[:, D * n:D * n + D], cT[:, 128 * n:128 * n + 128], b2[:],
                                                   start=True, stop=True)
                        ins.then_inc(sg["yb_done"], 1)

                @block.scalar
                def _(act):
                    act.wait_ge(sg["var_ready"], 1)
                    act_std(nc, stat, k["eps6" if x1 is not None else "eps5"][:]).then_inc(sg["std_ready"], 1)
                    act.wait_ge(sg["uT_done"], 1)
                    nc.scalar.copy(uT[0:D, :], MP[0:D, 0:FTOK]).then_inc(sg["uT_copied"], 1)
                    if deep:
                        act.wait_ge(sg["rh_done"], 1)
                        for hf in range(2):
                            nc.scalar.activation(rhT[0:RH, HALF * hf:HALF * hf + HALF], MP[0:RH, 512 * hf:512 * hf + HALF],
                                                 ACT.Relu).then_inc(sg["rh_copied"], 1)
                    if mode != "logits":
                        act.wait_ge(sg["shifted_ready"], 1)
                        nc.scalar.activation(lg[:, :, 0:E], lg[:, :, 0:E], ACT.Exp).then_inc(sg["exp_ready"], 1)
                    for z, (un, la, hf) in enumerate(items):
                        cols = slice(HALF * hf, HALF * hf + HALF)
                        act.wait_ge(sg["hid_done"], z + 1)
                        if glu:
                            if z >= 4:
                                act.wait_ge(sg["hid_used"], z - 3)
                            nc.scalar.activation(gT[0:M, un % 2, cols], HP[0:M, 2 * (z % 2), 0:HALF], FUNC) \
                                .then_inc(sg["gate_used"], 1)
                        else:
                            if un >= 2:
                                act.wait_ge(sg["unit_done"], un - 1)
                            dst = gT if (deep and la == 0) else hT
                            bias = bm[:, un:un + 1] if la == 1 else 0.0
                            nc.scalar.activation(dst[0:M, un % 2, cols], HP[0:M, z % 4, 0:HALF], FUNC, bias=bias) \
                                .then_inc(sg["hid_used"], 1)
                        if mode != "probs" and un == 1 and la == layers - 1 and hf == 1:
                            act.wait_ge(sg["gap_ready"], 1)
                            nc.scalar.activation(rst[:, 3], rst[:, 2], ACT.Exp).then_inc(sg["gap_exp"], 1)
                    if biased:
                        act.wait_ge(sg["cT_done"], 1)
                        nc.scalar.copy(cT[:], MP[0:E, 0:FTOK]).then_inc(sg["cT_copied"], 1)
                    if cfg["post"]:
                        act.wait_ge(sg["var_ready"], 2)
                        act_std(nc, stat, k["eps5"][:]).then_inc(sg["std_ready"], 1)

                @block.vector
                def _(dve):
                    link = Chain(dve, sg["dve_step"])
                    if x1 is not None:
                        dve.wait_ge(sg["x1_in"], 16)
                        link(nc.vector.tensor_tensor(sq[:], x1[:], x1[:], ALU.mult))
                        nc.vector.tensor_reduce(stat[:, 1], sq[:], AX, ALU.add).then_inc(sg["var_ready"], 1)
                        dve.wait_ge(sg["std_ready"], 1)
                        link(dve_scale_rows(nc, link, xc[:], x1[:], stat, SH))
                        nc.vector.tensor_tensor(u[:], xc[:], lnw[:].unsqueeze(1).to_broadcast(SH), ALU.mult) \
                            .then_inc(sg["u_ready"], 1)
                    else:
                        dve.wait_ge(sg["x_in"], 16)
                        dve_center(nc, link, x[:], xc[:], sq[:], stat, SH).then_inc(sg["var_ready"], 1)
                        dve.wait_ge(sg["std_ready"], 1)
                        dve_scale_rows(nc, link, u[:], xc[:], stat, SH).then_inc(sg["u_ready"], 1)
                    dve.wait_ge(sg["logits_done"], 1)
                    if mode == "logits":
                        link(nc.vector.tensor_copy(lg[:, :, 0:E], lgP[:, :, 0:E]))
                    else:
                        link(nc.vector.tensor_reduce(rst[:, 0], lgP[:, :, 0:E], AX, ALU.max))
                        nc.vector.tensor_tensor(lg[:, :, 0:E], lgP[:, :, 0:E], per_row(rst[:, 0], [128, FT, E]),
                                                ALU.subtract).then_inc(sg["shifted_ready"], 1)
                        dve.wait_ge(sg["exp_ready"], 1)
                        link(nc.vector.tensor_reduce(rst[:, 0], lg[:, :, 0:E], AX, ALU.add))
                        link(nc.vector.reciprocal(rst[:, 1], rst[:, 0]))
                        link(nc.vector.tensor_tensor(lg[:, :, 0:E], lg[:, :, 0:E], per_row(rst[:, 1], [128, FT, E]),
                                                     ALU.mult))
                    for n in range(FT):
                        ins = nc.vector.max(top[:, n, :], lg[:, n, :])
                    link(ins)
                    for n in range(FT):
                        ins = nc.vector.max_index(idx[:, n, :], top[:, n, :], lg[:, n, :])
                    link(ins)
                    link(nc.vector.tensor_copy(idxf[:], idx[:]))
                    if mode == "probs":
                        link(nc.vector.tensor_tensor(rst[:, 0], top[:, :, 0], top[:, :, 1], ALU.add))
                        link(nc.vector.tensor_scalar(rst[:, 0], rst[:, 0], cfg["guard"], None,
                                                     ALU.max if cfg["guard"] < 1e-10 else ALU.add))
                        link(nc.vector.reciprocal(rst[:, 1], rst[:, 0]))
                        link(nc.vector.tensor_tensor(wt[:], top[:, :, 0:2], per_row(rst[:, 1], [128, FT, 2]), ALU.mult))
                    else:
                        nc.vector.tensor_tensor(rst[:, 2], top[:, :, 1], top[:, :, 0], ALU.subtract) \
                            .then_inc(sg["gap_ready"], 1)
                        dve.wait_ge(sg["gap_exp"], 1)
                        link(nc.vector.tensor_scalar(rst[:, 0], rst[:, 3], 1.0, None, ALU.add))
                        link(nc.vector.reciprocal(wt[:, :, 0], rst[:, 0]))
                        link(nc.vector.tensor_tensor(wt[:, :, 1], rst[:, 3], wt[:, :, 0], ALU.mult))
                    for n in range(FT):
                        nc.vector.tensor_scalar(c[:, n, :], k["iota"][:, 0:E], idxf[:, n, 0:1], wt[:, n, 0:1],
                                                ALU.is_equal, ALU.mult)
                        ins = nc.vector.tensor_scalar(c2[:, n, :], k["iota"][:, 0:E], idxf[:, n, 1:2], wt[:, n, 1:2],
                                                      ALU.is_equal, ALU.mult)
                    link(ins)
                    nc.vector.tensor_tensor(c[:], c[:], c2[:], ALU.add).then_inc(sg["c_ready"], 1)
                    dve.wait_ge(sg["c_ready"], 1)

                    def add_outputs(un):
                        for e in experts_of(un):
                            dve.wait_ge(sg["unit_done"], un + 1)
                            if e >= 1:
                                dve.wait_ge(sg["y_used"], e)
                            for n in range(FT):
                                ye = YP[:, e % 2, D * n:D * n + D]
                                if e == 0:
                                    ins = nc.vector.tensor_scalar(acc[:, n, :], ye, c[:, n, e:e + 1], None, ALU.mult)
                                else:
                                    ins = nc.vector.scalar_tensor_tensor(acc[:, n, :], ye, c[:, n, e:e + 1], acc[:, n, :],
                                                                         ALU.mult, ALU.add)
                            ins.then_inc(sg["y_used"], 1)

                    if glu:
                        for z, (un, la, hf) in enumerate(items):
                            cols = slice(HALF * hf, HALF * hf + HALF)
                            dve.wait_ge(sg["gate_used"], z + 1)
                            if un >= 2:
                                dve.wait_ge(sg["unit_done"], un - 1)
                            nc.vector.tensor_tensor(hT[0:M, un % 2, cols], gT[0:M, un % 2, cols],
                                                    HP[0:M, 2 * (z % 2) + 1, 0:HALF], ALU.mult).then_inc(sg["hid_used"], 1)
                            if hf == 1 and un >= 1 and (un - 1) % chunks == chunks - 1:
                                add_outputs(un - 1)
                        add_outputs(UNITS - 1)
                    else:
                        for un in range(UNITS):
                            add_outputs(un)
                    dve.wait_ge(sg["y_used"], E)
                    dve.wait_ge(sg["x_in"], 16)
                    if biased:
                        dve.wait_ge(sg["yb_done"], 1)
                        link(nc.vector.tensor_tensor(acc[:], MP[:, 0:FT * D].rearrange("p (n d) -> p n d", d=D), acc[:],
                                                     ALU.add))
                    if cfg["inner"]:
                        link(nc.vector.tensor_tensor(acc[:], acc[:], (x1 if x1 is not None else u)[:], ALU.add))
                    if cfg["post"]:
                        dve_center(nc, link, acc[:], xc[:], sq[:], stat, SH).then_inc(sg["var_ready"], 1)
                        dve.wait_ge(sg["std_ready"], 2)
                        link(dve_scale_rows(nc, link, acc[:], xc[:], stat, SH))
                        link(nc.vector.tensor_tensor(acc[:], acc[:], gb[:, 0:1, :].to_broadcast(SH), ALU.mult))
                        link(nc.vector.tensor_tensor(acc[:], acc[:], gb[:, 1:2, :].to_broadcast(SH), ALU.add))
                    nc.vector.tensor_tensor(y[:], acc[:], x[:], ALU.add).then_inc(sg["out_ready"], 1)
            sg.end_turn()


FFN = {
    "L0": dict(name="ffn0", E=8, F=64, mode="probs", guard=1e-12, pair=True, glu=False, deep=False, biased=True, chunks=1,
               act="gelu", router_bias=False, post=False, inner=True),
    "L1": dict(name="ffn1", E=16, F=128, mode="logits", guard=0.0, pair=False, glu=False, deep=False, biased=True, chunks=1,
               act="relu", router_bias=True, post=True, inner=True),
    "L2": dict(name="ffn2", E=8, F=85, mode="probs", guard=1e-9, pair=False, glu=True, deep=False, biased=False, chunks=2,
               act="silu", router_bias=False, post=False, inner=True),
    "L3": dict(name="ffn3", E=6, F=64, mode="both", guard=0.0, pair=True, glu=False, deep=True, biased=True, chunks=1,
               act="relu", router_bias=True, post=False, inner=False),
}


def ffn_weights(I, L):
    import numpy as np
    p = L + "_ffn_"
    cat = np.concatenate
    if L == "L0":
        w1 = cat([I[p + "w1"], I[p + "b1"][:, None]], 1).transpose(1, 0, 2)
        w2 = I[p + "w2"].reshape(4, 128, 64).transpose(1, 0, 2)
        return dict(w1=w1.reshape(65, 4, 128), w2=w2, b2=I[p + "b2"], rw=I[p + "router_w"].T)
    if L == "L1":
        w1 = cat([I[p + "w1"], I[p + "b1"][:, None]], 1).transpose(1, 0, 2)
        return dict(w1=w1, w2=I[p + "w2"].transpose(1, 0, 2), b2=I[p + "b2"],
                    rw=cat([I[p + "gate_w"], I[p + "gate_b"][None]]), gamma=I[p + "gamma"], beta=I[p + "beta"])
    if L == "L2":
        f = lambda n: I[p + n].transpose(2, 0, 1).reshape(64, 16, 85)
        w2 = I[p + "w2"].transpose(0, 2, 1).reshape(16, 85, 64).transpose(1, 0, 2)
        return dict(w1=f("w1"), w3=f("w3"), w2=w2, rw=I[p + "router_w"].T, ln=I[p + "ln2_w"])
    w1 = cat([I[p + "expert_w1"], I[p + "expert_b1"][:, None]], 1).transpose(1, 0, 2)
    return dict(w1=w1.reshape(65, 3, 128), w2=I[p + "expert_w3"].reshape(3, 128, 64).transpose(1, 0, 2),
                b2=I[p + "expert_b3"], rw1=cat([I[p + "router_w1"], I[p + "router_b1"][None]]),
                rw=cat([I[p + "router_w2"], I[p + "router_b2"][None]]),
                wm=I[p + "expert_w2"].reshape(3, 2, 64, 64).transpose(1, 2, 0, 3),
                bm=I[p + "expert_b2"].reshape(3, 128).T)



def linear_attention_stage(nc, k, h_in, h_out, w):
    SH = [128, NT, D]
    HEADS, HD = 8, 8
    GR = [128, NT * HEADS, HD]
    last = S % 128
    with ExitStack() as ctx:
        def sb(name, shape, dt=F32):
            return ctx.enter_context(nc.sbuf_tensor("l_" + name, shape, dt))

        sg = Signals(nc, ctx, "lin", "w_in x_in dve_step var_ready std_ready u_ready uT_done uT_copied kv_ready kv_done kvm_ready "
                              "y_done out_ready store_done")
        x, xc, sq, u, kk, vv, y = (sb(n, SH) for n in ("x", "xc", "sq", "u", "kk", "vv", "y"))
        stat, gst = sb("stat", [128, 4, NT]), sb("gst", [128, 4, NT * HEADS])
        uT = sb("uT", [D, NT * 128])
        kvm = sb("kvm", [D, D])
        blk = sb("blk", [D, D])
        wts = sb("wts", [128, 4, D])
        psT = ctx.enter_context(nc.psum_tensor("l_psT", [128, 3 * 512], F32))
        psY = ctx.enter_context(nc.psum_tensor("l_psY", [128, 2 * 512], F32))
        psK = ctx.enter_context(nc.psum_tensor("l_psK", [128, 512], F32))
        with nc.Block() as block:
            @block.sync
            def _(sp):
                for n, name in enumerate(("kw", "kb", "vw", "vb")):
                    sp.dma_start(wts[:, n, :], w[name].partition_broadcast(128)).then_inc(sg["w_in"], 16)
                sp.dma_start(blk[:], w["blk"]).then_inc(sg["w_in"], 16)
                sp.wait_ge(sg["w_in"], 80)
        sg.end_turn()
        with nc.Fori(0, B) as b:
            with nc.Block() as block:
                @block.sync
                def _(sp):
                    sp.dma_start(x[:], h_in[ds(b * S, NT * 128), :].rearrange("(n p) d -> p n d", p=128)) \
                        .then_inc(sg["x_in"], 16)
                    sp.wait_ge(sg["out_ready"], 1)
                    sp.dma_start(h_out[ds(b * S, S - last), :].rearrange("(n p) d -> p n d", p=128), y[:, 0:NT - 1]) \
                        .then_inc(sg["store_done"], 16)
                    sp.dma_start(h_out[ds(b * S + S - last, last), :], y[0:last, NT - 1]).then_inc(sg["store_done"], 16)
                    sp.wait_ge(sg["store_done"], 32)

                @block.vector
                def _(dve):
                    link = Chain(dve, sg["dve_step"])
                    g3 = lambda t: t[:].rearrange("p n (h d) -> p (n h) d", d=HD)
                    dve.wait_ge(sg["x_in"], 16)
                    dve_center(nc, link, x[:], xc[:], sq[:], stat, SH).then_inc(sg["var_ready"], 1)
                    dve.wait_ge(sg["std_ready"], 1)
                    dve_scale_rows(nc, link, u[:], xc[:], stat, SH).then_inc(sg["u_ready"], 1)
                    dve.wait_ge(sg["u_ready"], 1)
                    link(nc.vector.tensor_reduce(gst[:, 0], g3(u), AX, ALU.add))
                    link(nc.vector.tensor_scalar(gst[:, 0], gst[:, 0], -1.0 / HD, None, ALU.mult))
                    link(nc.vector.tensor_tensor(g3(xc), g3(u), per_row(gst[:, 0], GR), ALU.add))
                    link(nc.vector.tensor_tensor(sq[:], xc[:], xc[:], ALU.mult))
                    nc.vector.tensor_reduce(gst[:, 1], g3(sq), AX, ALU.add).then_inc(sg["var_ready"], 1)
                    dve.wait_ge(sg["std_ready"], 2)
                    link(nc.vector.tensor_scalar(gst[:, 2], gst[:, 2], LN_EPS, None, ALU.add))
                    link(dve_scale_rows(nc, link, g3(sq), g3(xc), gst, GR))
                    for out, i in ((kk, 0), (vv, 2)):
                        link(nc.vector.tensor_tensor(out[:], sq[:], wts[:, i:i + 1, :].to_broadcast(SH), ALU.mult))
                        nc.vector.tensor_tensor(out[:], out[:], wts[:, i + 1:i + 2, :].to_broadcast(SH), ALU.add) \
                            .then_inc(sg["kv_ready"], 1)
                    dve.wait_ge(sg["kv_done"], 1)
                    nc.vector.tensor_tensor(kvm[:], psK[0:D, 0:D], blk[:], ALU.mult).then_inc(sg["kvm_ready"], 1)
                    link(nc.vector.tensor_tensor(xc[:], u[:], x[:], ALU.add))
                    dve.wait_ge(sg["y_done"], 1)
                    nc.vector.tensor_tensor(y[:], psY[:, 0:NT * D].rearrange("p (n d) -> p n d", d=D), xc[:], ALU.add) \
                        .then_inc(sg["out_ready"], 1)

                @block.scalar
                def _(act):
                    act.wait_ge(sg["var_ready"], 1)
                    act_std(nc, stat, k["eps5"][:]).then_inc(sg["std_ready"], 1)
                    act.wait_ge(sg["uT_done"], 1)
                    nc.scalar.copy(uT[:], psT[0:D, 0:NT * 128]).then_inc(sg["uT_copied"], 1)
                    act.wait_ge(sg["var_ready"], 2)
                    nc.scalar.activation(gst[:, 2], gst[:, 1], ACT.Sqrt, bias=k["zero"][:], scale=1.0 / (HD - 1)) \
                        .then_inc(sg["std_ready"], 1)

                @block.tensor
                def _(pe):
                    pe.wait_ge(sg["u_ready"], 1)
                    for n in range(NT):
                        ins = nc.tensor.transpose(psT[0:D, 128 * n:128 * n + 128], u[:, n, :], k["ident"][:])
                    ins.then_inc(sg["uT_done"], 1)
                    pe.wait_ge(sg["kv_ready"], 2)
                    for n in range(NT):
                        m = min(128, S - 128 * n)
                        ins = nc.tensor.matmul(psK[0:D, 0:D], kk[0:m, n, :], vv[0:m, n, :], start=(n == 0),
                                               stop=(n == NT - 1))
                    ins.then_inc(sg["kv_done"], 1)
                    pe.wait_ge(sg["uT_copied"], 1)
                    pe.wait_ge(sg["kvm_ready"], 1)
                    for n in range(NT):
                        ins = nc.tensor.matmul(psY[:, D * n:D * n + D], uT[:, 128 * n:128 * n + 128], kvm[:],
                                               start=True, stop=True)
                    ins.then_inc(sg["y_done"], 1)
            sg.end_turn()



def text_stage(nc, k, h_out, w):
    EW = 75
    with ExitStack() as ctx:
        def sb(name, shape, dt=F32):
            return ctx.enter_context(nc.sbuf_tensor("t_" + name, shape, dt))

        sg = Signals(nc, ctx, "txt", "w_in tok_in preset dve_step eT_done eT_copied p_done p_copied shifted exp_ready out_ready "
                              "store_done")
        rows_in = nc.alloc_semaphore("embeddings_gathered")
        tok = sb("tok", [128, B], I32)
        e = sb("e", [128, 2, B, EW])
        eT = sb("eT", [EW + 1, 2, B * 128])
        wt = sb("wt", [EW + 1, 2, D])
        wa = sb("wa", [128, D])
        ba = sb("ba", [128, 1])
        p, q = sb("p", [128, 2 * B, D]), sb("q", [128, 2 * B, D])
        lg = sb("lg", [128, 4, 2 * B])
        psE = ctx.enter_context(nc.psum_tensor("t_psE", [128, 2, 1024], F32))
        psP = ctx.enter_context(nc.psum_tensor("t_psP", [128, 1024], F32))
        with nc.Block() as block:
            @block.sync
            def _(sp):
                sp.dma_start(tok[:], w["tokens"]).then_inc(sg["tok_in"], 16)
                sp.dma_start(wt[:], w["wt"]).then_inc(sg["w_in"], 16)
                sp.dma_start(wa[:], w["wa"].partition_broadcast(128)).then_inc(sg["w_in"], 16)
                sp.dma_start(ba[:], w["ba"].partition_broadcast(128)).then_inc(sg["w_in"], 16)
                sp.wait_ge(sg["out_ready"], 1)
                for b in range(B):
                    sp.dma_start(h_out[b * S + VIS:(b + 1) * S, :], p[:, b, :]).then_inc(sg["store_done"], 16)
                sp.wait_ge(sg["store_done"], 16 * B)

            @block.gpsimd
            def _(pool):
                pool.wait_ge(sg["tok_in"], 16)
                for i, table in enumerate((w["E0"], w["E1"])):
                    for b in range(B):
                        pool.indirect_dma_start(
                            out=e[:, i, b, :], out_offset=None, in_=table,
                            in_offset=bass.IndirectOffsetOnAxis(ap=tok[:, b:b + 1].bitcast(U32), axis=0)) \
                            .then_inc(rows_in, 16)
                pool.wait_ge(rows_in, 32 * B)

            @block.tensor
            def _(pe):
                pe.wait_ge(rows_in, 32 * B)
                for i in range(2):
                    for b in range(B):
                        ins = nc.tensor.transpose(psE[0:EW, i, 128 * b:128 * b + 128], e[:, i, b, :], k["ident"][:])
                    ins.then_inc(sg["eT_done"], 1)
                pe.wait_ge(sg["w_in"], 48)
                for i in range(2):
                    pe.wait_ge(sg["eT_copied"], i + 1)
                    for b in range(B):
                        c = D * (B * i + b)
                        ins = nc.tensor.matmul(psP[:, c:c + D], eT[:, i, 128 * b:128 * b + 128], wt[:, i, :],
                                               start=True, stop=True)
                ins.then_inc(sg["p_done"], 1)

            @block.scalar
            def _(act):
                act.wait_ge(sg["preset"], 1)
                for i in range(2):
                    act.wait_ge(sg["eT_done"], i + 1)
                    nc.scalar.copy(eT[0:EW, i, :], psE[0:EW, i, :]).then_inc(sg["eT_copied"], 1)
                act.wait_ge(sg["shifted"], 1)
                nc.scalar.activation(lg[:, 2], lg[:, 1], ACT.Exp).then_inc(sg["exp_ready"], 1)

            @block.vector
            def _(dve):
                link = Chain(dve, sg["dve_step"])
                nc.vector.memset(eT[:], 1.0).then_inc(sg["preset"], 1)
                dve.wait_ge(sg["p_done"], 1)
                dve.wait_ge(sg["w_in"], 48)
                SH = [128, 2 * B, D]
                link(nc.vector.tensor_copy(p[:], psP[:, :].rearrange("p (n d) -> p n d", d=D)))
                link(nc.vector.tensor_tensor(q[:], p[:], wa[:].unsqueeze(1).to_broadcast(SH), ALU.mult))
                link(nc.vector.tensor_reduce(lg[:, 0], q[:], AX, ALU.add))
                link(nc.vector.tensor_scalar(lg[:, 0], lg[:, 0], ba[:, 0:1], None, ALU.add))
                link(nc.vector.tensor_tensor(lg[:, 3, 0:B], lg[:, 0, 0:B], lg[:, 0, B:2 * B], ALU.max))
                nc.vector.tensor_tensor(lg[:, 1, 0:B], lg[:, 0, 0:B], lg[:, 3, 0:B], ALU.subtract)
                nc.vector.tensor_tensor(lg[:, 1, B:2 * B], lg[:, 0, B:2 * B], lg[:, 3, 0:B], ALU.subtract) \
                    .then_inc(sg["shifted"], 1)
                dve.wait_ge(sg["exp_ready"], 1)
                link(nc.vector.tensor_tensor(lg[:, 0, 0:B], lg[:, 2, 0:B], lg[:, 2, B:2 * B], ALU.add))
                link(nc.vector.reciprocal(lg[:, 0, B:2 * B], lg[:, 0, 0:B]))
                nc.vector.tensor_tensor(lg[:, 3, 0:B], lg[:, 2, 0:B], lg[:, 0, B:2 * B], ALU.mult)
                link(nc.vector.tensor_tensor(lg[:, 3, B:2 * B], lg[:, 2, B:2 * B], lg[:, 0, B:2 * B], ALU.mult))
                link(nc.vector.tensor_tensor(q[:], p[:], per_row(lg[:, 3], SH), ALU.mult))
                nc.vector.tensor_tensor(p[:, 0:B], q[:, 0:B], q[:, B:2 * B], ALU.add).then_inc(sg["out_ready"], 1)
        sg.end_turn()



HW = 96
PX = HW * HW
HALF_PX = PX // 2
CH = 9
VC = 128
KS, STRIDE = 8, 3
GI = 4
PT = GI * GRID
TILES = (B // GI) * GRID
BAND = STRIDE * HW
GRP = 4


def similarity_maps(nc, k, ctx, wn, x_d, sim_d, best_d, w):
    def sb(name, shape, dt=F32):
        return ctx.enter_context(nc.sbuf_tensor("s_" + name, shape, dt))

    sg = Signals(nc, ctx, "sim", "w_in x_in wsq_ready wn_done wstd_ready dve_step wn_ready sq_ready norm_done std_ready xn_ready "
                          "map_done map_copied map_stored px_done px_taken best_ready")
    x = sb("x", [128, HALF_PX])
    sq = sb("sq", [128, HALF_PX])
    xn = sb("xn", [128, HALF_PX])
    maps = sb("maps", [128, 2, HALF_PX])
    best = sb("best", [128, 2, 36])
    halves = sb("halves", [128, 128])
    cw = sb("cw", [128, VC])
    cq = sb("cq", [128, VC])
    PN = ctx.enter_context(nc.psum_tensor("s_PN", [128, 2, 512], F32))
    PM = ctx.enter_context(nc.psum_tensor("s_PM", [128, 3, 512], F32))
    PB = ctx.enter_context(nc.psum_tensor("s_PB", [128, 3, 512], F32))
    with nc.Block() as block:
        @block.sync
        def _(sp):
            sp.dma_start(cw[0:64, :], w["conv_wT"]).then_inc(sg["w_in"], 16)
            sp.dma_start(cw[64:128, :], w["conv_wT"]).then_inc(sg["w_in"], 16)
            sp.dma_start(halves[:], w["halves"]).then_inc(sg["w_in"], 16)

        @block.vector
        def _(dve):
            link = Chain(dve, sg["dve_step"])
            dve.wait_ge(sg["w_in"], 48)
            nc.vector.tensor_tensor(cq[:], cw[:], cw[:], ALU.mult).then_inc(sg["wsq_ready"], 1)
            dve.wait_ge(sg["wstd_ready"], 1)
            link(nc.vector.reciprocal(cq[:], cq[:]))
            link(nc.vector.tensor_tensor(wn[:], cw[:], cq[:], ALU.mult))

        @block.tensor
        def _(pe):
            pe.wait_ge(sg["w_in"], 48)
            pe.wait_ge(sg["wsq_ready"], 1)
            nc.tensor.matmul(PN[:, 0, 0:VC], halves[:], cq[:], start=True, stop=True).then_inc(sg["wn_done"], 1)

        @block.scalar
        def _(act):
            act.wait_ge(sg["wn_done"], 1)
            nc.scalar.activation(cq[:], PN[:, 0, 0:VC], ACT.Sqrt).then_inc(sg["wstd_ready"], 1)
    sg.end_turn()
    cols = lambda c: slice(512 * c, 512 * c + 512)
    with nc.Fori(0, B) as b:
        with nc.Block() as block:
            @block.sync
            def _(sp):
                for hf in range(2):
                    sp.dma_start(x[64 * hf:64 * hf + 64, :], x_d[ds(b, 1), :, HALF_PX * hf:HALF_PX * hf + HALF_PX]
                                 .rearrange("o c t -> (o c) t")).then_inc(sg["x_in"], 16)
                for hf in range(2):
                    for z, (c0, c1) in enumerate(((0, 3), (3, 6), (6, 9))):
                        sp.wait_ge(sg["map_copied"], CH * hf + c1)
                        sp.dma_start(sim_d[ds(b, 1), :, HALF_PX * hf + 512 * c0:HALF_PX * hf + 512 * c1]
                                     .rearrange("o v t -> (o v) t"), maps[:, hf, 512 * c0:512 * c1]) \
                            .then_inc(sg["map_stored"], 16)
                sp.wait_ge(sg["best_ready"], 1)
                sp.dma_start(best_d[ds(b, 1), :].rearrange("o (h p t) -> p (o h) t", h=2, p=128), best[:]) \
                    .then_inc(sg["map_stored"], 16)
                sp.wait_ge(sg["map_stored"], 7 * 16)

            @block.scalar
            def _(act):
                act.wait_ge(sg["x_in"], 32)
                for c in range(CH):
                    nc.scalar.activation(sq[:, cols(c)], x[:, cols(c)], ACT.Square).then_inc(sg["sq_ready"], 1)
                for c in range(CH):
                    act.wait_ge(sg["norm_done"], c + 1)
                    nc.scalar.activation(sq[:, cols(c)], PN[:, c % 2, :], ACT.Sqrt).then_inc(sg["std_ready"], 1)
                for z in range(2 * CH):
                    act.wait_ge(sg["map_done"], z + 1)
                    nc.scalar.copy(maps[:, z // CH, cols(z % CH)], PM[:, z % 3, :]).then_inc(sg["map_copied"], 1)

            @block.tensor
            def _(pe):
                for c in range(CH):
                    pe.wait_ge(sg["sq_ready"], c + 1)
                    if c >= 2:
                        pe.wait_ge(sg["std_ready"], c - 1)
                    nc.tensor.matmul(PN[:, c % 2, :], halves[:], sq[:, cols(c)], start=True, stop=True) \
                        .then_inc(sg["norm_done"], 1)
                for hf in range(2):
                    r = slice(64 * hf, 64 * hf + 64)
                    for c in range(CH):
                        z = CH * hf + c
                        pe.wait_ge(sg["xn_ready"], c + 1)
                        if z >= 3:
                            pe.wait_ge(sg["map_copied"], z - 2)
                        nc.tensor.matmul(PM[:, z % 3, :], wn[r, :], xn[r, cols(c)], start=True, stop=True) \
                            .then_inc(sg["map_done"], 1)
                pe.wait_ge(sg["xn_ready"], CH)
                for hf in range(2):
                    r = slice(64 * hf, 64 * hf + 64)
                    xs = xn[r, :].rearrange("c (p t) -> c p t", t=36)
                    for g in range(9):
                        z = 9 * hf + g
                        if z >= 3:
                            pe.wait_ge(sg["px_taken"], z - 2)
                        for j in range(4):
                            ins = nc.tensor.matmul(PB[:, z % 3, 128 * j:128 * j + 128], xs[:, :, 4 * g + j], wn[r, :],
                                                   start=True, stop=True)
                        ins.then_inc(sg["px_done"], 1)

            @block.vector
            def _(dve):
                link = Chain(dve, sg["dve_step"])
                for c in range(CH):
                    dve.wait_ge(sg["std_ready"], c + 1)
                    link(nc.vector.reciprocal(sq[:, cols(c)], sq[:, cols(c)]))
                    nc.vector.tensor_tensor(xn[:, cols(c)], x[:, cols(c)], sq[:, cols(c)], ALU.mult) \
                        .then_inc(sg["xn_ready"], 1)
                for z in range(18):
                    dve.wait_ge(sg["px_done"], z + 1)
                    nc.vector.tensor_reduce(best[:, z // 9, 4 * (z % 9):4 * (z % 9) + 4],
                                            PB[:, z % 3, :].rearrange("p (j v) -> p j v", v=128), AX, ALU.max) \
                        .then_inc(sg["px_taken"], 1)
                dve.wait_ge(sg["px_taken"], 18)
                nc.vector.tensor_copy(best[0:1, 0, 0:1], best[0:1, 0, 0:1]).then_inc(sg["best_ready"], 1)
        sg.end_turn()


def visual_stage(nc, k, h_out, w):
    sim_d = nc.dram_tensor("similarities", [B, VC, PX], F32).ap()
    best_d = nc.dram_tensor("best_of_pixel", [B, PX], F32).ap()
    with ExitStack() as ctx:
        def sb(c, name, shape, dt=F32):
            return c.enter_context(nc.sbuf_tensor("v_" + name, shape, dt))

        wn = sb(ctx, "wn", [128, VC])
        with ExitStack() as c2:
            similarity_maps(nc, k, c2, wn, w["x"], sim_d, best_d, w)
        pix_in = nc.alloc_semaphore("pixels_gathered")
        con_in = nc.alloc_semaphore("concepts_gathered")
        RING = 8
        band_in = [nc.alloc_semaphore(f"bands_gathered_{i}") for i in range(RING)]
        sg = Signals(nc, ctx, "vis", "w_in bands_in dve_step win_ready top_ready pix_ready sq_ready std_ready n_ready nT_done "
                              "nT_copied sv_done sv_copied concept_ready band_used mix_ready sims_ready inT_done inT_copied "
                              "h_done h_biased h_ready o_done o_ready store_done")
        xs = sb(ctx, "xs", [PT, TILES, D])
        ms = sb(ctx, "ms", [PT, TILES])
        vrow = sb(ctx, "vrow", [PT, TILES], U32)
        srow = sb(ctx, "srow", [PT, 3, TILES], U32)
        base = sb(ctx, "base", [PT, 2, TILES])
        with ExitStack() as c2:
            band = sb(c2, "band", [PT, 2, 3 * BAND])
            win = sb(c2, "win", [PT, TILES, KS * KS])
            m8 = sb(c2, "m8", [PT, TILES, 8])
            i8 = sb(c2, "i8", [PT, TILES, 8], U32)
            pos = sb(c2, "pos", [PT, 3, TILES], U32)
            posf = sb(c2, "posf", [PT, 2, TILES])
            window = lambda t: band[:, t // GRID, :].rearrange("p (r c) -> p r c", c=HW)[
                :, 0:KS, STRIDE * (t % GRID):STRIDE * (t % GRID) + KS]
            with nc.Block() as block:
                @block.sync
                def _(sp):
                    sp.dma_start(base[:], w["patch_base"]).then_inc(sg["w_in"], 16)
                    src = best_d.rearrange("b (q t) -> b q t", t=BAND)
                    for b in range(B):
                        p0 = GRID * (b % GI)
                        for z in range(3):
                            sp.dma_start(band[p0:p0 + GRID, b // GI, BAND * z:BAND * z + BAND], src[b, z:z + GRID, :]) \
                                .then_inc(sg["bands_in"], 16)

                @block.scalar
                def _(act):
                    act.wait_ge(sg["bands_in"], 16 * 24)
                    for t in range(TILES):
                        nc.scalar.copy(win[:, t, :].rearrange("p (r c) -> p r c", c=KS), window(t)) \
                            .then_inc(sg["win_ready"], 1)

                @block.vector
                def _(dve):
                    link = Chain(dve, sg["dve_step"])
                    dve.wait_ge(sg["w_in"], 16)
                    dve.wait_ge(sg["win_ready"], TILES)
                    for t in range(TILES):
                        ins = nc.vector.max(m8[:, t, :], win[:, t, :])
                    link(ins)
                    for t in range(TILES):
                        ins = nc.vector.max_index(i8[:, t, :], m8[:, t, :], win[:, t, :])
                    link(ins)
                    link(nc.vector.tensor_copy(pos[:, 2, :], i8[:, :, 0]))
                    nc.vector.tensor_scalar(pos[:, 0, :], pos[:, 2, :], 3, None, ALU.logical_shift_right)
                    link(nc.vector.tensor_scalar(pos[:, 1, :], pos[:, 2, :], 7, None, ALU.bitwise_and))
                    link(nc.vector.tensor_copy(posf[:], pos[:, 0:2, :]))
                    link(nc.vector.scalar_tensor_tensor(posf[:, 0, :], posf[:, 0, :], float(HW), posf[:, 1, :],
                                                        ALU.mult, ALU.add))
                    nc.vector.tensor_tensor(pos[:, 0, :], posf[:, 0, :], base[:, 0, :], ALU.add) \
                        .then_inc(sg["pix_ready"], 1)

                @block.gpsimd
                def _(pool):
                    pool.wait_ge(sg["pix_ready"], 1)
                    for t in range(TILES):
                        pool.indirect_dma_start(out=xs[:, t, :], out_offset=None, in_=w["x_px"],
                                                in_offset=bass.IndirectOffsetOnAxis(ap=pos[:, 0, t:t + 1], axis=0)) \
                            .then_inc(pix_in, 16)
                    pool.wait_ge(pix_in, 16 * TILES)
            sg.end_turn()
        groups = range(TILES // GRP)
        with ExitStack() as c2:
            sq = sb(c2, "sq", [PT, TILES, D])
            st = sb(c2, "st", [PT, 4, TILES])
            nT = sb(c2, "nT", [D, 2, GRP * 128])
            sv = sb(c2, "sv", [PT, 2, GRP, VC])
            m8 = sb(c2, "n8", [PT, TILES, 8])
            i8 = sb(c2, "j8", [PT, TILES, 8], U32)
            vf = sb(c2, "vf", [PT, 2, TILES])
            PT_ = c2.enter_context(nc.psum_tensor("v_PT", [128, 2, 512], F32))
            PV = c2.enter_context(nc.psum_tensor("v_PV", [128, 2, 512], F32))
            with nc.Block() as block:
                @block.vector
                def _(dve):
                    link = Chain(dve, sg["dve_step"])
                    SH = [PT, TILES, D]
                    link(nc.vector.tensor_tensor(sq[:], xs[:], xs[:], ALU.mult))
                    nc.vector.tensor_reduce(st[:, 1], sq[:], AX, ALU.add).then_inc(sg["sq_ready"], 1)
                    dve.wait_ge(sg["std_ready"], 1)
                    dve_scale_rows(nc, link, sq[:], xs[:], st, SH).then_inc(sg["n_ready"], 1)
                    for g in groups:
                        dve.wait_ge(sg["sv_copied"], g + 1)
                        for j in range(GRP):
                            ins = nc.vector.max(m8[:, GRP * g + j, :], sv[:, g % 2, j, :])
                        link(ins)
                        for j in range(GRP):
                            ins = nc.vector.max_index(i8[:, GRP * g + j, :], m8[:, GRP * g + j, :], sv[:, g % 2, j, :])
                        ins.then_inc(sg["top_ready"], 1)
                    dve.wait_ge(sg["top_ready"], len(groups))
                    nc.vector.tensor_copy(vrow[:], i8[:, :, 0]).then_inc(sg["concept_ready"], 1)
                    link(nc.vector.tensor_copy(ms[:], m8[:, :, 0]))
                    link(nc.vector.tensor_copy(vf[:, 0], i8[:, :, 0]))
                    link(nc.vector.scalar_tensor_tensor(vf[:, 1], vf[:, 0], float(PX // BAND), base[:, 1, :],
                                                        ALU.mult, ALU.add))
                    for z in range(3):
                        ins = nc.vector.tensor_scalar(srow[:, z, :], vf[:, 1], float(z), None, ALU.add)
                    link(ins)

                @block.scalar
                def _(act):
                    act.wait_ge(sg["sq_ready"], 1)
                    nc.scalar.activation(st[:, 2], st[:, 1], ACT.Sqrt).then_inc(sg["std_ready"], 1)
                    for g in groups:
                        act.wait_ge(sg["nT_done"], g + 1)
                        nc.scalar.copy(nT[:, g % 2, 0:GRP * PT], PT_[0:D, g % 2, 0:GRP * PT]).then_inc(sg["nT_copied"], 1)
                        act.wait_ge(sg["sv_done"], g + 1)
                        if g >= 2:
                            act.wait_ge(sg["top_ready"], g - 1)
                        nc.scalar.copy(sv[:, g % 2].rearrange("p j v -> p (j v)"), PV[0:PT, g % 2, :]) \
                            .then_inc(sg["sv_copied"], 1)

                @block.tensor
                def _(pe):
                    pe.wait_ge(sg["n_ready"], 1)
                    for g in groups:
                        if g >= 2:
                            pe.wait_ge(sg["nT_copied"], g - 1)
                            pe.wait_ge(sg["sv_copied"], g - 1)
                        for j in range(GRP):
                            ins = nc.tensor.transpose(PT_[0:D, g % 2, PT * j:PT * j + PT], sq[:, GRP * g + j, :],
                                                      k["ident"][0:PT, 0:PT])
                        ins.then_inc(sg["nT_done"], 1)
                        pe.wait_ge(sg["nT_copied"], g + 1)
                        for j in range(GRP):
                            ins = nc.tensor.matmul(PV[0:PT, g % 2, VC * j:VC * j + VC], nT[:, g % 2, PT * j:PT * j + PT],
                                                   wn[0:D, :], start=True, stop=True)
                        ins.then_inc(sg["sv_done"], 1)
            sg.end_turn()
        with ExitStack() as c2:
            ws = sb(c2, "ws", [PT, TILES, D])
            inp = sb(c2, "inp", [PT, TILES, 2 * D])
            bands = sb(c2, "bands", [PT, RING, 3 * BAND])
            om = sb(c2, "om", [PT, TILES])
            inT = sb(c2, "inT", [2 * D, 2, GRP * PT])
            hb = sb(c2, "hb", [96, 2, 2, GRP * PT])
            ha = sb(c2, "ha", [96, 2, 2, GRP * PT])
            w1 = sb(c2, "w1", [2 * D, 192])
            b1 = sb(c2, "b1", [96, 2])
            w2 = sb(c2, "w2", [96, 2, D])
            b2 = sb(c2, "b2", [1, D])
            one = sb(c2, "one", [1, PT])
            PI = c2.enter_context(nc.psum_tensor("v_PI", [128, 2, 512], F32))
            PH = c2.enter_context(nc.psum_tensor("v_PH", [128, 4, 512], F32))
            PO = c2.enter_context(nc.psum_tensor("v_PO", [128, 2, 512], F32))
            with nc.Block() as block:
                @block.sync
                def _(sp):
                    for dst, src in ((w1, "tW1"), (b1, "tb1"), (w2, "tW2"), (b2, "tb2"), (one, "one")):
                        sp.dma_start(dst[:], w[src]).then_inc(sg["w_in"], 16)
                    sp.wait_ge(sg["o_ready"], len(groups))
                    for b in range(B):
                        p0, t0 = GRID * (b % GI), GRID * (b // GI)
                        sp.dma_start(h_out[b * S:b * S + VIS, :].rearrange("(q t) d -> q t d", t=GRID),
                                     xs[p0:p0 + GRID, t0:t0 + GRID, :]).then_inc(sg["store_done"], 16)
                    sp.wait_ge(sg["store_done"], 16 * B)

                @block.gpsimd
                def _(pool):
                    for t in range(TILES):
                        pool.indirect_dma_start(out=ws[:, t, :], out_offset=None, in_=w["conv_w"],
                                                in_offset=bass.IndirectOffsetOnAxis(ap=vrow[:, t:t + 1], axis=0)) \
                            .then_inc(con_in, 16)
                    for t in range(TILES):
                        if t >= RING:
                            pool.wait_ge(sg["band_used"], t - RING + 1)
                        for z in range(3):
                            pool.indirect_dma_start(
                                out=bands[:, t % RING, BAND * z:BAND * z + BAND], out_offset=None, in_=sim_d.rearrange("b v (q t) -> (b v q) t", t=BAND),
                                in_offset=bass.IndirectOffsetOnAxis(ap=srow[:, z, t:t + 1], axis=0)) \
                                .then_inc(band_in[t % RING], 16)
                    for i in range(RING):
                        pool.wait_ge(band_in[i], 48 * len(range(i, TILES, RING)))

                def leaky(dve, g):
                    dve.wait_ge(sg["h_biased"], 2 * g + 2)
                    if g >= 2:
                        dve.wait_ge(sg["o_done"], g - 1)
                    nc.vector.scalar_tensor_tensor(ha[:, g % 2], hb[:, g % 2], 0.2, hb[:, g % 2], ALU.mult, ALU.max) \
                        .then_inc(sg["h_ready"], 1)

                @block.vector
                def _(dve):
                    link = Chain(dve, sg["dve_step"])
                    SH = [PT, TILES, D]
                    link(nc.vector.tensor_scalar(om[:], ms[:], -1.0, 1.0, ALU.mult, ALU.add))
                    link(nc.vector.tensor_tensor(inp[:, :, 0:D], xs[:], per_row(ms[:], SH), ALU.mult))
                    dve.wait_ge(con_in, 16 * TILES)
                    link(nc.vector.tensor_tensor(ws[:], ws[:], per_row(om[:], SH), ALU.mult))
                    nc.vector.tensor_tensor(inp[:, :, 0:D], inp[:, :, 0:D], ws[:], ALU.add).then_inc(sg["mix_ready"], 1)
                    for t in range(TILES):
                        dve.wait_ge(band_in[t % RING], 48 * (t // RING + 1))
                        nc.vector.tensor_copy(
                            inp[:, t, D:2 * D].rearrange("p (r c) -> p r c", c=KS),
                            bands[:, t % RING, :].rearrange("p (r c) -> p r c", c=HW)[
                                :, 0:KS, STRIDE * (t % GRID):STRIDE * (t % GRID) + KS]).then_inc(sg["band_used"], 1)
                        g = t // GRP
                        if t % GRP == GRP - 1 and g >= 1:
                            leaky(dve, g - 1)
                    leaky(dve, len(groups) - 1)

                def tanh(act, g):
                    act.wait_ge(sg["o_done"], g + 1)
                    act.wait_ge(sg["mix_ready"], 1)
                    nc.scalar.activation(xs[:, GRP * g:GRP * g + GRP, :].rearrange("p j d -> p (j d)"),
                                         PO[0:PT, g % 2, 0:GRP * D], ACT.Tanh).then_inc(sg["o_ready"], 1)

                @block.scalar
                def _(act):
                    act.wait_ge(sg["w_in"], 80)
                    for g in groups:
                        act.wait_ge(sg["inT_done"], g + 1)
                        if g >= 2:
                            act.wait_ge(sg["h_done"], 2 * g - 2)
                        nc.scalar.copy(inT[:, g % 2, :], PI[:, g % 2, 0:GRP * PT]).then_inc(sg["inT_copied"], 1)
                        for z in range(2):
                            act.wait_ge(sg["h_done"], 2 * g + z + 1)
                            if g >= 2:
                                act.wait_ge(sg["h_ready"], g - 1)
                            nc.scalar.activation(hb[:, g % 2, z], PH[0:96, 2 * (g % 2) + z, 0:GRP * PT], ACT.Identity,
                                                 bias=b1[:, z:z + 1]).then_inc(sg["h_biased"], 1)
                        if g >= 1:
                            tanh(act, g - 1)
                    tanh(act, len(groups) - 1)

                @block.tensor
                def _(pe):
                    pe.wait_ge(sg["w_in"], 80)
                    pe.wait_ge(sg["mix_ready"], 1)

                    def second(g):
                        pe.wait_ge(sg["h_ready"], g + 1)
                        if g >= 2:
                            pe.wait_ge(sg["o_ready"], g - 1)
                        for j in range(GRP):
                            o = PO[0:PT, g % 2, D * j:D * j + D]
                            for z in range(2):
                                nc.tensor.matmul(o, ha[:, g % 2, z, PT * j:PT * j + PT], w2[:, z, :], start=(z == 0),
                                                 stop=False)
                            ins = nc.tensor.matmul(o, one[:], b2[:], start=False, stop=True)
                        ins.then_inc(sg["o_done"], 1)

                    for g in groups:
                        pe.wait_ge(sg["band_used"], GRP * g + GRP)
                        if g >= 2:
                            pe.wait_ge(sg["inT_copied"], g - 1)
                        for j in range(GRP):
                            ins = nc.tensor.transpose(PI[:, g % 2, PT * j:PT * j + PT], inp[:, GRP * g + j, :],
                                                      k["ident"][0:PT, 0:PT])
                        ins.then_inc(sg["inT_done"], 1)
                        pe.wait_ge(sg["inT_copied"], g + 1)
                        if g >= 2:
                            pe.wait_ge(sg["h_biased"], 2 * g - 2)
                        for z in range(2):
                            nc.tensor.matmul(PH[0:96, 2 * (g % 2) + z, 0:GRP * PT], w1[:, 96 * z:96 * z + 96],
                                             inT[:, g % 2, :], start=True, stop=True).then_inc(sg["h_done"], 1)
                        if g >= 1:
                            second(g - 1)
                    second(len(groups) - 1)
            sg.end_turn()


def token_constants():
    import numpy as np
    p, t = np.arange(PT)[:, None], np.arange(TILES)[None, :]
    img = t // GRID * GI + p // GRID
    row, col = p % GRID, t % GRID
    first = img * PX + STRIDE * row * HW + STRIDE * col
    bandrow = img * VC * (PX // BAND) + row + 0 * col
    half = np.arange(128) // 64
    blk = np.arange(D) // 8
    return {
        "patch_base": np.ascontiguousarray(np.stack([first, bandrow], 1).astype(np.float32)),
        "halves": (half[:, None] == half[None, :]).astype(np.float32),
        "one": np.ones((1, PT), np.float32),
        "blk": np.where(blk[:, None] == blk[None, :], np.float32(1.0 / S), np.float32(0)).astype(np.float32),
    }



def program(nc, a, out):
    buf = [nc.dram_tensor(f"tokens_{i}", [PAD_ROWS, D], F32).ap() for i in range(2)]
    mid = nc.dram_tensor("tokens_inner", [PAD_ROWS, D], F32).ap()
    sub = lambda pre: {n[len(pre):]: v for n, v in a.items() if n.startswith(pre)}
    with ExitStack() as ctx:
        k = load_constants(nc, ctx, dict(sub("c_"), pads=buf + [mid]))
        visual_stage(nc, k, buf[0], dict(sub("c_"), **sub("tok_")))
        text_stage(nc, k, buf[0], sub("txt_"))
        attention_stage(nc, k, ATT["L0"], buf[0], buf[1], sub("a0_"))
        ffn_stage(nc, k, FFN["L0"], buf[1], buf[0], sub("f0_"))
        ones = {"ones": a["c_ones3"]}
        attention_stage(nc, k, ATT["L1"], buf[0], buf[1], dict(sub("a1_"), **ones))
        ffn_stage(nc, k, FFN["L1"], buf[1], buf[0], sub("f1_"))
        attention_stage(nc, k, ATT["L2"], buf[0], buf[1], dict(sub("a2_"), **ones))
        attention_stage(nc, k, ATT["L2f"], buf[1], None, dict(sub("a3_"), rope=a["c_rope"], **ones), x1_d=mid)
        ffn_stage(nc, k, FFN["L2"], buf[1], buf[0], sub("f2_"), x1_d=mid)
        linear_attention_stage(nc, k, buf[0], buf[1], dict(sub("a4_"), blk=a["c_blk"]))
        ffn_stage(nc, k, FFN["L3"], buf[1], out, sub("f3_"))


def lay_out(I):
    import numpy as np
    cat, st = np.concatenate, np.stack
    x = I["x"]
    a = {"c_" + n: v for n, v in {**constants(), **token_constants()}.items()}
    a.update(
        tok_x=x.reshape(B, D, PX), tok_x_px=x.transpose(0, 2, 3, 1).reshape(-1, D),
        tok_conv_wT=I["L0_tok_conv_w"].T, tok_conv_w=I["L0_tok_conv_w"], tok_tW1=I["L0_tok_W1"].T,
        tok_tb1=I["L0_tok_b1"].reshape(2, 96).T, tok_tW2=I["L0_tok_W2"].T.reshape(2, 96, D).transpose(1, 0, 2),
        tok_tb2=I["L0_tok_b2"][None],
        txt_tokens=I["x_txt"].T, txt_E0=I["L0_txt_E0"], txt_E1=I["L0_txt_E1"],
        txt_wt=st([cat([I[f"L0_txt_W{i}"], I[f"L0_txt_b{i}"][None]]) for i in (0, 1)], 1),
        txt_wa=I["L0_txt_Wa"].reshape(-1), txt_ba=I["L0_txt_ba"],
        a0_wT=I["L0_attn_w_qkv"].T, a0_wo=I["L0_attn_w_proj"].T, a0_qn=I["L0_attn_qn_w"], a0_kn=I["L0_attn_kn_w"],
        a1_wT=cat([cat([I["L1_attn_W" + n] for n in "qkv"], 1), cat([I["L1_attn_b" + n] for n in "qkv"])[None]]),
        a2_wT=I["L2_attn_w_qkv"].T, a2_wo=cat([I["L2_attn_w_proj"].T, I["L2_attn_b_proj"][None]]),
        a2_table=I["L2_attn_rel_table"],
        a2_index=st([I["L2_attn_rel_index"].reshape(WS2, WS2).T, I["L2_attn_rel_index"].reshape(WS2, WS2)]),
        a3_wT=cat([I["L2_ffn_w" + n] for n in "qkv"]).T, a3_wo=I["L2_ffn_wo"].T, a3_ln1=I["L2_ffn_ln1_w"],
        a4_kw=I["L3_attn_kln_weight"].reshape(-1), a4_kb=I["L3_attn_kln_bias"].reshape(-1),
        a4_vw=I["L3_attn_vln_weight"].reshape(-1), a4_vb=I["L3_attn_vln_bias"].reshape(-1))
    for n in range(4):
        a.update({f"f{n}_{m}": v for m, v in ffn_weights(I, f"L{n}").items()})
    return a


def kernel(**inputs):
    import numpy as np
    import concourse.bacc as bacc
    from concourse.bass_utils import run_bass_kernel_spmd

    arrays = {n: np.ascontiguousarray(v) for n, v in lay_out({n: np.asarray(v) for n, v in inputs.items()}).items()}
    nc = bacc.Bacc("TRN2", target_bir_lowering=False, num_devices=1)
    a = {n: nc.dram_tensor("in_" + n, v.shape, mybir.dt.from_np(v.dtype), kind="ExternalInput").ap()
         for n, v in arrays.items()}
    out = nc.dram_tensor("out_tokens", (F_TURNS * FTOK, D), F32, kind="ExternalOutput").ap()
    program(nc, a, out)
    r = run_bass_kernel_spmd(nc, [{"in_" + n: v for n, v in arrays.items()}], core_ids=[0])
    return r.results[0]["out_tokens"][:N_TOK].reshape(B, S, D)
```

```python
from contextlib import ExitStack

import concourse.bass as bass
from concourse import mybir

ALU = mybir.AluOpType
ACT = mybir.ActivationFunctionType
F32 = mybir.dt.float32
BF16 = mybir.dt.bfloat16
U32 = mybir.dt.uint32
I32 = mybir.dt.int32
AX = mybir.AxisListType.X
ds = bass.ds

B = 8
D = 64
GRID = 30
VIS = GRID * GRID
TXT = 128
S = VIS + TXT
N_TOK = B * S
NT = -(-S // 128)
PAD_ROWS = (B - 1) * S + NT * 128 + 100
FT = 5
FTOK = FT * 128
F_TURNS = -(-N_TOK // FTOK)
PAD_ROWS = max(PAD_ROWS, F_TURNS * FTOK)
LN_EPS = 1e-5
RMS_EPS = 1e-6
WS2 = 49
NEG = -1e30
COMBOS = [(0, 0), (0, 1), (1, 0), (1, 1), (0, 2), (2, 0), (1, 2), (2, 1)]


class Signals:

    def __init__(self, nc, ctx, stage, names):
        self.nc = nc
        self.all = {n: ctx.enter_context(nc.semaphore(f"{stage}_{n}")) for n in names.split()}

    def __getitem__(self, name):
        return self.all[name]

    def end_turn(self):
        for s in self.all.values():
            self.nc.sync.sem_clear(s)
        self.nc.all_engine_barrier()


class Chain:

    def __init__(self, eng, sem):
        self.eng, self.sem, self.n = eng, sem, 0

    def __call__(self, ins):
        ins.then_inc(self.sem, 1)
        self.n += 1
        self.eng.wait_ge(self.sem, self.n)


def per_row(stat, shape):
    return stat.unsqueeze(len(shape) - 1).to_broadcast(shape)


def dve_center(nc, link, x, xc, sq, stat, shape):
    link(nc.vector.tensor_reduce(stat[:, 0], x, AX, ALU.add))
    link(nc.vector.tensor_scalar(stat[:, 0], stat[:, 0], -1.0 / D, None, ALU.mult))
    link(nc.vector.tensor_tensor(xc, x, per_row(stat[:, 0], shape), ALU.add))
    link(nc.vector.tensor_tensor(sq, xc, xc, ALU.mult))
    return nc.vector.tensor_reduce(stat[:, 1], sq, AX, ALU.add)


def dve_scale_rows(nc, link, out, xc, stat, shape):
    link(nc.vector.reciprocal(stat[:, 3], stat[:, 2]))
    return nc.vector.tensor_tensor(out, xc, per_row(stat[:, 3], shape), ALU.mult)


def act_std(nc, stat, eps, n=D):
    return nc.scalar.activation(stat[:, 2], stat[:, 1], ACT.Sqrt, bias=eps, scale=1.0 / n)



def load_constants(nc, ctx, c):
    k = {}

    def sb(name, shape, dt):
        k[name] = ctx.enter_context(nc.sbuf_tensor("k_" + name, shape, dt))
        return k[name]

    sg = Signals(nc, ctx, "k", "const_in const_set")
    ident = sb("ident", [128, 128], F32)
    identb = sb("identb", [128, 128], BF16)
    mask_st = sb("mask_st", [128, 128], BF16)
    mask_ts = sb("mask_ts", [128, 128], BF16)
    shift = sb("shift", [WS2, 132], F32)
    iota = sb("iota", [128, 16], F32)
    eps5 = sb("eps5", [128, 1], F32)
    eps6 = sb("eps6", [128, 1], F32)
    zero = sb("zero", [128, 1], F32)
    zrows = sb("zrows", [128, 128], F32)
    with nc.Block() as block:
        @block.sync
        def _(sp):
            for t, n in ((ident, "ident"), (identb, "identb"), (mask_st, "mask_st"), (mask_ts, "mask_ts"),
                         (shift, "shift"), (iota, "iota")):
                sp.dma_start(t[:], c[n]).then_inc(sg["const_in"], 16)
            sp.wait_ge(sg["const_in"], 6 * 16)
            sp.wait_ge(sg["const_set"], 4)
            for n, h in enumerate(c["pads"]):
                rows = PAD_ROWS - N_TOK
                half = rows // 2
                sp.dma_start(h[N_TOK:N_TOK + 2 * half, :].rearrange("(p a) d -> p (a d)", a=2),
                             zrows[0:half, :]).then_inc(sg["const_in"], 16)
                sp.wait_ge(sg["const_in"], (7 + n) * 16)

        @block.vector
        def _(dve):
            nc.vector.memset(eps5[:], LN_EPS).then_inc(sg["const_set"], 1)
            nc.vector.memset(eps6[:], RMS_EPS).then_inc(sg["const_set"], 1)
            nc.vector.memset(zero[:], 0.0).then_inc(sg["const_set"], 1)
            nc.vector.memset(zrows[:], 0.0).then_inc(sg["const_set"], 1)
    sg.end_turn()
    return k



def heads_acc(cfg):
    return min(cfg["heads_turn"], max(1, 32 // (cfg["hd"] + 1))) // (cfg["hq"] // cfg["hk"]) or 1


def v_cols(cfg):
    return 32 if cfg["hd"] < 32 else cfg["hd"] + 32


def attention_project(nc, k, cfg, h_in, w, parts_d, v_d, x_d):
    hd, hq, hk = cfg["hd"], cfg["hq"], cfg["hk"]
    QK = D + hk * hd
    W = QK + hk * hd
    KR = D + 1 if cfg["bias"] else D
    SH = [128, NT, D]
    with ExitStack() as ctx:
        def sb(name, shape, dt=F32):
            return ctx.enter_context(nc.sbuf_tensor(f"{cfg['name']}_p_{name}", shape, dt))

        sg = Signals(nc, ctx, cfg["name"] + "_p", "w_in x_in ones_set dve_step act_step var_ready std_ready u_ready uT_done uT_copied "
                              "qkv_done v_copied qk_ready part_ready part_turned part_copied store_done")
        x, xc, sq, u = (sb(n, SH) for n in ("x", "xc", "sq", "u"))
        stat = sb("stat", [128, 4, NT])
        uT = sb("uT", [128, NT * 128])
        wT = sb("wT", [128, W])
        qk = sb("qk", [128, NT, QK])
        qk2 = sb("qk2", [128, NT, QK])
        part = sb("part", [128, 3, NT, QK], BF16)
        partT = sb("partT", [QK, 3, NT * 128], BF16)
        hpa, VR = heads_acc(cfg), v_cols(cfg)
        va = sb("va", [128, NT, hk, VR])
        pstat = sb("pstat", [128, 4, NT * 64]) if cfg["kind"] == "rmspair" else None
        nw = sb("nw", [128, QK]) if cfg["kind"] == "rmspair" else None
        ln1 = sb("ln1", [128, D]) if cfg["kind"] == "rope" else None
        rope = sb("rope", [128, 2, NT, 16]) if cfg["kind"] == "rope" else None
        psT = ctx.enter_context(nc.psum_tensor(f"{cfg['name']}_p_psT", [128, 3 * 512], F32))
        psQ = ctx.enter_context(nc.psum_tensor(f"{cfg['name']}_p_psQ", [128, 5 * 512], F32))
        qkv = psQ[:, :].rearrange("p (n w) -> p n w", w=256)[:, 0:NT, :]
        turned = [psT[:, :].bitcast(BF16)[0:QK, 0:NT * 128], psQ[:, 0:1024].bitcast(BF16)[0:QK, 0:NT * 128],
                  psQ[:, 1024:2048].bitcast(BF16)[0:QK, 0:NT * 128]]
        n_w = 0
        with nc.Block() as block:
            @block.sync
            def _(sp):
                n = 0
                sp.wait_ge(sg["ones_set"], 3)
                loads = [(wT[0:KR, :], w["wT"])]
                if nw is not None:
                    loads += [(nw[:, 0:D].rearrange("p (h d) -> p h d", d=2),
                               w["qn"].partition_broadcast(128).unsqueeze(1).to_broadcast([128, 32, 2])),
                              (nw[:, D:QK].rearrange("p (h d) -> p h d", d=2),
                               w["kn"].partition_broadcast(128).unsqueeze(1).to_broadcast([128, 32, 2]))]
                if ln1 is not None:
                    loads += [(ln1[:], w["ln1"].partition_broadcast(128)), (rope[:], w["rope"])]
                for dst, src in loads:
                    sp.dma_start(dst, src).then_inc(sg["w_in"], 16)
                    n += 16
                    sp.wait_ge(sg["w_in"], n)

            @block.vector
            def _(dve):
                nc.vector.memset(va[:], 0.0).then_inc(sg["ones_set"], 1)
                nc.vector.memset(uT[:], 0.0).then_inc(sg["ones_set"], 1)
                nc.vector.memset(wT[:], 0.0).then_inc(sg["ones_set"], 1)
                dve.wait_ge(sg["ones_set"], 3)
                nc.vector.memset(uT[D:D + 1, :], 1.0).then_inc(sg["ones_set"], 1)
                dve.wait_ge(sg["ones_set"], 4)
                for i in range(hpa):
                    nc.vector.memset(va[:, :, i:hk:hpa, hpa * hd + i:hpa * hd + i + 1], 1.0).then_inc(sg["ones_set"], 1)
                dve.wait_ge(sg["ones_set"], 4 + hpa)
        sg.end_turn()
        with nc.Fori(0, B) as b:
            with nc.Block() as block:
                @block.sync
                def _(sp):
                    sp.dma_start(x[:], h_in[ds(b * S, NT * 128), :].rearrange("(n p) d -> p n d", p=128)) \
                        .then_inc(sg["x_in"], 16)
                    sp.wait_ge(sg["v_copied"], 1)
                    sp.dma_start(v_d[ds(b, 1)].rearrange("o p n v -> p (o n) v"),
                                 va[:].rearrange("p n h e -> p n (h e)")).then_inc(sg["store_done"], 16)
                    n = 16
                    if x_d is not None:
                        sp.wait_ge(sg["u_ready"], 1)
                        sp.dma_start(x_d[ds(b * NT * 128, NT * 128), :].rearrange("(n p) d -> p n d", p=128), u[:]) \
                            .then_inc(sg["store_done"], 16)
                        n += 16
                    for i in range(3):
                        sp.wait_ge(sg["part_copied"], i + 1)
                        sp.dma_start(parts_d[ds(b * 3 + i, 1)].rearrange("o r t -> (o r) t"), partT[:, i, 0:S]) \
                            .then_inc(sg["store_done"], 16)
                        n += 16
                    sp.wait_ge(sg["store_done"], n)

                @block.vector
                def _(dve):
                    link = Chain(dve, sg["dve_step"])
                    dve.wait_ge(sg["x_in"], 16)
                    dve_center(nc, link, x[:], xc[:], sq[:], stat, SH).then_inc(sg["var_ready"], 1)
                    dve.wait_ge(sg["std_ready"], 1)
                    ins = dve_scale_rows(nc, link, u[:], xc[:], stat, SH)
                    feed = u
                    if ln1 is not None:
                        ins.then_inc(sg["u_ready"], 1)
                        dve.wait_ge(sg["u_ready"], 1)
                        link(nc.vector.tensor_tensor(sq[:], u[:], u[:], ALU.mult))
                        nc.vector.tensor_reduce(stat[:, 1], sq[:], AX, ALU.add).then_inc(sg["var_ready"], 1)
                        dve.wait_ge(sg["std_ready"], 2)
                        link(dve_scale_rows(nc, link, xc[:], u[:], stat, SH))
                        ins = nc.vector.tensor_tensor(x[:], xc[:], ln1[:].unsqueeze(1).to_broadcast(SH), ALU.mult)
                        feed = x
                    ins.then_inc(sg["u_ready"], 1)
                    dve.wait_ge(sg["qkv_done"], 1)
                    vs = qkv[:, :, QK:W].rearrange("p n (h d) -> p n h d", d=hd)
                    for i in range(hpa):
                        ins = nc.vector.tensor_copy(va[:, :, i:hk:hpa, i * hd:i * hd + hd], vs[:, :, i:hk:hpa, :])
                    ins.then_inc(sg["v_copied"], 1)
                    dve.wait_ge(sg["qk_ready"], 1)
                    src, oth = qk, qk2
                    if cfg["kind"] == "rmspair":
                        pairs = [128, NT * 64, 2]
                        v3 = lambda t: t[:].rearrange("p n (h d) -> p (n h) d", d=2)
                        link(nc.vector.tensor_tensor(oth[:], src[:], src[:], ALU.mult))
                        nc.vector.tensor_reduce(pstat[:, 1], v3(oth), AX, ALU.add).then_inc(sg["var_ready"], 1)
                        dve.wait_ge(sg["std_ready"], 2)
                        link(dve_scale_rows(nc, link, v3(oth), v3(src), pstat, pairs))
                        link(nc.vector.tensor_tensor(src[:], oth[:], nw[:].unsqueeze(1).to_broadcast([128, NT, QK]),
                                                     ALU.mult))
                    if cfg["kind"] == "rope":
                        H = QK // 16
                        for hh in range(H):
                            q_, o_ = src[:, :, 16 * hh:16 * hh + 16], oth[:, :, 16 * hh:16 * hh + 16]
                            nc.vector.tensor_tensor(o_[:, :, 0:8], q_[:, :, 8:16], rope[:, 1, :, 0:8], ALU.mult)
                            ins = nc.vector.tensor_tensor(o_[:, :, 8:16], q_[:, :, 0:8], rope[:, 1, :, 8:16], ALU.mult)
                        link(ins)
                        for hh in range(H):
                            q_ = src[:, :, 16 * hh:16 * hh + 16]
                            ins = nc.vector.tensor_tensor(q_, q_, rope[:, 0], ALU.mult)
                        link(ins)
                        link(nc.vector.tensor_tensor(src[:], src[:], oth[:], ALU.add))
                    link(nc.vector.tensor_scalar(src[:, :, 0:D], src[:, :, 0:D], float(hd) ** -0.5, None, ALU.mult))
                    nc.vector.tensor_copy(part[:, 0], src[:]).then_inc(sg["part_ready"], 1)
                    dve.wait_ge(sg["part_ready"], 1)
                    link(nc.vector.tensor_tensor(oth[:], src[:], part[:, 0], ALU.subtract))
                    nc.vector.tensor_copy(part[:, 1], oth[:]).then_inc(sg["part_ready"], 1)
                    dve.wait_ge(sg["part_ready"], 2)
                    link(nc.vector.tensor_tensor(src[:], oth[:], part[:, 1], ALU.subtract))
                    nc.vector.tensor_copy(part[:, 2], src[:]).then_inc(sg["part_ready"], 1)
                    for i in range(3):
                        dve.wait_ge(sg["part_turned"], i + 1)
                        nc.vector.tensor_copy(partT[:, i], turned[i]).then_inc(sg["part_copied"], 1)

                @block.scalar
                def _(act):
                    act.wait_ge(sg["var_ready"], 1)
                    act_std(nc, stat, k["eps5"][:]).then_inc(sg["std_ready"], 1)
                    if ln1 is not None:
                        act.wait_ge(sg["var_ready"], 2)
                        act_std(nc, stat, k["eps6"][:]).then_inc(sg["std_ready"], 1)
                    act.wait_ge(sg["uT_done"], 1)
                    nc.scalar.copy(uT[0:D, :], psT[0:D, 0:NT * 128]).then_inc(sg["uT_copied"], 1)
                    act.wait_ge(sg["v_copied"], 1)
                    nc.scalar.copy(qk[:], qkv[:, :, 0:QK]).then_inc(sg["qk_ready"], 1)
                    if cfg["kind"] == "rmspair":
                        act.wait_ge(sg["var_ready"], 2)
                        act_std(nc, pstat, k["eps6"][:], 2).then_inc(sg["std_ready"], 1)

                @block.tensor
                def _(pe):
                    feed = x if ln1 is not None else u
                    pe.wait_ge(sg["u_ready"], 2 if ln1 is not None else 1)
                    for n in range(NT):
                        ins = nc.tensor.transpose(psT[0:D, n * 128:n * 128 + 128], feed[:, n, :], k["ident"][:])
                    ins.then_inc(sg["uT_done"], 1)
                    pe.wait_ge(sg["uT_copied"], 1)
                    for n in range(NT):
                        ins = nc.tensor.matmul(qkv[:, n, 0:W], uT[:, n * 128:n * 128 + 128], wT[:, :],
                                               start=True, stop=True)
                    ins.then_inc(sg["qkv_done"], 1)
                    pe.wait_ge(sg["v_copied"], 1)
                    pe.wait_ge(sg["qk_ready"], 1)
                    for i in range(3):
                        pe.wait_ge(sg["part_ready"], i + 1)
                        for n in range(NT):
                            ins = nc.tensor.transpose(turned[i][:, n * 128:n * 128 + 128], part[:, i, n, :],
                                                      k["identb"][:])
                        ins.then_inc(sg["part_turned"], 1)
            sg.end_turn()


def gather_bias(nc, ctx, sg, table, index, tiles):
    idx = [ctx.enter_context(nc.sbuf_tensor(f"bias_idx{i}", [WS2, WS2], I32)) for i in range(2)]
    gathered = nc.alloc_semaphore("bias_gathered")
    with nc.Block() as block:
        @block.sync
        def _(sp):
            sp.dma_start(idx[0][:], index[0]).then_inc(sg["loaded"], 16)
            sp.dma_start(idx[1][:], index[1]).then_inc(sg["loaded"], 16)

        @block.gpsimd
        def _(pool):
            pool.wait_ge(sg["loaded"], 32)
            n = 0
            for i in range(2):
                for c in range(WS2):
                    pool.indirect_dma_start(
                        out=tiles[i][:, c, :], out_offset=None, in_=table,
                        in_offset=bass.IndirectOffsetOnAxis(ap=idx[i][:, c:c + 1].bitcast(U32), axis=0)) \
                        .then_inc(gathered, 16)
                    n += 16
            pool.wait_ge(gathered, n)
    sg.end_turn()


def attention_core(nc, k, cfg, parts_d, v_d, nm_d, o_d, w):
    hd, hk, rep = cfg["hd"], cfg["hk"], cfg["hq"] // cfg["hk"]
    HG = cfg["heads_turn"]
    KG = HG // rep
    G = cfg["hq"] // HG
    causal, window, shifted = cfg["causal"], cfg["window"], cfg["rowmax"]
    HS = cfg["stack"]
    combos = COMBOS if hd * HS * len(COMBOS) <= 128 and not shifted else COMBOS[0:6]
    per = min(len(combos), 128 // (hd * HS))
    NCH = len(combos) // per
    R0 = per * hd * HS
    RX = 3 * HS if (shifted and NCH == 1) else 0
    hpa, VR = heads_acc(cfg), v_cols(cfg)
    RW = hpa * (hd + 1)
    accs = [list(range(a, min(a + hpa, HG))) for a in range(0, HG, hpa)]
    acc_of = {h: a for a, hs in enumerate(accs) for h in hs}
    if hd > 32:
        pieces = [(0, 512, 0, hd, 0, 0, 0), (512, 1024, 0, hd, 64, 0, 0), (1024, S, 0, hd, 0, 1, 0),
                  (0, 512, hd, VR, 64, 1, 0), (512, 1024, hd, VR, 96, 1, 0), (1024, S, hd, VR, 0, 1, 8)]
        held = 1
        evac = [(0, 128, 0, 0, 512), (64, 64, 1, 0, 512), (0, 64, 1, 0, S - 1024), (0, 32, 1, 8, S - 1024)]
        stores = [(0, hd, 0, 0, 0, 0, 512), (64, hd, 0, 0, 0, 512, 512), (0, hd, 1, 0, 0, 1024, S - 1024),
                  (64, 1, 1, 0, hd, 0, 512), (96, 1, 1, 0, hd, 512, 512), (0, 1, 1, 8, hd, 1024, S - 1024)]
    elif causal:
        pieces = [(128 * i, min(128 * i + 128, S), 0, VR, 32 * (i % 4), 0, 128 * (i // 4)) for i in range(NT)]
        held = 2
        evac = [(0, 128, 0, 0, 256), (0, 32, 0, 256, S - 1024)]
        stores = [(0, RW, 0, 256, 0, 1024, S - 1024)]
    else:
        CW = S // 4
        pieces = [(CW * i, CW * i + CW, 0, VR, 32 * i, 0, 0) for i in range(4)]
        held = 2
        evac = [(0, 128, 0, 0, CW)]
        stores = [(32 * i, RW, 0, 0, 0, CW * i, CW) for i in range(4)]
    n_stores = len(stores) + (4 if causal else 0)
    if causal:
        groups = [[(0, 0)]] + [[(j, 0), (NT - 1 - j, S - 128 * j)] for j in range(1, NT // 2)] + [[(NT // 2, 0)]]
        groups[1].append((NT - 1, 2 * S - 128 * (NT - 1)))
    else:
        groups = [[(j, 0)] for j in range(NT)]
    steps = [(h, g) for h in range(HG) for g in range(len(groups))]
    q_tiles = [(h, i) for h in range(HG) for i in range(NT)]
    rows = lambda i: min(128, S - 128 * i)
    width = lambda j: S - 128 * j if causal else S
    key_rows = lambda j: 128 if causal else rows(j)
    PW = max(base + width(j) for g in groups for j, base in g)
    QKR = D + hk * hd
    with ExitStack() as ctx:
        def sb(name, shape, dt=F32):
            return ctx.enter_context(nc.sbuf_tensor(f"{cfg['name']}_c_{name}", shape, dt))

        sg = Signals(nc, ctx, cfg["name"] + "_c", "loaded dve_step logits_ready max_taken nm_ready nmT_done nmT_copied nm_stored negmax_in "
                              "scores_ready exp_done pv_done o_taken own_ready rows_set store_done bound_in bound_set")
        QA = sb("QA", [128, NCH, HG // HS, NT * 128], BF16)
        KA = sb("KA", [128, NCH, KG // HS, NT * 128], BF16)
        if HS > 1:
            KM = sb("KM", [128, HG, NT * 128], BF16)
            own = sb("own", [128, HS])
            km = lambda c, h: KM[:, h, :]
        else:
            km = lambda c, h: KA[:, c, h // rep, :]
        V = sb("V", [128, NT, KG, VR])
        P = sb("P", [128, 2, PW])
        O = sb("O", [128, max(2, len(accs)), 512])
        if shifted:
            NM = sb("NM", [128, HG * NT])
            nmp = sb("nmp", [128, 3, HG * NT], BF16)
            nmT = sb("nmT", [HG * NT, 3, 128], BF16)
            if NCH > 1:
                QX = sb("QX", [128, HG, NT * 128], BF16)
                KX = sb("KX", [128, NT * 128], BF16)
        if not shifted:
            wq = sb("wq", [128, 2])
            wk = sb("wk", [128, 2])
            bound = sb("bound", [128, 1])
        blank = [QA, KA] + ([QX, KX] if shifted and NCH > 1 else [])
        SC = ctx.enter_context(nc.psum_tensor(f"{cfg['name']}_c_SC", [128, 2, 3 * 512], F32))
        OP = ctx.enter_context(nc.psum_tensor(f"{cfg['name']}_c_OP", [128, 2, 512], F32))

        if window:
            biases = [sb("biasT", [WS2, WS2, 8]), sb("biasA", [WS2, WS2, 8])]
            gather_bias(nc, ctx, sg, w["table"], w["index"], biases)
        with nc.Block() as block:
            @block.sync
            def _(sp):
                n_in = 0
                sp.wait_ge(sg["rows_set"], len(blank))
                if HS > 1:
                    sp.dma_start(own[:], w["own"]).then_inc(sg["loaded"], 16)
                    n_in += 16
                if shifted:
                    dst = KA[R0:R0 + RX, 0, :, 0:S] if NCH == 1 else KX[0:3, 0:S].unsqueeze(1)
                    n = KG // HS if NCH == 1 else 1
                    sp.dma_start(dst, w["ones"][0:max(RX, 3), 0:n * S].rearrange("r (h t) -> r h t", t=S)) \
                        .then_inc(sg["loaded"], 16)
                    n_in += 16
                if n_in:
                    sp.wait_ge(sg["loaded"], n_in)
                if not shifted:
                    sp.dma_start(wq[:], w["qn"].partition_broadcast(128)).then_inc(sg["bound_in"], 16)
                    sp.dma_start(wk[:], w["kn"].partition_broadcast(128)).then_inc(sg["bound_in"], 16)

            @block.vector
            def _(dve):
                for t in blank:
                    nc.vector.memset(t[:], 0.0).then_inc(sg["rows_set"], 1)
                if shifted:
                    nc.vector.memset(NM[:], 0.0).then_inc(sg["bound_set"], 1)
                    dve.wait_ge(sg["bound_set"], 1)
                else:
                    link = Chain(dve, sg["dve_step"])
                    dve.wait_ge(sg["bound_in"], 32)
                    link(nc.vector.tensor_tensor(wq[:], wq[:], wk[:], ALU.mult))
                    link(nc.vector.tensor_reduce(bound[:], wq[:], AX, ALU.max, apply_absolute_value=True))
                    link(nc.vector.tensor_scalar(bound[:], bound[:], -(float(hd) ** 0.5), None, ALU.mult))
        sg.end_turn()

        def turn(b, g):
            with nc.Block() as block:
                @block.sync
                def _(sp):
                    n = 0
                    for c, (pq, pk) in enumerate(combos):
                        ch, r0 = c // per, (c % per) * hd * HS
                        q = parts_d[ds(b * 3 + pq, 1), ds(g * (HG * hd), HG * hd), :]
                        kk = parts_d[ds(b * 3 + pk, 1), ds(g * (KG * hd) + D, KG * hd), :]
                        sp.dma_start(QA[r0:r0 + hd * HS, ch, :, 0:S], q.rearrange("o (h d) t -> d (o h) t", d=hd * HS)) \
                            .then_inc(sg["loaded"], 16)
                        sp.dma_start(KA[r0:r0 + hd * HS, ch, :, 0:S], kk.rearrange("o (h d) t -> d (o h) t", d=hd * HS)) \
                            .then_inc(sg["loaded"], 16)
                        n += 32
                    sp.dma_start(V[:].rearrange("p n h v -> p n (h v)"),
                                 v_d[ds(b, 1), :, :, ds(g * (KG * VR), KG * VR)]
                                 .rearrange("o p n v -> p (o n) v")).then_inc(sg["loaded"], 16)
                    if shifted:
                        sp.wait_ge(sg["nmT_copied"], 1)
                        sp.dma_start(nm_d.rearrange("r m p -> m r p"), nmT[:]).then_inc(sg["nm_stored"], 16)
                        sp.wait_ge(sg["nm_stored"], 16)
                        for e in range(HS):
                            dst = QA[R0 + 3 * e:R0 + 3 * e + 3, 0, :, 0:S] if NCH == 1 else QX[0:3, :, 0:S]
                            sp.dma_start(dst, nm_d.rearrange("r (h i) p -> r h (i p)", i=NT)[:, e:HG:HS, 0:S]) \
                                .then_inc(sg["negmax_in"], 16)
                    for a in range(len(accs)):
                        sp.wait_ge(sg["o_taken"], a + 1)
                        dst = o_d[ds(b * (G * len(accs)) + g * len(accs) + a, 1)].rearrange("o r t -> (o r) t")
                        for p0, nr, bank, col, r0, t0, nt in stores:
                            sp.dma_start(dst[r0:r0 + nr, t0:t0 + nt], O[p0:p0 + nr, a + bank, col:col + nt]) \
                                .then_inc(sg["store_done"], 16)
                        if causal:
                            tiles = dst[:, 0:1024].rearrange("r (m q c) -> r q m c", q=4, c=128)
                            for q in range(4):
                                sp.dma_start(tiles[0:RW, q], O[32 * q:32 * q + RW, a, 0:256]
                                             .rearrange("r (m c) -> r m c", c=128)).then_inc(sg["store_done"], 16)
                    sp.wait_ge(sg["store_done"], 16 * n_stores * len(accs))

                def logits(buf, base, ncols, m, lhs, rhs, extra):
                    edges = [0] + [e - base for e in range(512, 1536, 512) if base < e < base + ncols] + [ncols]
                    for c0, c1 in zip(edges, edges[1:]):
                        adds = [(max(a0, c0), min(a1, c1), a0, l, r) for a0, a1, l, r in extra
                                if max(a0, c0) < min(a1, c1)]
                        ops = [(c0, c1, l, r[..., c0:c1]) for l, r in zip(lhs, rhs)]
                        ops += [(x0, x1, l, r[:, x0 - a0:x1 - a0]) for x0, x1, a0, l, r in adds]
                        for z, (x0, x1, l, r) in enumerate(ops):
                            ins = nc.tensor.matmul(SC[0:m, buf, base + x0:base + x1], l, r, start=(z == 0),
                                                   stop=(z == len(ops) - 1), skip_group_check=True)
                    return ins

                @block.tensor
                def _(pe):
                    pe.wait_ge(sg["loaded"], 16 * (2 * len(combos) + 1))
                    if shifted:
                        for z, (h, i) in enumerate(q_tiles):
                            m = rows(i)
                            if z >= 2:
                                pe.wait_ge(sg["max_taken"], z - 1)
                            t = slice(128 * i, 128 * i + m)
                            extra = []
                            if window and i >= NT - 2:
                                e0 = 0 if i == NT - 2 else 128
                                extra.append((S - WS2, S, k["shift"][:, e0:e0 + m], biases[1][:, :, h]))
                            if HS > 1 and i == 0:
                                pe.wait_ge(sg["own_ready"], h + 1)
                            logits(z % 2, 0, S, m, [QA[0:R0 if RX else 128, c, h // HS, t] for c in range(NCH)],
                                   [km(c, h)[0:R0 if RX else 128, 0:S] for c in range(NCH)], extra) \
                                .then_inc(sg["logits_ready"], 1)
                        pe.wait_ge(sg["nm_ready"], 1)
                        nt = SC[0:HG * NT, 0, 0:192].bitcast(BF16)
                        for r in range(3):
                            ins = nc.tensor.transpose(nt[:, 128 * r:128 * r + 128], nmp[:, r, :], k["identb"][:])
                        ins.then_inc(sg["nmT_done"], 1)
                        pe.wait_ge(sg["nmT_copied"], 1)
                        pe.wait_ge(sg["negmax_in"], 16 * HS)

                    def weigh(z):
                        h, g = steps[z]
                        pe.wait_ge(sg["exp_done"], z + 1)
                        a = acc_of[h]
                        first = g == 0 and h == accs[a][0]
                        if first and a >= held:
                            pe.wait_ge(sg["o_taken"], a - held + 1)
                        begun = set()
                        for j, base in groups[g]:
                            m = rows(j)
                            t_first = 128 * j if causal else 0
                            for t0, t1, v0, v1, p0, bank, col in pieces:
                                if t0 < t_first:
                                    continue
                                bank += a % 2 if held == 2 else 0
                                start = first and (p0 // 32, bank) not in begun
                                begun |= {(q, bank) for q in range(p0 // 32, -(-(p0 + v1 - v0) // 32))}
                                ins = nc.tensor.matmul(
                                    OP[p0:p0 + v1 - v0, bank, col:col + t1 - t0], V[0:m, j, h // rep, v0:v1],
                                    P[0:m, z % 2, base + t0 - t_first:base + t1 - t_first], start=start,
                                    stop=(h == accs[a][-1] and g == len(groups) - 1), skip_group_check=True)
                        ins.then_inc(sg["pv_done"], 1)

                    for z, (h, g) in enumerate(steps):
                        if z >= 2:
                            pe.wait_ge(sg["exp_done"], z - 1)
                        if HS > 1 and g == 0:
                            pe.wait_ge(sg["own_ready"], h + 1)
                        for j, base in groups[g]:
                            m, n = key_rows(j), rows(j)
                            t0 = 128 * j if causal else 0
                            s = slice(128 * j, 128 * j + m)
                            extra = []
                            if causal:
                                extra.append((0, n, k["identb"][:], k["mask_st"][:, 0:n]))
                            if window and j >= NT - 2:
                                e0 = 0 if j == NT - 2 else 128
                                extra.append((S - WS2, S, k["shift"][:, e0:e0 + m], biases[0][:, :, h]))
                            lhs = [km(c, h)[:, s] for c in range(NCH)]
                            rhs = [QA[:, c, h // HS, t0:S] for c in range(NCH)]
                            if shifted and NCH > 1:
                                lhs.append(KX[:, s])
                                rhs.append(QX[:, h, t0:S])
                            ins = logits(z % 2, base, width(j), m, lhs, rhs, extra)
                        ins.then_inc(sg["scores_ready"], 1)
                        if z >= 1:
                            weigh(z - 1)
                    weigh(len(steps) - 1)

                @block.scalar
                def _(act):
                    for z, (h, g) in enumerate(steps):
                        j, base = groups[g][-1]
                        m, n = key_rows(j), base + width(j)
                        act.wait_ge(sg["scores_ready"], z + 1)
                        if z >= 2:
                            act.wait_ge(sg["pv_done"], z - 1)
                        bias = k["zero"] if shifted else bound
                        nc.scalar.activation(P[0:m, z % 2, 0:n], SC[0:m, z % 2, 0:n], ACT.Exp, bias=bias[0:m, :]) \
                            .then_inc(sg["exp_done"], 1)

                @block.vector
                def _(dve):
                    link = Chain(dve, sg["dve_step"])
                    if HS > 1:
                        dve.wait_ge(sg["loaded"], 16 * (2 * len(combos) + 1))
                        for h in range(HG):
                            nc.vector.tensor_scalar(KM[:, h, :], KA[:, 0, h // HS, :], own[:, h % HS:h % HS + 1], None,
                                                    ALU.mult).then_inc(sg["own_ready"], 1)
                    if shifted:
                        for z, (h, i) in enumerate(q_tiles):
                            m = rows(i)
                            dve.wait_ge(sg["logits_ready"], z + 1)
                            nc.vector.tensor_reduce(NM[0:m, z:z + 1], SC[0:m, z % 2, 0:S], AX, ALU.max, negate=True) \
                                .then_inc(sg["max_taken"], 1)
                        dve.wait_ge(sg["max_taken"], len(q_tiles))
                        for r in range(3):
                            ins = nc.vector.tensor_copy(nmp[:, r, :], NM[:])
                            if r < 2:
                                link(ins)
                                link(nc.vector.tensor_tensor(NM[:], NM[:], nmp[:, r, :], ALU.subtract))
                        ins.then_inc(sg["nm_ready"], 1)
                        dve.wait_ge(sg["nmT_done"], 1)
                        nc.vector.tensor_copy(nmT[:].rearrange("m r p -> m (r p)"),
                                              SC[0:HG * NT, 0, 0:192].bitcast(BF16)).then_inc(sg["nmT_copied"], 1)
                    for a, hs in enumerate(accs):
                        dve.wait_ge(sg["pv_done"], (hs[-1] + 1) * len(groups))
                        bank0 = a % 2 if held == 2 else 0
                        for p0, nr, bank, col, n in evac:
                            ins = nc.vector.tensor_copy(O[p0:p0 + nr, a + bank, col:col + n],
                                                        OP[p0:p0 + nr, bank0 + bank, col:col + n])
                        ins.then_inc(sg["o_taken"], 1)
            sg.end_turn()

        with nc.Fori(0, B) as b:
            if G == 1:
                turn(b, 0)
            else:
                with nc.Fori(0, G) as g:
                    turn(b, g)


def attention_output(nc, k, cfg, h_in, h_out, o_d, x_d, x1_d, w):
    SH = [128, NT, D]
    hd, hq = cfg["hd"], cfg["hq"]
    hpa = heads_acc(cfg)
    n_acc = -(-cfg["heads_turn"] // hpa) * (hq // cfg["heads_turn"])
    RO = D + hq
    BT = 512 // RO
    last = S % 128
    proj = w is not None
    with ExitStack() as ctx:
        def sb(name, shape, dt=F32):
            return ctx.enter_context(nc.sbuf_tensor(f"{cfg['name']}_o_{name}", shape, dt))

        sg = Signals(nc, ctx, cfg["name"] + "_o", "w_in in_done x_in turned dve_step o_ready oT_done oT_copied y_done "
                                                  "out_ready store_done ones_set")
        OD = sb("OD", [RO, S])
        O, x, y = (sb(n, SH) for n in ("O", "x", "y"))
        rden = sb("rden", [128, NT, hq])
        oT = sb("oT", [D + 1, NT * 128])
        wT = sb("wT", [D + 1, D])
        psN = ctx.enter_context(nc.psum_tensor(f"{cfg['name']}_o_psN", [128, 3, 512], F32))
        psT = ctx.enter_context(nc.psum_tensor(f"{cfg['name']}_o_psT", [128, 3 * 512], F32))
        psY = ctx.enter_context(nc.psum_tensor(f"{cfg['name']}_o_psY", [128, 2 * 512], F32))
        KR = D + 1 if cfg["out_bias"] else D
        with nc.Block() as block:
            @block.sync
            def _(sp):
                if proj:
                    sp.dma_start(wT[0:KR, :], w).then_inc(sg["w_in"], 16)
                    sp.wait_ge(sg["w_in"], 16)

            @block.vector
            def _(dve):
                nc.vector.memset(oT[:], 1.0).then_inc(sg["ones_set"], 1)
                nc.vector.memset(O[:], 0.0).then_inc(sg["ones_set"], 1)
                dve.wait_ge(sg["ones_set"], 2)
        sg.end_turn()
        with nc.Fori(0, B) as b:
            with nc.Block() as block:
                @block.sync
                def _(sp):
                    src = o_d[ds(b * n_acc, n_acc)]
                    for a in range(n_acc):
                        n = min(hpa, hq - a * hpa)
                        h0 = a * hpa
                        sp.dma_start(OD[h0 * hd:(h0 + n) * hd, :], src[a, 0:n * hd, 0:S]).then_inc(sg["in_done"], 16)
                        sp.dma_start(OD[D + h0:D + h0 + n, :], src[a, hpa * hd:hpa * hd + n, 0:S]) \
                            .then_inc(sg["in_done"], 16)
                    if x_d is None:
                        src = h_in[ds(b * S, NT * 128), :]
                    else:
                        src = x_d[ds(b * NT * 128, NT * 128), :]
                    sp.dma_start(x[:], src.rearrange("(n p) d -> p n d", p=128)).then_inc(sg["x_in"], 16)
                    sp.wait_ge(sg["out_ready"], 1)
                    out = h_out if x1_d is None else x1_d
                    sp.dma_start(out[ds(b * S, S - last), :].rearrange("(n p) d -> p n d", p=128), y[:, 0:NT - 1]) \
                        .then_inc(sg["store_done"], 16)
                    sp.dma_start(out[ds(b * S + S - last, last), :], y[0:last, NT - 1]).then_inc(sg["store_done"], 16)
                    sp.wait_ge(sg["store_done"], 32)

                @block.tensor
                def _(pe):
                    pe.wait_ge(sg["in_done"], 32 * n_acc)
                    for n in range(NT):
                        m = min(128, S - 128 * n)
                        c = RO * (n % BT)
                        ins = nc.tensor.transpose(psN[0:m, n // BT, c:c + RO], OD[:, 128 * n:128 * n + m],
                                                  k["ident"][0:RO, 0:RO])
                    ins.then_inc(sg["turned"], 1)
                    if proj:
                        pe.wait_ge(sg["o_ready"], 1)
                        for n in range(NT):
                            ins = nc.tensor.transpose(psT[0:D, n * 128:n * 128 + 128], O[:, n, :], k["ident"][:])
                        ins.then_inc(sg["oT_done"], 1)
                        pe.wait_ge(sg["oT_copied"], 1)
                        for n in range(NT):
                            ins = nc.tensor.matmul(psY[:, n * D:n * D + D], oT[0:KR, n * 128:n * 128 + 128], wT[0:KR, :],
                                                   start=True, stop=True)
                        ins.then_inc(sg["y_done"], 1)

                @block.scalar
                def _(act):
                    if proj:
                        act.wait_ge(sg["oT_done"], 1)
                        nc.scalar.copy(oT[0:D, :], psT[0:D, 0:NT * 128]).then_inc(sg["oT_copied"], 1)

                @block.vector
                def _(dve):
                    link = Chain(dve, sg["dve_step"])
                    dve.wait_ge(sg["turned"], 1)
                    parts = [(128, n, min(n + BT, NT - 1)) for n in range(0, NT - 1, BT)] + [(last, NT - 1, NT)]
                    for m, n0, n1 in parts:
                        c = RO * (n0 % BT)
                        t = psN[0:m, n0 // BT, c:c + RO * (n1 - n0)].rearrange("p (n r) -> p n r", r=RO)
                        link(nc.vector.reciprocal(rden[0:m, n0:n1, :], t[:, :, D:RO]))
                        for n in range(n0, n1):
                            ins = nc.vector.tensor_tensor(
                                O[0:m, n, :].rearrange("p (h d) -> p h d", d=hd),
                                t[:, n - n0, 0:D].rearrange("p (h d) -> p h d", d=hd),
                                per_row(rden[0:m, n, :], [m, hq, hd]), ALU.mult)
                    ins.then_inc(sg["o_ready"], 1)
                    dve.wait_ge(sg["x_in"], 16)
                    if proj:
                        dve.wait_ge(sg["y_done"], 1)
                        a = psY[:, 0:NT * D].rearrange("p (n d) -> p n d", d=D)
                    else:
                        dve.wait_ge(sg["o_ready"], 1)
                        a = O[:]
                    nc.vector.tensor_tensor(y[:], a, x[:], ALU.add).then_inc(sg["out_ready"], 1)
            sg.end_turn()


def attention_stage(nc, k, cfg, h_in, h_out, w, x1_d=None):
    name = cfg["name"]
    hd, hk = cfg["hd"], cfg["hk"]
    parts_d = nc.dram_tensor(name + "_parts", [B * 3, D + hk * hd, S], BF16).ap()
    v_d = nc.dram_tensor(name + "_v", [B, 128, NT, hk * v_cols(cfg)], F32).ap()
    hpa = heads_acc(cfg)
    n_acc = -(-cfg["heads_turn"] // hpa) * (cfg["hq"] // cfg["heads_turn"])
    o_d = nc.dram_tensor(name + "_o", [B * n_acc, hpa * (hd + 1), NT * 128], F32).ap()
    nm_d = nc.dram_tensor(name + "_nm", [3, cfg["heads_turn"] * NT, 128], BF16).ap()
    x_d = nc.dram_tensor(name + "_x", [B * NT * 128, D], F32).ap() if x1_d is not None else None
    attention_project(nc, k, cfg, h_in, w, parts_d, v_d, x_d)
    attention_core(nc, k, cfg, parts_d, v_d, nm_d, o_d, w)
    attention_output(nc, k, cfg, h_in, h_out, o_d, x_d, x1_d, w.get("wo"))


ATT = {
    "L0": dict(name="att0", stack=8, hd=2, hq=32, hk=32, heads_turn=32, causal=True, window=False, rowmax=False, bias=False, kind="rmspair",
               out_bias=False),
    "L1": dict(name="att1", stack=1, hd=64, hq=1, hk=1, heads_turn=1, causal=False, window=False, rowmax=True, bias=True, kind="plain",
               out_bias=False),
    "L2": dict(name="att2", stack=2, hd=8, hq=8, hk=8, heads_turn=8, causal=False, window=True, rowmax=True, bias=False, kind="plain",
               out_bias=True),
    "L2f": dict(name="att2f", stack=1, hd=16, hq=4, hk=2, heads_turn=4, causal=True, window=False, rowmax=True, bias=False, kind="rope",
                out_bias=False),
}


def own_rows(hd, stack, extra):
    import numpy as np
    head = np.concatenate([np.tile(np.repeat(np.arange(stack), hd), 6 if extra else 8), np.repeat(np.arange(stack), extra)])
    head = np.concatenate([head, np.full(128 - len(head), stack)])
    return (head[:, None] == np.arange(stack)[None, :]).astype(np.float32)


def constants():
    import numpy as np
    from concourse import mybir as mb
    bf = mb.dt.np(mb.dt.bfloat16)
    r = np.arange(128)
    inv = 1.0 / 10000.0 ** (np.arange(0, 16, 2, dtype=np.float32) / 16)
    emb = np.outer(np.arange(NT * 128, dtype=np.float32), inv)
    emb = np.concatenate([emb, emb], -1)
    sin = np.sin(emb)
    sin[:, :8] *= -1
    rope = np.stack([np.cos(emb), sin]).reshape(2, NT, 128, 16).transpose(2, 0, 1, 3)
    return {
        "ident": np.eye(128, dtype=np.float32),
        "identb": np.eye(128, dtype=np.float32).astype(bf),
        "mask_st": np.where(r[:, None] > r[None, :], NEG, 0.0).astype(np.float32).astype(bf),
        "mask_ts": np.where(r[None, :] > r[:, None], NEG, 0.0).astype(np.float32).astype(bf),
        "shift": (np.arange(WS2)[:, None] == np.arange(132)[None, :] - (S - WS2) % 128).astype(np.float32),
        "iota": np.tile(np.arange(16, dtype=np.float32), (128, 1)),
        "rope": np.ascontiguousarray(rope.astype(np.float32)),
        "ones3": np.ones((6, 8 * S), np.float32).astype(bf),
        "own0": own_rows(2, 8, 0),
        "own2": own_rows(8, 2, 3),
    }



def ffn_stage(nc, k, cfg, h_in, h_out, w, x1_d=None):
    E, F, mode = cfg["E"], cfg["F"], cfg["mode"]
    EP = max(8, E)
    pair, glu, deep, biased = cfg["pair"], cfg["glu"], cfg["deep"], cfg["biased"]
    chunks = cfg["chunks"]
    UNITS = E // 2 if pair else E * chunks
    M = 128
    layers = 2 if deep else 1
    KR = D + 1 if biased else D
    SH = [128, FT, D]
    HALF = FTOK // 2
    FUNC = {"gelu": ACT.Gelu, "relu": ACT.Relu, "silu": ACT.Silu}[cfg["act"]]
    RH = 32
    experts_of = (lambda u: (2 * u, 2 * u + 1)) if pair else (lambda u: (u // chunks,))
    n_std = 2 if cfg["post"] else 1
    with ExitStack() as ctx:
        def sb(name, shape, dt=F32):
            return ctx.enter_context(nc.sbuf_tensor(f"{cfg['name']}_{name}", shape, dt))

        sg = Signals(nc, ctx, cfg["name"], "w_in x_in x1_in preset dve_step var_ready std_ready u_ready uT_done uT_copied rh_done "
                              "rh_copied logits_done shifted_ready exp_ready gap_ready gap_exp c_ready cT_done cT_copied "
                              "yb_done hid_done hid_used gate_used unit_done y_used out_ready store_done")
        x, xc, sq, u, y = (sb(n, SH) for n in ("x", "xc", "sq", "u", "y"))
        x1 = sb("x1", SH) if x1_d is not None else None
        stat = sb("stat", [128, 4, FT])
        uT = sb("uT", [128, FTOK])
        w1 = sb("w1", [128, UNITS, M])
        w3 = sb("w3", [128, UNITS, M]) if glu else None
        wm = sb("wm", [128, UNITS, 128]) if deep else None
        bm = sb("bm", [128, UNITS]) if deep else None
        w2 = sb("w2", [128, UNITS, D])
        b2 = sb("b2", [E, D]) if biased else None
        rw = sb("rw", [128, E])
        rw1 = sb("rw1", [128, RH]) if deep else None
        rhT = sb("rhT", [128, FTOK]) if deep else None
        gb = sb("gb", [128, 2, D]) if cfg["post"] else None
        lnw = sb("lnw", [128, D]) if x1_d is not None else None
        hT = sb("hT", [128, 2, FTOK])
        gT = sb("gT", [128, 2, FTOK]) if (deep or glu) else None
        lg = sb("lg", [128, FT, EP])
        top = sb("top", [128, FT, 8])
        idx = sb("idx", [128, FT, 8], U32)
        idxf = sb("idxf", [128, FT, 8])
        rst = sb("rst", [128, 4, FT])
        wt = sb("wt", [128, FT, 2])
        c = sb("c", [128, FT, E])
        c2 = sb("c2", [128, FT, E])
        cT = sb("cT", [E, FTOK])
        acc = sb("acc", SH)
        HP = ctx.enter_context(nc.psum_tensor(f"{cfg['name']}_HP", [128, 4, 512], F32))
        YP = ctx.enter_context(nc.psum_tensor(f"{cfg['name']}_YP", [128, 2, 512], F32))
        MP = ctx.enter_context(nc.psum_tensor(f"{cfg['name']}_MP", [128, 2 * 512], F32))
        lgP = MP[:, 768:768 + FT * 16].rearrange("p (n e) -> p n e", e=16)
        blank = [uT, w1, w2, rw, c, c2] + ([w3] if glu else []) + ([rw1, rhT, wm] if deep else [])
        n_preset = len(blank) + (3 if deep else 2)
        REXT = D + 1 if cfg["router_bias"] else D
        with nc.Block() as block:
            @block.sync
            def _(sp):
                sp.wait_ge(sg["preset"], n_preset)
                FU = M if pair else F
                loads = [(w1[0:KR, :, 0:FU], w["w1"]), (rw[0:(RH + 1 if deep else REXT), :], w["rw"])]
                if chunks == 1:
                    loads.append((w2[:], w["w2"]))
                else:
                    loads.append((w2[0:F], w["w2"]))
                if glu:
                    loads.append((w3[0:KR, :, 0:FU], w["w3"]))
                if biased:
                    loads.append((b2[:], w["b2"]))
                if deep:
                    loads += [(rw1[0:KR], w["rw1"]), (bm[:], w["bm"]),
                              (wm[0:64, :, 0:64], w["wm"][0]), (wm[64:128, :, 64:128], w["wm"][1])]
                if cfg["post"]:
                    loads += [(gb[:, 0, :], w["gamma"].partition_broadcast(128)),
                              (gb[:, 1, :], w["beta"].partition_broadcast(128))]
                if lnw is not None:
                    loads.append((lnw[:], w["ln"].partition_broadcast(128)))
                for n, (dst, src) in enumerate(loads):
                    sp.dma_start(dst, src).then_inc(sg["w_in"], 16)
                    sp.wait_ge(sg["w_in"], 16 * (n + 1))

            @block.vector
            def _(dve):
                for t in blank:
                    nc.vector.memset(t[:], 0.0).then_inc(sg["preset"], 1)
                nc.vector.memset(lg[:], NEG).then_inc(sg["preset"], 1)
                dve.wait_ge(sg["preset"], len(blank) + 1)
                nc.vector.memset(uT[D:D + 1, :], 1.0).then_inc(sg["preset"], 1)
                if deep:
                    nc.vector.memset(rhT[RH:RH + 1, :], 1.0).then_inc(sg["preset"], 1)
                dve.wait_ge(sg["preset"], n_preset)
        sg.end_turn()
        items = [(un, la, hf) for un in range(UNITS) for la in range(layers) for hf in range(2)]
        unit_items = 2 * layers
        with nc.Fori(0, F_TURNS) as it:
            with nc.Block() as block:
                @block.sync
                def _(sp):
                    tok = lambda t: t[ds(it * FTOK, FTOK), :].rearrange("(p n) d -> p n d", n=FT)
                    if x1 is not None:
                        sp.dma_start(x1[:], tok(x1_d)).then_inc(sg["x1_in"], 16)
                    sp.dma_start(x[:], tok(h_in)).then_inc(sg["x_in"], 16)
                    sp.wait_ge(sg["out_ready"], 1)
                    sp.dma_start(tok(h_out), y[:]).then_inc(sg["store_done"], 16)
                    sp.wait_ge(sg["store_done"], 16)

                @block.tensor
                def _(pe):
                    pe.wait_ge(sg["u_ready"], 1)
                    for n in range(FT):
                        ins = nc.tensor.transpose(MP[0:D, 128 * n:128 * n + 128], u[:, n, :], k["ident"][:])
                    ins.then_inc(sg["uT_done"], 1)
                    pe.wait_ge(sg["uT_copied"], 1)
                    if deep:
                        for hf in range(2):
                            ins = nc.tensor.matmul(MP[0:RH, 512 * hf:512 * hf + HALF], rw1[:],
                                                   uT[:, HALF * hf:HALF * hf + HALF], start=True, stop=True)
                        ins.then_inc(sg["rh_done"], 1)
                        pe.wait_ge(sg["rh_copied"], 2)
                    for n in range(FT):
                        src = (rhT if deep else uT)[:, 128 * n:128 * n + 128]
                        ins = nc.tensor.matmul(lgP[:, n, 0:E], src, rw[:],
                                               start=True, stop=True)
                    ins.then_inc(sg["logits_done"], 1)

                    def hidden(un):
                        for la in range(layers):
                            for hf in range(2):
                                z = items.index((un, la, hf))
                                cols = slice(HALF * hf, HALF * hf + HALF)
                                if glu:
                                    if z >= 2:
                                        pe.wait_ge(sg["hid_used"], z - 1)
                                    nc.tensor.matmul(HP[0:M, 2 * (z % 2), 0:HALF], w1[:, un, :], uT[:, cols],
                                                     start=True, stop=True)
                                    nc.tensor.matmul(HP[0:M, 2 * (z % 2) + 1, 0:HALF], w3[:, un, :], uT[:, cols],
                                                     start=True, stop=True).then_inc(sg["hid_done"], 1)
                                    continue
                                if z >= 4:
                                    pe.wait_ge(sg["hid_used"], z - 3)
                                if la == 0:
                                    ins = nc.tensor.matmul(HP[0:M, z % 4, 0:HALF], w1[:, un, :], uT[:, cols],
                                                           start=True, stop=True)
                                else:
                                    pe.wait_ge(sg["hid_used"], z - 1)
                                    ins = nc.tensor.matmul(HP[0:M, z % 4, 0:HALF], wm[:, un, :], gT[:, un % 2, cols],
                                                           start=True, stop=True)
                                ins.then_inc(sg["hid_done"], 1)

                    def outputs(un):
                        pe.wait_ge(sg["hid_used"], (un + 1) * unit_items)
                        for e in experts_of(un):
                            ch = un % chunks
                            if ch == 0 and e >= 2:
                                pe.wait_ge(sg["y_used"], e - 1)
                            p0 = 64 * (e % 2) if pair else 0
                            r = slice(p0, p0 + F) if pair else slice(0, 128)
                            for n in range(FT):
                                ins = nc.tensor.matmul(YP[:, e % 2, D * n:D * n + D], hT[r, un % 2, 128 * n:128 * n + 128],
                                                       w2[r, un, :], start=(ch == 0 and n == 0), stop=(ch == chunks - 1),
                                                       skip_group_check=True)
                        ins.then_inc(sg["unit_done"], 1)

                    for un in range(UNITS):
                        hidden(un)
                        if un >= 1:
                            outputs(un - 1)
                    outputs(UNITS - 1)
                    if biased:
                        pe.wait_ge(sg["c_ready"], 1)
                        for n in range(FT):
                            ins = nc.tensor.transpose(MP[0:E, 128 * n:128 * n + 128], c[:, n, :], k["ident"][:])
                        ins.then_inc(sg["cT_done"], 1)
                        pe.wait_ge(sg["cT_copied"], 1)
                        for n in range(FT):
                            ins = nc.tensor.matmul(MP[:, D * n:D * n + D], cT[:, 128 * n:128 * n + 128], b2[:],
                                                   start=True, stop=True)
                        ins.then_inc(sg["yb_done"], 1)

                @block.scalar
                def _(act):
                    act.wait_ge(sg["var_ready"], 1)
                    act_std(nc, stat, k["eps6" if x1 is not None else "eps5"][:]).then_inc(sg["std_ready"], 1)
                    act.wait_ge(sg["uT_done"], 1)
                    nc.scalar.copy(uT[0:D, :], MP[0:D, 0:FTOK]).then_inc(sg["uT_copied"], 1)
                    if deep:
                        act.wait_ge(sg["rh_done"], 1)
                        for hf in range(2):
                            nc.scalar.activation(rhT[0:RH, HALF * hf:HALF * hf + HALF], MP[0:RH, 512 * hf:512 * hf + HALF],
                                                 ACT.Relu).then_inc(sg["rh_copied"], 1)
                    if mode != "logits":
                        act.wait_ge(sg["shifted_ready"], 1)
                        nc.scalar.activation(lg[:, :, 0:E], lg[:, :, 0:E], ACT.Exp).then_inc(sg["exp_ready"], 1)
                    for z, (un, la, hf) in enumerate(items):
                        cols = slice(HALF * hf, HALF * hf + HALF)
                        act.wait_ge(sg["hid_done"], z + 1)
                        if glu:
                            if z >= 4:
                                act.wait_ge(sg["hid_used"], z - 3)
                            nc.scalar.activation(gT[0:M, un % 2, cols], HP[0:M, 2 * (z % 2), 0:HALF], FUNC) \
                                .then_inc(sg["gate_used"], 1)
                        else:
                            if un >= 2:
                                act.wait_ge(sg["unit_done"], un - 1)
                            dst = gT if (deep and la == 0) else hT
                            bias = bm[:, un:un + 1] if la == 1 else 0.0
                            nc.scalar.activation(dst[0:M, un % 2, cols], HP[0:M, z % 4, 0:HALF], FUNC, bias=bias) \
                                .then_inc(sg["hid_used"], 1)
                        if mode != "probs" and un == 1 and la == layers - 1 and hf == 1:
                            act.wait_ge(sg["gap_ready"], 1)
                            nc.scalar.activation(rst[:, 3], rst[:, 2], ACT.Exp).then_inc(sg["gap_exp"], 1)
                    if biased:
                        act.wait_ge(sg["cT_done"], 1)
                        nc.scalar.copy(cT[:], MP[0:E, 0:FTOK]).then_inc(sg["cT_copied"], 1)
                    if cfg["post"]:
                        act.wait_ge(sg["var_ready"], 2)
                        act_std(nc, stat, k["eps5"][:]).then_inc(sg["std_ready"], 1)

                @block.vector
                def _(dve):
                    link = Chain(dve, sg["dve_step"])
                    if x1 is not None:
                        dve.wait_ge(sg["x1_in"], 16)
                        link(nc.vector.tensor_tensor(sq[:], x1[:], x1[:], ALU.mult))
                        nc.vector.tensor_reduce(stat[:, 1], sq[:], AX, ALU.add).then_inc(sg["var_ready"], 1)
                        dve.wait_ge(sg["std_ready"], 1)
                        link(dve_scale_rows(nc, link, xc[:], x1[:], stat, SH))
                        nc.vector.tensor_tensor(u[:], xc[:], lnw[:].unsqueeze(1).to_broadcast(SH), ALU.mult) \
                            .then_inc(sg["u_ready"], 1)
                    else:
                        dve.wait_ge(sg["x_in"], 16)
                        dve_center(nc, link, x[:], xc[:], sq[:], stat, SH).then_inc(sg["var_ready"], 1)
                        dve.wait_ge(sg["std_ready"], 1)
                        dve_scale_rows(nc, link, u[:], xc[:], stat, SH).then_inc(sg["u_ready"], 1)
                    dve.wait_ge(sg["logits_done"], 1)
                    if mode == "logits":
                        link(nc.vector.tensor_copy(lg[:, :, 0:E], lgP[:, :, 0:E]))
                    else:
                        link(nc.vector.tensor_reduce(rst[:, 0], lgP[:, :, 0:E], AX, ALU.max))
                        nc.vector.tensor_tensor(lg[:, :, 0:E], lgP[:, :, 0:E], per_row(rst[:, 0], [128, FT, E]),
                                                ALU.subtract).then_inc(sg["shifted_ready"], 1)
                        dve.wait_ge(sg["exp_ready"], 1)
                        link(nc.vector.tensor_reduce(rst[:, 0], lg[:, :, 0:E], AX, ALU.add))
                        link(nc.vector.reciprocal(rst[:, 1], rst[:, 0]))
                        link(nc.vector.tensor_tensor(lg[:, :, 0:E], lg[:, :, 0:E], per_row(rst[:, 1], [128, FT, E]),
                                                     ALU.mult))
                    for n in range(FT):
                        ins = nc.vector.max(top[:, n, :], lg[:, n, :])
                    link(ins)
                    for n in range(FT):
                        ins = nc.vector.max_index(idx[:, n, :], top[:, n, :], lg[:, n, :])
                    link(ins)
                    link(nc.vector.tensor_copy(idxf[:], idx[:]))
                    if mode == "probs":
                        link(nc.vector.tensor_tensor(rst[:, 0], top[:, :, 0], top[:, :, 1], ALU.add))
                        link(nc.vector.tensor_scalar(rst[:, 0], rst[:, 0], cfg["guard"], None,
                                                     ALU.max if cfg["guard"] < 1e-10 else ALU.add))
                        link(nc.vector.reciprocal(rst[:, 1], rst[:, 0]))
                        link(nc.vector.tensor_tensor(wt[:], top[:, :, 0:2], per_row(rst[:, 1], [128, FT, 2]), ALU.mult))
                    else:
                        nc.vector.tensor_tensor(rst[:, 2], top[:, :, 1], top[:, :, 0], ALU.subtract) \
                            .then_inc(sg["gap_ready"], 1)
                        dve.wait_ge(sg["gap_exp"], 1)
                        link(nc.vector.tensor_scalar(rst[:, 0], rst[:, 3], 1.0, None, ALU.add))
                        link(nc.vector.reciprocal(wt[:, :, 0], rst[:, 0]))
                        link(nc.vector.tensor_tensor(wt[:, :, 1], rst[:, 3], wt[:, :, 0], ALU.mult))
                    for n in range(FT):
                        nc.vector.tensor_scalar(c[:, n, :], k["iota"][:, 0:E], idxf[:, n, 0:1], wt[:, n, 0:1],
                                                ALU.is_equal, ALU.mult)
                        ins = nc.vector.tensor_scalar(c2[:, n, :], k["iota"][:, 0:E], idxf[:, n, 1:2], wt[:, n, 1:2],
                                                      ALU.is_equal, ALU.mult)
                    link(ins)
                    nc.vector.tensor_tensor(c[:], c[:], c2[:], ALU.add).then_inc(sg["c_ready"], 1)
                    dve.wait_ge(sg["c_ready"], 1)

                    def add_outputs(un):
                        for e in experts_of(un):
                            dve.wait_ge(sg["unit_done"], un + 1)
                            if e >= 1:
                                dve.wait_ge(sg["y_used"], e)
                            for n in range(FT):
                                ye = YP[:, e % 2, D * n:D * n + D]
                                if e == 0:
                                    ins = nc.vector.tensor_scalar(acc[:, n, :], ye, c[:, n, e:e + 1], None, ALU.mult)
                                else:
                                    ins = nc.vector.scalar_tensor_tensor(acc[:, n, :], ye, c[:, n, e:e + 1], acc[:, n, :],
                                                                         ALU.mult, ALU.add)
                            ins.then_inc(sg["y_used"], 1)

                    if glu:
                        for z, (un, la, hf) in enumerate(items):
                            cols = slice(HALF * hf, HALF * hf + HALF)
                            dve.wait_ge(sg["gate_used"], z + 1)
                            if un >= 2:
                                dve.wait_ge(sg["unit_done"], un - 1)
                            nc.vector.tensor_tensor(hT[0:M, un % 2, cols], gT[0:M, un % 2, cols],
                                                    HP[0:M, 2 * (z % 2) + 1, 0:HALF], ALU.mult).then_inc(sg["hid_used"], 1)
                            if hf == 1 and un >= 1 and (un - 1) % chunks == chunks - 1:
                                add_outputs(un - 1)
                        add_outputs(UNITS - 1)
                    else:
                        for un in range(UNITS):
                            add_outputs(un)
                    dve.wait_ge(sg["y_used"], E)
                    dve.wait_ge(sg["x_in"], 16)
                    if biased:
                        dve.wait_ge(sg["yb_done"], 1)
                        link(nc.vector.tensor_tensor(acc[:], MP[:, 0:FT * D].rearrange("p (n d) -> p n d", d=D), acc[:],
                                                     ALU.add))
                    if cfg["inner"]:
                        link(nc.vector.tensor_tensor(acc[:], acc[:], (x1 if x1 is not None else u)[:], ALU.add))
                    if cfg["post"]:
                        dve_center(nc, link, acc[:], xc[:], sq[:], stat, SH).then_inc(sg["var_ready"], 1)
                        dve.wait_ge(sg["std_ready"], 2)
                        link(dve_scale_rows(nc, link, acc[:], xc[:], stat, SH))
                        link(nc.vector.tensor_tensor(acc[:], acc[:], gb[:, 0:1, :].to_broadcast(SH), ALU.mult))
                        link(nc.vector.tensor_tensor(acc[:], acc[:], gb[:, 1:2, :].to_broadcast(SH), ALU.add))
                    nc.vector.tensor_tensor(y[:], acc[:], x[:], ALU.add).then_inc(sg["out_ready"], 1)
            sg.end_turn()


FFN = {
    "L0": dict(name="ffn0", E=8, F=64, mode="probs", guard=1e-12, pair=True, glu=False, deep=False, biased=True, chunks=1,
               act="gelu", router_bias=False, post=False, inner=True),
    "L1": dict(name="ffn1", E=16, F=128, mode="logits", guard=0.0, pair=False, glu=False, deep=False, biased=True, chunks=1,
               act="relu", router_bias=True, post=True, inner=True),
    "L2": dict(name="ffn2", E=8, F=85, mode="probs", guard=1e-9, pair=False, glu=True, deep=False, biased=False, chunks=2,
               act="silu", router_bias=False, post=False, inner=True),
    "L3": dict(name="ffn3", E=6, F=64, mode="both", guard=0.0, pair=True, glu=False, deep=True, biased=True, chunks=1,
               act="relu", router_bias=True, post=False, inner=False),
}


def ffn_weights(I, L):
    import numpy as np
    p = L + "_ffn_"
    cat = np.concatenate
    if L == "L0":
        w1 = cat([I[p + "w1"], I[p + "b1"][:, None]], 1).transpose(1, 0, 2)
        w2 = I[p + "w2"].reshape(4, 128, 64).transpose(1, 0, 2)
        return dict(w1=w1.reshape(65, 4, 128), w2=w2, b2=I[p + "b2"], rw=I[p + "router_w"].T)
    if L == "L1":
        w1 = cat([I[p + "w1"], I[p + "b1"][:, None]], 1).transpose(1, 0, 2)
        return dict(w1=w1, w2=I[p + "w2"].transpose(1, 0, 2), b2=I[p + "b2"],
                    rw=cat([I[p + "gate_w"], I[p + "gate_b"][None]]), gamma=I[p + "gamma"], beta=I[p + "beta"])
    if L == "L2":
        f = lambda n: I[p + n].transpose(2, 0, 1).reshape(64, 16, 85)
        w2 = I[p + "w2"].transpose(0, 2, 1).reshape(16, 85, 64).transpose(1, 0, 2)
        return dict(w1=f("w1"), w3=f("w3"), w2=w2, rw=I[p + "router_w"].T, ln=I[p + "ln2_w"])
    w1 = cat([I[p + "expert_w1"], I[p + "expert_b1"][:, None]], 1).transpose(1, 0, 2)
    return dict(w1=w1.reshape(65, 3, 128), w2=I[p + "expert_w3"].reshape(3, 128, 64).transpose(1, 0, 2),
                b2=I[p + "expert_b3"], rw1=cat([I[p + "router_w1"], I[p + "router_b1"][None]]),
                rw=cat([I[p + "router_w2"], I[p + "router_b2"][None]]),
                wm=I[p + "expert_w2"].reshape(3, 2, 64, 64).transpose(1, 2, 0, 3),
                bm=I[p + "expert_b2"].reshape(3, 128).T)



def linear_attention_stage(nc, k, h_in, h_out, w):
    SH = [128, NT, D]
    HEADS, HD = 8, 8
    GR = [128, NT * HEADS, HD]
    last = S % 128
    with ExitStack() as ctx:
        def sb(name, shape, dt=F32):
            return ctx.enter_context(nc.sbuf_tensor("l_" + name, shape, dt))

        sg = Signals(nc, ctx, "lin", "w_in x_in dve_step var_ready std_ready u_ready uT_done uT_copied kv_ready kv_done kvm_ready "
                              "y_done out_ready store_done")
        x, xc, sq, u, kk, vv, y = (sb(n, SH) for n in ("x", "xc", "sq", "u", "kk", "vv", "y"))
        stat, gst = sb("stat", [128, 4, NT]), sb("gst", [128, 4, NT * HEADS])
        uT = sb("uT", [D, NT * 128])
        kvm = sb("kvm", [D, D])
        blk = sb("blk", [D, D])
        wts = sb("wts", [128, 4, D])
        psT = ctx.enter_context(nc.psum_tensor("l_psT", [128, 3 * 512], F32))
        psY = ctx.enter_context(nc.psum_tensor("l_psY", [128, 2 * 512], F32))
        psK = ctx.enter_context(nc.psum_tensor("l_psK", [128, 512], F32))
        with nc.Block() as block:
            @block.sync
            def _(sp):
                for n, name in enumerate(("kw", "kb", "vw", "vb")):
                    sp.dma_start(wts[:, n, :], w[name].partition_broadcast(128)).then_inc(sg["w_in"], 16)
                sp.dma_start(blk[:], w["blk"]).then_inc(sg["w_in"], 16)
                sp.wait_ge(sg["w_in"], 80)
        sg.end_turn()
        with nc.Fori(0, B) as b:
            with nc.Block() as block:
                @block.sync
                def _(sp):
                    sp.dma_start(x[:], h_in[ds(b * S, NT * 128), :].rearrange("(n p) d -> p n d", p=128)) \
                        .then_inc(sg["x_in"], 16)
                    sp.wait_ge(sg["out_ready"], 1)
                    sp.dma_start(h_out[ds(b * S, S - last), :].rearrange("(n p) d -> p n d", p=128), y[:, 0:NT - 1]) \
                        .then_inc(sg["store_done"], 16)
                    sp.dma_start(h_out[ds(b * S + S - last, last), :], y[0:last, NT - 1]).then_inc(sg["store_done"], 16)
                    sp.wait_ge(sg["store_done"], 32)

                @block.vector
                def _(dve):
                    link = Chain(dve, sg["dve_step"])
                    g3 = lambda t: t[:].rearrange("p n (h d) -> p (n h) d", d=HD)
                    dve.wait_ge(sg["x_in"], 16)
                    dve_center(nc, link, x[:], xc[:], sq[:], stat, SH).then_inc(sg["var_ready"], 1)
                    dve.wait_ge(sg["std_ready"], 1)
                    dve_scale_rows(nc, link, u[:], xc[:], stat, SH).then_inc(sg["u_ready"], 1)
                    dve.wait_ge(sg["u_ready"], 1)
                    link(nc.vector.tensor_reduce(gst[:, 0], g3(u), AX, ALU.add))
                    link(nc.vector.tensor_scalar(gst[:, 0], gst[:, 0], -1.0 / HD, None, ALU.mult))
                    link(nc.vector.tensor_tensor(g3(xc), g3(u), per_row(gst[:, 0], GR), ALU.add))
                    link(nc.vector.tensor_tensor(sq[:], xc[:], xc[:], ALU.mult))
                    nc.vector.tensor_reduce(gst[:, 1], g3(sq), AX, ALU.add).then_inc(sg["var_ready"], 1)
                    dve.wait_ge(sg["std_ready"], 2)
                    link(nc.vector.tensor_scalar(gst[:, 2], gst[:, 2], LN_EPS, None, ALU.add))
                    link(dve_scale_rows(nc, link, g3(sq), g3(xc), gst, GR))
                    for out, i in ((kk, 0), (vv, 2)):
                        link(nc.vector.tensor_tensor(out[:], sq[:], wts[:, i:i + 1, :].to_broadcast(SH), ALU.mult))
                        nc.vector.tensor_tensor(out[:], out[:], wts[:, i + 1:i + 2, :].to_broadcast(SH), ALU.add) \
                            .then_inc(sg["kv_ready"], 1)
                    dve.wait_ge(sg["kv_done"], 1)
                    nc.vector.tensor_tensor(kvm[:], psK[0:D, 0:D], blk[:], ALU.mult).then_inc(sg["kvm_ready"], 1)
                    link(nc.vector.tensor_tensor(xc[:], u[:], x[:], ALU.add))
                    dve.wait_ge(sg["y_done"], 1)
                    nc.vector.tensor_tensor(y[:], psY[:, 0:NT * D].rearrange("p (n d) -> p n d", d=D), xc[:], ALU.add) \
                        .then_inc(sg["out_ready"], 1)

                @block.scalar
                def _(act):
                    act.wait_ge(sg["var_ready"], 1)
                    act_std(nc, stat, k["eps5"][:]).then_inc(sg["std_ready"], 1)
                    act.wait_ge(sg["uT_done"], 1)
                    nc.scalar.copy(uT[:], psT[0:D, 0:NT * 128]).then_inc(sg["uT_copied"], 1)
                    act.wait_ge(sg["var_ready"], 2)
                    nc.scalar.activation(gst[:, 2], gst[:, 1], ACT.Sqrt, bias=k["zero"][:], scale=1.0 / (HD - 1)) \
                        .then_inc(sg["std_ready"], 1)

                @block.tensor
                def _(pe):
                    pe.wait_ge(sg["u_ready"], 1)
                    for n in range(NT):
                        ins = nc.tensor.transpose(psT[0:D, 128 * n:128 * n + 128], u[:, n, :], k["ident"][:])
                    ins.then_inc(sg["uT_done"], 1)
                    pe.wait_ge(sg["kv_ready"], 2)
                    for n in range(NT):
                        m = min(128, S - 128 * n)
                        ins = nc.tensor.matmul(psK[0:D, 0:D], kk[0:m, n, :], vv[0:m, n, :], start=(n == 0),
                                               stop=(n == NT - 1))
                    ins.then_inc(sg["kv_done"], 1)
                    pe.wait_ge(sg["uT_copied"], 1)
                    pe.wait_ge(sg["kvm_ready"], 1)
                    for n in range(NT):
                        ins = nc.tensor.matmul(psY[:, D * n:D * n + D], uT[:, 128 * n:128 * n + 128], kvm[:],
                                               start=True, stop=True)
                    ins.then_inc(sg["y_done"], 1)
            sg.end_turn()



def text_stage(nc, k, h_out, w):
    EW = 75
    with ExitStack() as ctx:
        def sb(name, shape, dt=F32):
            return ctx.enter_context(nc.sbuf_tensor("t_" + name, shape, dt))

        sg = Signals(nc, ctx, "txt", "w_in tok_in preset dve_step eT_done eT_copied p_done p_copied shifted exp_ready out_ready "
                              "store_done")
        rows_in = nc.alloc_semaphore("embeddings_gathered")
        tok = sb("tok", [128, B], I32)
        e = sb("e", [128, 2, B, EW])
        eT = sb("eT", [EW + 1, 2, B * 128])
        wt = sb("wt", [EW + 1, 2, D])
        wa = sb("wa", [128, D])
        ba = sb("ba", [128, 1])
        p, q = sb("p", [128, 2 * B, D]), sb("q", [128, 2 * B, D])
        lg = sb("lg", [128, 4, 2 * B])
        psE = ctx.enter_context(nc.psum_tensor("t_psE", [128, 2, 1024], F32))
        psP = ctx.enter_context(nc.psum_tensor("t_psP", [128, 1024], F32))
        with nc.Block() as block:
            @block.sync
            def _(sp):
                sp.dma_start(tok[:], w["tokens"]).then_inc(sg["tok_in"], 16)
                sp.dma_start(wt[:], w["wt"]).then_inc(sg["w_in"], 16)
                sp.dma_start(wa[:], w["wa"].partition_broadcast(128)).then_inc(sg["w_in"], 16)
                sp.dma_start(ba[:], w["ba"].partition_broadcast(128)).then_inc(sg["w_in"], 16)
                sp.wait_ge(sg["out_ready"], 1)
                for b in range(B):
                    sp.dma_start(h_out[b * S + VIS:(b + 1) * S, :], p[:, b, :]).then_inc(sg["store_done"], 16)
                sp.wait_ge(sg["store_done"], 16 * B)

            @block.gpsimd
            def _(pool):
                pool.wait_ge(sg["tok_in"], 16)
                for i, table in enumerate((w["E0"], w["E1"])):
                    for b in range(B):
                        pool.indirect_dma_start(
                            out=e[:, i, b, :], out_offset=None, in_=table,
                            in_offset=bass.IndirectOffsetOnAxis(ap=tok[:, b:b + 1].bitcast(U32), axis=0)) \
                            .then_inc(rows_in, 16)
                pool.wait_ge(rows_in, 32 * B)

            @block.tensor
            def _(pe):
                pe.wait_ge(rows_in, 32 * B)
                for i in range(2):
                    for b in range(B):
                        ins = nc.tensor.transpose(psE[0:EW, i, 128 * b:128 * b + 128], e[:, i, b, :], k["ident"][:])
                    ins.then_inc(sg["eT_done"], 1)
                pe.wait_ge(sg["w_in"], 48)
                for i in range(2):
                    pe.wait_ge(sg["eT_copied"], i + 1)
                    for b in range(B):
                        c = D * (B * i + b)
                        ins = nc.tensor.matmul(psP[:, c:c + D], eT[:, i, 128 * b:128 * b + 128], wt[:, i, :],
                                               start=True, stop=True)
                ins.then_inc(sg["p_done"], 1)

            @block.scalar
            def _(act):
                act.wait_ge(sg["preset"], 1)
                for i in range(2):
                    act.wait_ge(sg["eT_done"], i + 1)
                    nc.scalar.copy(eT[0:EW, i, :], psE[0:EW, i, :]).then_inc(sg["eT_copied"], 1)
                act.wait_ge(sg["shifted"], 1)
                nc.scalar.activation(lg[:, 2], lg[:, 1], ACT.Exp).then_inc(sg["exp_ready"], 1)

            @block.vector
            def _(dve):
                link = Chain(dve, sg["dve_step"])
                nc.vector.memset(eT[:], 1.0).then_inc(sg["preset"], 1)
                dve.wait_ge(sg["p_done"], 1)
                dve.wait_ge(sg["w_in"], 48)
                SH = [128, 2 * B, D]
                link(nc.vector.tensor_copy(p[:], psP[:, :].rearrange("p (n d) -> p n d", d=D)))
                link(nc.vector.tensor_tensor(q[:], p[:], wa[:].unsqueeze(1).to_broadcast(SH), ALU.mult))
                link(nc.vector.tensor_reduce(lg[:, 0], q[:], AX, ALU.add))
                link(nc.vector.tensor_scalar(lg[:, 0], lg[:, 0], ba[:, 0:1], None, ALU.add))
                link(nc.vector.tensor_tensor(lg[:, 3, 0:B], lg[:, 0, 0:B], lg[:, 0, B:2 * B], ALU.max))
                nc.vector.tensor_tensor(lg[:, 1, 0:B], lg[:, 0, 0:B], lg[:, 3, 0:B], ALU.subtract)
                nc.vector.tensor_tensor(lg[:, 1, B:2 * B], lg[:, 0, B:2 * B], lg[:, 3, 0:B], ALU.subtract) \
                    .then_inc(sg["shifted"], 1)
                dve.wait_ge(sg["exp_ready"], 1)
                link(nc.vector.tensor_tensor(lg[:, 0, 0:B], lg[:, 2, 0:B], lg[:, 2, B:2 * B], ALU.add))
                link(nc.vector.reciprocal(lg[:, 0, B:2 * B], lg[:, 0, 0:B]))
                nc.vector.tensor_tensor(lg[:, 3, 0:B], lg[:, 2, 0:B], lg[:, 0, B:2 * B], ALU.mult)
                link(nc.vector.tensor_tensor(lg[:, 3, B:2 * B], lg[:, 2, B:2 * B], lg[:, 0, B:2 * B], ALU.mult))
                link(nc.vector.tensor_tensor(q[:], p[:], per_row(lg[:, 3], SH), ALU.mult))
                nc.vector.tensor_tensor(p[:, 0:B], q[:, 0:B], q[:, B:2 * B], ALU.add).then_inc(sg["out_ready"], 1)
        sg.end_turn()



HW = 96
PX = HW * HW
HALF_PX = PX // 2
CH = 9
VC = 128
KS, STRIDE = 8, 3
GI = 4
PT = GI * GRID
TILES = (B // GI) * GRID
BAND = STRIDE * HW
GRP = 4


def similarity_maps(nc, k, ctx, wn, x_d, sim_d, best_d, w):
    def sb(name, shape, dt=F32):
        return ctx.enter_context(nc.sbuf_tensor("s_" + name, shape, dt))

    sg = Signals(nc, ctx, "sim", "w_in x_in wsq_ready wn_done wstd_ready dve_step wn_ready sq_ready norm_done std_ready xn_ready "
                          "map_done map_copied map_stored px_done px_taken best_ready")
    x = sb("x", [128, HALF_PX])
    sq = sb("sq", [128, HALF_PX])
    xn = sb("xn", [128, HALF_PX])
    wz = sb("wz", [128, 2, VC])
    maps = sb("maps", [128, 2, HALF_PX])
    best = sb("best", [128, 2, 36])
    halves = sb("halves", [128, 128])
    cw = sb("cw", [128, VC])
    cq = sb("cq", [128, VC])
    PN = ctx.enter_context(nc.psum_tensor("s_PN", [128, 2, 512], F32))
    PM = ctx.enter_context(nc.psum_tensor("s_PM", [128, 3, 512], F32))
    PB = ctx.enter_context(nc.psum_tensor("s_PB", [128, 3, 512], F32))
    with nc.Block() as block:
        @block.sync
        def _(sp):
            sp.dma_start(cw[0:64, :], w["conv_wT"]).then_inc(sg["w_in"], 16)
            sp.dma_start(cw[64:128, :], w["conv_wT"]).then_inc(sg["w_in"], 16)
            sp.dma_start(halves[:], w["halves"]).then_inc(sg["w_in"], 16)

        @block.vector
        def _(dve):
            link = Chain(dve, sg["dve_step"])
            dve.wait_ge(sg["w_in"], 48)
            nc.vector.tensor_tensor(cq[:], cw[:], cw[:], ALU.mult).then_inc(sg["wsq_ready"], 1)
            dve.wait_ge(sg["wstd_ready"], 1)
            link(nc.vector.reciprocal(cq[:], cq[:]))
            link(nc.vector.tensor_tensor(wn[:], cw[:], cq[:], ALU.mult))
            link(nc.vector.memset(wz[:], 0.0))
            for hf in range(2):
                r = slice(64 * hf, 64 * hf + 64)
                link(nc.vector.tensor_copy(wz[r, hf, :], wn[r, :]))

        @block.tensor
        def _(pe):
            pe.wait_ge(sg["w_in"], 48)
            pe.wait_ge(sg["wsq_ready"], 1)
            nc.tensor.matmul(PN[:, 0, 0:VC], halves[:], cq[:], start=True, stop=True).then_inc(sg["wn_done"], 1)

        @block.scalar
        def _(act):
            act.wait_ge(sg["wn_done"], 1)
            nc.scalar.activation(cq[:], PN[:, 0, 0:VC], ACT.Sqrt).then_inc(sg["wstd_ready"], 1)
    sg.end_turn()
    cols = lambda c: slice(512 * c, 512 * c + 512)
    with nc.Fori(0, B) as b:
        with nc.Block() as block:
            @block.sync
            def _(sp):
                for hf in range(2):
                    sp.dma_start(x[64 * hf:64 * hf + 64, :], x_d[ds(b, 1), :, HALF_PX * hf:HALF_PX * hf + HALF_PX]
                                 .rearrange("o c t -> (o c) t")).then_inc(sg["x_in"], 16)
                for hf in range(2):
                    for z, (c0, c1) in enumerate(((0, 3), (3, 6), (6, 9))):
                        sp.wait_ge(sg["map_copied"], CH * hf + c1)
                        sp.dma_start(sim_d[ds(b, 1), :, HALF_PX * hf + 512 * c0:HALF_PX * hf + 512 * c1]
                                     .rearrange("o v t -> (o v) t"), maps[:, hf, 512 * c0:512 * c1]) \
                            .then_inc(sg["map_stored"], 16)
                sp.wait_ge(sg["best_ready"], 1)
                sp.dma_start(best_d[ds(b, 1), :].rearrange("o (h p t) -> p (o h) t", h=2, p=128), best[:]) \
                    .then_inc(sg["map_stored"], 16)
                sp.wait_ge(sg["map_stored"], 7 * 16)

            @block.scalar
            def _(act):
                act.wait_ge(sg["x_in"], 32)
                for c in range(CH):
                    nc.scalar.activation(sq[:, cols(c)], x[:, cols(c)], ACT.Square).then_inc(sg["sq_ready"], 1)
                for c in range(CH):
                    act.wait_ge(sg["norm_done"], c + 1)
                    nc.scalar.activation(sq[:, cols(c)], PN[:, c % 2, :], ACT.Sqrt).then_inc(sg["std_ready"], 1)
                for z in range(2 * CH):
                    act.wait_ge(sg["map_done"], z + 1)
                    nc.scalar.copy(maps[:, z // CH, cols(z % CH)], PM[:, z % 3, :]).then_inc(sg["map_copied"], 1)

            @block.tensor
            def _(pe):
                for c in range(CH):
                    pe.wait_ge(sg["sq_ready"], c + 1)
                    if c >= 2:
                        pe.wait_ge(sg["std_ready"], c - 1)
                    nc.tensor.matmul(PN[:, c % 2, :], halves[:], sq[:, cols(c)], start=True, stop=True) \
                        .then_inc(sg["norm_done"], 1)
                for hf in range(2):
                    for c in range(CH):
                        z = CH * hf + c
                        pe.wait_ge(sg["xn_ready"], c + 1)
                        if z >= 3:
                            pe.wait_ge(sg["map_copied"], z - 2)
                        nc.tensor.matmul(PM[:, z % 3, :], wz[:, hf, :], xn[:, cols(c)], start=True, stop=True) \
                            .then_inc(sg["map_done"], 1)
                pe.wait_ge(sg["xn_ready"], CH)
                xs = xn[:].rearrange("c (p t) -> c p t", t=36)
                for z in range(18):
                    if z >= 3:
                        pe.wait_ge(sg["px_taken"], z - 2)
                    for j in range(2):
                        ins = nc.tensor.matmul(PB[:, z % 3, 256 * j:256 * j + 256], xs[:, :, 2 * z + j],
                                               wz[:].rearrange("c h v -> c (h v)"), start=True, stop=True)
                    ins.then_inc(sg["px_done"], 1)

            @block.vector
            def _(dve):
                link = Chain(dve, sg["dve_step"])
                for c in range(CH):
                    dve.wait_ge(sg["std_ready"], c + 1)
                    link(nc.vector.reciprocal(sq[:, cols(c)], sq[:, cols(c)]))
                    nc.vector.tensor_tensor(xn[:, cols(c)], x[:, cols(c)], sq[:, cols(c)], ALU.mult) \
                        .then_inc(sg["xn_ready"], 1)
                for z in range(18):
                    dve.wait_ge(sg["px_done"], z + 1)
                    nc.vector.tensor_reduce(best[:, :, 2 * z:2 * z + 2].rearrange("p h j -> p j h"),
                                            PB[:, z % 3, :].rearrange("p (j h v) -> p j h v", h=2, v=128), AX, ALU.max) \
                        .then_inc(sg["px_taken"], 1)
                dve.wait_ge(sg["px_taken"], 18)
                nc.vector.tensor_copy(best[0:1, 0, 0:1], best[0:1, 0, 0:1]).then_inc(sg["best_ready"], 1)
        sg.end_turn()


def visual_stage(nc, k, h_out, w):
    sim_d = nc.dram_tensor("similarities", [B, VC, PX], F32).ap()
    best_d = nc.dram_tensor("best_of_pixel", [B, PX], F32).ap()
    with ExitStack() as ctx:
        def sb(c, name, shape, dt=F32):
            return c.enter_context(nc.sbuf_tensor("v_" + name, shape, dt))

        wn = sb(ctx, "wn", [128, VC])
        with ExitStack() as c2:
            similarity_maps(nc, k, c2, wn, w["x"], sim_d, best_d, w)
        pix_in = nc.alloc_semaphore("pixels_gathered")
        con_in = nc.alloc_semaphore("concepts_gathered")
        RING = 8
        band_in = [nc.alloc_semaphore(f"bands_gathered_{i}") for i in range(RING)]
        sg = Signals(nc, ctx, "vis", "w_in bands_in dve_step win_ready top_ready pix_ready sq_ready std_ready n_ready nT_done "
                              "nT_copied sv_done sv_copied concept_ready band_used mix_ready sims_ready inT_done inT_copied "
                              "h_done h_biased h_ready o_done o_ready store_done")
        xs = sb(ctx, "xs", [PT, TILES, D])
        ms = sb(ctx, "ms", [PT, TILES])
        vrow = sb(ctx, "vrow", [PT, TILES], U32)
        srow = sb(ctx, "srow", [PT, 3, TILES], U32)
        base = sb(ctx, "base", [PT, 2, TILES])
        with ExitStack() as c2:
            band = sb(c2, "band", [PT, 2, 3 * BAND])
            win = sb(c2, "win", [PT, TILES, KS * KS])
            m8 = sb(c2, "m8", [PT, TILES, 8])
            i8 = sb(c2, "i8", [PT, TILES, 8], U32)
            pos = sb(c2, "pos", [PT, 3, TILES], U32)
            posf = sb(c2, "posf", [PT, 2, TILES])
            window = lambda t: band[:, t // GRID, :].rearrange("p (r c) -> p r c", c=HW)[
                :, 0:KS, STRIDE * (t % GRID):STRIDE * (t % GRID) + KS]
            with nc.Block() as block:
                @block.sync
                def _(sp):
                    sp.dma_start(base[:], w["patch_base"]).then_inc(sg["w_in"], 16)
                    src = best_d.rearrange("b (q t) -> b q t", t=BAND)
                    for b in range(B):
                        p0 = GRID * (b % GI)
                        for z in range(3):
                            sp.dma_start(band[p0:p0 + GRID, b // GI, BAND * z:BAND * z + BAND], src[b, z:z + GRID, :]) \
                                .then_inc(sg["bands_in"], 16)

                @block.scalar
                def _(act):
                    act.wait_ge(sg["bands_in"], 16 * 24)
                    for t in range(TILES):
                        nc.scalar.copy(win[:, t, :].rearrange("p (r c) -> p r c", c=KS), window(t)) \
                            .then_inc(sg["win_ready"], 1)

                @block.vector
                def _(dve):
                    link = Chain(dve, sg["dve_step"])
                    dve.wait_ge(sg["w_in"], 16)
                    dve.wait_ge(sg["win_ready"], TILES)
                    for t in range(TILES):
                        ins = nc.vector.max(m8[:, t, :], win[:, t, :])
                    link(ins)
                    for t in range(TILES):
                        ins = nc.vector.max_index(i8[:, t, :], m8[:, t, :], win[:, t, :])
                    link(ins)
                    link(nc.vector.tensor_copy(pos[:, 2, :], i8[:, :, 0]))
                    nc.vector.tensor_scalar(pos[:, 0, :], pos[:, 2, :], 3, None, ALU.logical_shift_right)
                    link(nc.vector.tensor_scalar(pos[:, 1, :], pos[:, 2, :], 7, None, ALU.bitwise_and))
                    link(nc.vector.tensor_copy(posf[:], pos[:, 0:2, :]))
                    link(nc.vector.scalar_tensor_tensor(posf[:, 0, :], posf[:, 0, :], float(HW), posf[:, 1, :],
                                                        ALU.mult, ALU.add))
                    nc.vector.tensor_tensor(pos[:, 0, :], posf[:, 0, :], base[:, 0, :], ALU.add) \
                        .then_inc(sg["pix_ready"], 1)

                @block.gpsimd
                def _(pool):
                    pool.wait_ge(sg["pix_ready"], 1)
                    for t in range(TILES):
                        pool.indirect_dma_start(out=xs[:, t, :], out_offset=None, in_=w["x_px"],
                                                in_offset=bass.IndirectOffsetOnAxis(ap=pos[:, 0, t:t + 1], axis=0)) \
                            .then_inc(pix_in, 16)
                    pool.wait_ge(pix_in, 16 * TILES)
            sg.end_turn()
        groups = range(TILES // GRP)
        with ExitStack() as c2:
            sq = sb(c2, "sq", [PT, TILES, D])
            st = sb(c2, "st", [PT, 4, TILES])
            nT = sb(c2, "nT", [D, 2, GRP * 128])
            sv = sb(c2, "sv", [PT, 2, GRP, VC])
            m8 = sb(c2, "n8", [PT, TILES, 8])
            i8 = sb(c2, "j8", [PT, TILES, 8], U32)
            vf = sb(c2, "vf", [PT, 2, TILES])
            PT_ = c2.enter_context(nc.psum_tensor("v_PT", [128, 2, 512], F32))
            PV = c2.enter_context(nc.psum_tensor("v_PV", [128, 2, 512], F32))
            with nc.Block() as block:
                @block.vector
                def _(dve):
                    link = Chain(dve, sg["dve_step"])
                    SH = [PT, TILES, D]
                    link(nc.vector.tensor_tensor(sq[:], xs[:], xs[:], ALU.mult))
                    nc.vector.tensor_reduce(st[:, 1], sq[:], AX, ALU.add).then_inc(sg["sq_ready"], 1)
                    dve.wait_ge(sg["std_ready"], 1)
                    dve_scale_rows(nc, link, sq[:], xs[:], st, SH).then_inc(sg["n_ready"], 1)
                    for g in groups:
                        dve.wait_ge(sg["sv_copied"], g + 1)
                        for j in range(GRP):
                            ins = nc.vector.max(m8[:, GRP * g + j, :], sv[:, g % 2, j, :])
                        link(ins)
                        for j in range(GRP):
                            ins = nc.vector.max_index(i8[:, GRP * g + j, :], m8[:, GRP * g + j, :], sv[:, g % 2, j, :])
                        ins.then_inc(sg["top_ready"], 1)
                    dve.wait_ge(sg["top_ready"], len(groups))
                    nc.vector.tensor_copy(vrow[:], i8[:, :, 0]).then_inc(sg["concept_ready"], 1)
                    link(nc.vector.tensor_copy(ms[:], m8[:, :, 0]))
                    link(nc.vector.tensor_copy(vf[:, 0], i8[:, :, 0]))
                    link(nc.vector.scalar_tensor_tensor(vf[:, 1], vf[:, 0], float(PX // BAND), base[:, 1, :],
                                                        ALU.mult, ALU.add))
                    for z in range(3):
                        ins = nc.vector.tensor_scalar(srow[:, z, :], vf[:, 1], float(z), None, ALU.add)
                    link(ins)

                @block.scalar
                def _(act):
                    act.wait_ge(sg["sq_ready"], 1)
                    nc.scalar.activation(st[:, 2], st[:, 1], ACT.Sqrt).then_inc(sg["std_ready"], 1)
                    for g in groups:
                        act.wait_ge(sg["nT_done"], g + 1)
                        nc.scalar.copy(nT[:, g % 2, 0:GRP * PT], PT_[0:D, g % 2, 0:GRP * PT]).then_inc(sg["nT_copied"], 1)
                        act.wait_ge(sg["sv_done"], g + 1)
                        if g >= 2:
                            act.wait_ge(sg["top_ready"], g - 1)
                        nc.scalar.copy(sv[:, g % 2].rearrange("p j v -> p (j v)"), PV[0:PT, g % 2, :]) \
                            .then_inc(sg["sv_copied"], 1)

                @block.tensor
                def _(pe):
                    pe.wait_ge(sg["n_ready"], 1)
                    for g in groups:
                        if g >= 2:
                            pe.wait_ge(sg["nT_copied"], g - 1)
                            pe.wait_ge(sg["sv_copied"], g - 1)
                        for j in range(GRP):
                            ins = nc.tensor.transpose(PT_[0:D, g % 2, PT * j:PT * j + PT], sq[:, GRP * g + j, :],
                                                      k["ident"][0:PT, 0:PT])
                        ins.then_inc(sg["nT_done"], 1)
                        pe.wait_ge(sg["nT_copied"], g + 1)
                        for j in range(GRP):
                            ins = nc.tensor.matmul(PV[0:PT, g % 2, VC * j:VC * j + VC], nT[:, g % 2, PT * j:PT * j + PT],
                                                   wn[0:D, :], start=True, stop=True)
                        ins.then_inc(sg["sv_done"], 1)
            sg.end_turn()
        with ExitStack() as c2:
            ws = sb(c2, "ws", [PT, TILES, D])
            inp = sb(c2, "inp", [PT, TILES, 2 * D])
            bands = sb(c2, "bands", [PT, RING, 3 * BAND])
            om = sb(c2, "om", [PT, TILES])
            inT = sb(c2, "inT", [2 * D, 2, GRP * PT])
            hb = sb(c2, "hb", [96, 2, 2, GRP * PT])
            ha = sb(c2, "ha", [96, 2, 2, GRP * PT])
            w1 = sb(c2, "w1", [2 * D, 192])
            b1 = sb(c2, "b1", [96, 2])
            w2 = sb(c2, "w2", [96, 2, D])
            b2 = sb(c2, "b2", [1, D])
            one = sb(c2, "one", [1, PT])
            PI = c2.enter_context(nc.psum_tensor("v_PI", [128, 2, 512], F32))
            PH = c2.enter_context(nc.psum_tensor("v_PH", [128, 4, 512], F32))
            PO = c2.enter_context(nc.psum_tensor("v_PO", [128, 2, 512], F32))
            with nc.Block() as block:
                @block.sync
                def _(sp):
                    for dst, src in ((w1, "tW1"), (b1, "tb1"), (w2, "tW2"), (b2, "tb2"), (one, "one")):
                        sp.dma_start(dst[:], w[src]).then_inc(sg["w_in"], 16)
                    sp.wait_ge(sg["o_ready"], len(groups))
                    for b in range(B):
                        p0, t0 = GRID * (b % GI), GRID * (b // GI)
                        sp.dma_start(h_out[b * S:b * S + VIS, :].rearrange("(q t) d -> q t d", t=GRID),
                                     xs[p0:p0 + GRID, t0:t0 + GRID, :]).then_inc(sg["store_done"], 16)
                    sp.wait_ge(sg["store_done"], 16 * B)

                @block.gpsimd
                def _(pool):
                    for t in range(TILES):
                        pool.indirect_dma_start(out=ws[:, t, :], out_offset=None, in_=w["conv_w"],
                                                in_offset=bass.IndirectOffsetOnAxis(ap=vrow[:, t:t + 1], axis=0)) \
                            .then_inc(con_in, 16)
                    for t in range(TILES):
                        if t >= RING:
                            pool.wait_ge(sg["band_used"], t - RING + 1)
                        for z in range(3):
                            pool.indirect_dma_start(
                                out=bands[:, t % RING, BAND * z:BAND * z + BAND], out_offset=None, in_=sim_d.rearrange("b v (q t) -> (b v q) t", t=BAND),
                                in_offset=bass.IndirectOffsetOnAxis(ap=srow[:, z, t:t + 1], axis=0)) \
                                .then_inc(band_in[t % RING], 16)
                    for i in range(RING):
                        pool.wait_ge(band_in[i], 48 * len(range(i, TILES, RING)))

                def leaky(dve, g):
                    dve.wait_ge(sg["h_biased"], 2 * g + 2)
                    if g >= 2:
                        dve.wait_ge(sg["o_done"], g - 1)
                    nc.vector.scalar_tensor_tensor(ha[:, g % 2], hb[:, g % 2], 0.2, hb[:, g % 2], ALU.mult, ALU.max) \
                        .then_inc(sg["h_ready"], 1)

                @block.vector
                def _(dve):
                    link = Chain(dve, sg["dve_step"])
                    SH = [PT, TILES, D]
                    link(nc.vector.tensor_scalar(om[:], ms[:], -1.0, 1.0, ALU.mult, ALU.add))
                    link(nc.vector.tensor_tensor(inp[:, :, 0:D], xs[:], per_row(ms[:], SH), ALU.mult))
                    dve.wait_ge(con_in, 16 * TILES)
                    link(nc.vector.tensor_tensor(ws[:], ws[:], per_row(om[:], SH), ALU.mult))
                    nc.vector.tensor_tensor(inp[:, :, 0:D], inp[:, :, 0:D], ws[:], ALU.add).then_inc(sg["mix_ready"], 1)
                    for t in range(TILES):
                        dve.wait_ge(band_in[t % RING], 48 * (t // RING + 1))
                        nc.vector.tensor_copy(
                            inp[:, t, D:2 * D].rearrange("p (r c) -> p r c", c=KS),
                            bands[:, t % RING, :].rearrange("p (r c) -> p r c", c=HW)[
                                :, 0:KS, STRIDE * (t % GRID):STRIDE * (t % GRID) + KS]).then_inc(sg["band_used"], 1)
                        g = t // GRP
                        if t % GRP == GRP - 1 and g >= 1:
                            leaky(dve, g - 1)
                    leaky(dve, len(groups) - 1)

                def tanh(act, g):
                    act.wait_ge(sg["o_done"], g + 1)
                    act.wait_ge(sg["mix_ready"], 1)
                    nc.scalar.activation(xs[:, GRP * g:GRP * g + GRP, :].rearrange("p j d -> p (j d)"),
                                         PO[0:PT, g % 2, 0:GRP * D], ACT.Tanh).then_inc(sg["o_ready"], 1)

                @block.scalar
                def _(act):
                    act.wait_ge(sg["w_in"], 80)
                    for g in groups:
                        act.wait_ge(sg["inT_done"], g + 1)
                        if g >= 2:
                            act.wait_ge(sg["h_done"], 2 * g - 2)
                        nc.scalar.copy(inT[:, g % 2, :], PI[:, g % 2, 0:GRP * PT]).then_inc(sg["inT_copied"], 1)
                        for z in range(2):
                            act.wait_ge(sg["h_done"], 2 * g + z + 1)
                            if g >= 2:
                                act.wait_ge(sg["h_ready"], g - 1)
                            nc.scalar.activation(hb[:, g % 2, z], PH[0:96, 2 * (g % 2) + z, 0:GRP * PT], ACT.Identity,
                                                 bias=b1[:, z:z + 1]).then_inc(sg["h_biased"], 1)
                        if g >= 1:
                            tanh(act, g - 1)
                    tanh(act, len(groups) - 1)

                @block.tensor
                def _(pe):
                    pe.wait_ge(sg["w_in"], 80)
                    pe.wait_ge(sg["mix_ready"], 1)

                    def second(g):
                        pe.wait_ge(sg["h_ready"], g + 1)
                        if g >= 2:
                            pe.wait_ge(sg["o_ready"], g - 1)
                        for j in range(GRP):
                            o = PO[0:PT, g % 2, D * j:D * j + D]
                            for z in range(2):
                                nc.tensor.matmul(o, ha[:, g % 2, z, PT * j:PT * j + PT], w2[:, z, :], start=(z == 0),
                                                 stop=False)
                            ins = nc.tensor.matmul(o, one[:], b2[:], start=False, stop=True)
                        ins.then_inc(sg["o_done"], 1)

                    for g in groups:
                        pe.wait_ge(sg["band_used"], GRP * g + GRP)
                        if g >= 2:
                            pe.wait_ge(sg["inT_copied"], g - 1)
                        for j in range(GRP):
                            ins = nc.tensor.transpose(PI[:, g % 2, PT * j:PT * j + PT], inp[:, GRP * g + j, :],
                                                      k["ident"][0:PT, 0:PT])
                        ins.then_inc(sg["inT_done"], 1)
                        pe.wait_ge(sg["inT_copied"], g + 1)
                        if g >= 2:
                            pe.wait_ge(sg["h_biased"], 2 * g - 2)
                        for z in range(2):
                            nc.tensor.matmul(PH[0:96, 2 * (g % 2) + z, 0:GRP * PT], w1[:, 96 * z:96 * z + 96],
                                             inT[:, g % 2, :], start=True, stop=True).then_inc(sg["h_done"], 1)
                        if g >= 1:
                            second(g - 1)
                    second(len(groups) - 1)
            sg.end_turn()


def token_constants():
    import numpy as np
    p, t = np.arange(PT)[:, None], np.arange(TILES)[None, :]
    img = t // GRID * GI + p // GRID
    row, col = p % GRID, t % GRID
    first = img * PX + STRIDE * row * HW + STRIDE * col
    bandrow = img * VC * (PX // BAND) + row + 0 * col
    half = np.arange(128) // 64
    blk = np.arange(D) // 8
    return {
        "patch_base": np.ascontiguousarray(np.stack([first, bandrow], 1).astype(np.float32)),
        "halves": (half[:, None] == half[None, :]).astype(np.float32),
        "one": np.ones((1, PT), np.float32),
        "blk": np.where(blk[:, None] == blk[None, :], np.float32(1.0 / S), np.float32(0)).astype(np.float32),
    }



def program(nc, a, out):
    buf = [nc.dram_tensor(f"tokens_{i}", [PAD_ROWS, D], F32).ap() for i in range(2)]
    mid = nc.dram_tensor("tokens_inner", [PAD_ROWS, D], F32).ap()
    sub = lambda pre: {n[len(pre):]: v for n, v in a.items() if n.startswith(pre)}
    with ExitStack() as ctx:
        k = load_constants(nc, ctx, dict(sub("c_"), pads=buf + [mid]))
        visual_stage(nc, k, buf[0], dict(sub("c_"), **sub("tok_")))
        text_stage(nc, k, buf[0], sub("txt_"))
        attention_stage(nc, k, ATT["L0"], buf[0], buf[1], dict(sub("a0_"), own=a["c_own0"]))
        ffn_stage(nc, k, FFN["L0"], buf[1], buf[0], sub("f0_"))
        ones = {"ones": a["c_ones3"]}
        attention_stage(nc, k, ATT["L1"], buf[0], buf[1], dict(sub("a1_"), **ones))
        ffn_stage(nc, k, FFN["L1"], buf[1], buf[0], sub("f1_"))
        attention_stage(nc, k, ATT["L2"], buf[0], buf[1], dict(sub("a2_"), own=a["c_own2"], **ones))
        attention_stage(nc, k, ATT["L2f"], buf[1], None, dict(sub("a3_"), rope=a["c_rope"], **ones), x1_d=mid)
        ffn_stage(nc, k, FFN["L2"], buf[1], buf[0], sub("f2_"), x1_d=mid)
        linear_attention_stage(nc, k, buf[0], buf[1], dict(sub("a4_"), blk=a["c_blk"]))
        ffn_stage(nc, k, FFN["L3"], buf[1], out, sub("f3_"))


def lay_out(I):
    import numpy as np
    cat, st = np.concatenate, np.stack
    x = I["x"]
    a = {"c_" + n: v for n, v in {**constants(), **token_constants()}.items()}
    a.update(
        tok_x=x.reshape(B, D, PX), tok_x_px=x.transpose(0, 2, 3, 1).reshape(-1, D),
        tok_conv_wT=I["L0_tok_conv_w"].T, tok_conv_w=I["L0_tok_conv_w"], tok_tW1=I["L0_tok_W1"].T,
        tok_tb1=I["L0_tok_b1"].reshape(2, 96).T, tok_tW2=I["L0_tok_W2"].T.reshape(2, 96, D).transpose(1, 0, 2),
        tok_tb2=I["L0_tok_b2"][None],
        txt_tokens=I["x_txt"].T, txt_E0=I["L0_txt_E0"], txt_E1=I["L0_txt_E1"],
        txt_wt=st([cat([I[f"L0_txt_W{i}"], I[f"L0_txt_b{i}"][None]]) for i in (0, 1)], 1),
        txt_wa=I["L0_txt_Wa"].reshape(-1), txt_ba=I["L0_txt_ba"],
        a0_wT=I["L0_attn_w_qkv"].T, a0_wo=I["L0_attn_w_proj"].T, a0_qn=I["L0_attn_qn_w"], a0_kn=I["L0_attn_kn_w"],
        a1_wT=cat([cat([I["L1_attn_W" + n] for n in "qkv"], 1), cat([I["L1_attn_b" + n] for n in "qkv"])[None]]),
        a2_wT=I["L2_attn_w_qkv"].T, a2_wo=cat([I["L2_attn_w_proj"].T, I["L2_attn_b_proj"][None]]),
        a2_table=I["L2_attn_rel_table"],
        a2_index=st([I["L2_attn_rel_index"].reshape(WS2, WS2).T, I["L2_attn_rel_index"].reshape(WS2, WS2)]),
        a3_wT=cat([I["L2_ffn_w" + n] for n in "qkv"]).T, a3_wo=I["L2_ffn_wo"].T, a3_ln1=I["L2_ffn_ln1_w"],
        a4_kw=I["L3_attn_kln_weight"].reshape(-1), a4_kb=I["L3_attn_kln_bias"].reshape(-1),
        a4_vw=I["L3_attn_vln_weight"].reshape(-1), a4_vb=I["L3_attn_vln_bias"].reshape(-1))
    for n in range(4):
        a.update({f"f{n}_{m}": v for m, v in ffn_weights(I, f"L{n}").items()})
    return a


def kernel(**inputs):
    import numpy as np
    import concourse.bacc as bacc
    from concourse.bass_utils import run_bass_kernel_spmd

    arrays = {n: np.ascontiguousarray(v) for n, v in lay_out({n: np.asarray(v) for n, v in inputs.items()}).items()}
    nc = bacc.Bacc("TRN2", target_bir_lowering=False, num_devices=1)
    a = {n: nc.dram_tensor("in_" + n, v.shape, mybir.dt.from_np(v.dtype), kind="ExternalInput").ap()
         for n, v in arrays.items()}
    out = nc.dram_tensor("out_tokens", (F_TURNS * FTOK, D), F32, kind="ExternalOutput").ap()
    program(nc, a, out)
    r = run_bass_kernel_spmd(nc, [{"in_" + n: v for n, v in arrays.items()}], core_ids=[0])
    return r.results[0]["out_tokens"][:N_TOK].reshape(B, S, D)
```

```python
from contextlib import ExitStack

import concourse.bass as bass
from concourse import mybir

ALU = mybir.AluOpType
ACT = mybir.ActivationFunctionType
F32 = mybir.dt.float32
BF16 = mybir.dt.bfloat16
U32 = mybir.dt.uint32
I32 = mybir.dt.int32
AX = mybir.AxisListType.X
ds = bass.ds

B = 8
D = 64
GRID = 30
VIS = GRID * GRID
TXT = 128
S = VIS + TXT
N_TOK = B * S
NT = -(-S // 128)
PAD_ROWS = (B - 1) * S + NT * 128 + 100
FT = 13
FTOK = FT * 128
F_TURNS = -(-N_TOK // FTOK)
PAD_ROWS = max(PAD_ROWS, F_TURNS * FTOK)
LN_EPS = 1e-5
RMS_EPS = 1e-6
WS2 = 49
NEG = -1e30
COMBOS = [(0, 0), (0, 1), (1, 0), (1, 1), (0, 2), (2, 0), (1, 2), (2, 1)]


class Signals:

    def __init__(self, nc, ctx, stage, names):
        self.nc = nc
        self.all = {n: ctx.enter_context(nc.semaphore(f"{stage}_{n}")) for n in names.split()}

    def __getitem__(self, name):
        return self.all[name]

    def end_turn(self):
        for s in self.all.values():
            self.nc.sync.sem_clear(s)
        self.nc.all_engine_barrier()


class Chain:

    def __init__(self, eng, sem):
        self.eng, self.sem, self.n = eng, sem, 0

    def __call__(self, ins):
        ins.then_inc(self.sem, 1)
        self.n += 1
        self.eng.wait_ge(self.sem, self.n)


def per_row(stat, shape):
    return stat.unsqueeze(len(shape) - 1).to_broadcast(shape)


def dve_center(nc, link, x, xc, sq, stat, shape):
    link(nc.vector.tensor_reduce(stat[:, 0], x, AX, ALU.add))
    link(nc.vector.tensor_scalar(stat[:, 0], stat[:, 0], -1.0 / D, None, ALU.mult))
    link(nc.vector.tensor_tensor(xc, x, per_row(stat[:, 0], shape), ALU.add))
    link(nc.vector.tensor_tensor(sq, xc, xc, ALU.mult))
    return nc.vector.tensor_reduce(stat[:, 1], sq, AX, ALU.add)


def dve_scale_rows(nc, link, out, xc, stat, shape):
    link(nc.vector.reciprocal(stat[:, 3], stat[:, 2]))
    return nc.vector.tensor_tensor(out, xc, per_row(stat[:, 3], shape), ALU.mult)


def act_std(nc, stat, eps, n=D):
    return nc.scalar.activation(stat[:, 2], stat[:, 1], ACT.Sqrt, bias=eps, scale=1.0 / n)



def load_constants(nc, ctx, c):
    k = {}

    def sb(name, shape, dt):
        k[name] = ctx.enter_context(nc.sbuf_tensor("k_" + name, shape, dt))
        return k[name]

    sg = Signals(nc, ctx, "k", "const_in const_set")
    ident = sb("ident", [128, 128], F32)
    identb = sb("identb", [128, 128], BF16)
    mask_st = sb("mask_st", [128, 128], BF16)
    mask_ts = sb("mask_ts", [128, 128], BF16)
    shift = sb("shift", [WS2, 132], F32)
    iota = sb("iota", [128, 16], F32)
    eps5 = sb("eps5", [128, 1], F32)
    eps6 = sb("eps6", [128, 1], F32)
    zero = sb("zero", [128, 1], F32)
    zrows = sb("zrows", [128, 128], F32)
    with nc.Block() as block:
        @block.sync
        def _(sp):
            for t, n in ((ident, "ident"), (identb, "identb"), (mask_st, "mask_st"), (mask_ts, "mask_ts"),
                         (shift, "shift"), (iota, "iota")):
                sp.dma_start(t[:], c[n]).then_inc(sg["const_in"], 16)
            sp.wait_ge(sg["const_in"], 6 * 16)
            sp.wait_ge(sg["const_set"], 4)
            for n, h in enumerate(c["pads"]):
                rows = PAD_ROWS - N_TOK
                half = rows // 2
                sp.dma_start(h[N_TOK:N_TOK + 2 * half, :].rearrange("(p a) d -> p (a d)", a=2),
                             zrows[0:half, :]).then_inc(sg["const_in"], 16)
                sp.wait_ge(sg["const_in"], (7 + n) * 16)

        @block.vector
        def _(dve):
            nc.vector.memset(eps5[:], LN_EPS).then_inc(sg["const_set"], 1)
            nc.vector.memset(eps6[:], RMS_EPS).then_inc(sg["const_set"], 1)
            nc.vector.memset(zero[:], 0.0).then_inc(sg["const_set"], 1)
            nc.vector.memset(zrows[:], 0.0).then_inc(sg["const_set"], 1)
    sg.end_turn()
    return k



def heads_acc(cfg):
    return min(cfg["heads_turn"], max(1, 32 // (cfg["hd"] + 1))) // (cfg["hq"] // cfg["hk"]) or 1


def v_cols(cfg):
    return 32 if cfg["hd"] < 32 else cfg["hd"] + 32


def attention_project(nc, k, cfg, h_in, w, parts_d, v_d, x_d):
    hd, hq, hk = cfg["hd"], cfg["hq"], cfg["hk"]
    QK = D + hk * hd
    W = QK + hk * hd
    KR = D + 1 if cfg["bias"] else D
    SH = [128, NT, D]
    with ExitStack() as ctx:
        def sb(name, shape, dt=F32):
            return ctx.enter_context(nc.sbuf_tensor(f"{cfg['name']}_p_{name}", shape, dt))

        once = Signals(nc, ctx, cfg["name"] + "_p", "w_in ones_set")
        sgs = [Signals(nc, ctx, f"{cfg['name']}_p{i}", "x_in dve_step act_step var_ready std_ready u_ready uT_done uT_copied "
                              "qkv_done v_copied qk_ready part_ready part_turned part_copied store_done") for i in range(2)]
        pair = lambda name, shape, dt=F32: [sb(f"{name}{i}", shape, dt) for i in range(2)]
        x_, xc_, sq_, u_ = (pair(n, SH) for n in ("x", "xc", "sq", "u"))
        stat_ = pair("stat", [128, 4, NT])
        uT_ = pair("uT", [128, NT * 128])
        wT = sb("wT", [128, W])
        qk_ = pair("qk", [128, NT, QK])
        qk2_ = pair("qk2", [128, NT, QK])
        part_ = pair("part", [128, 3, NT, QK], BF16)
        partT_ = pair("partT", [QK, 3, NT * 128], BF16)
        va_ = pair("va", [128, NT, hk * hd])
        pstat_ = pair("pstat", [128, 4, NT * 64]) if cfg["kind"] == "rmspair" else [None, None]
        nw = sb("nw", [128, QK]) if cfg["kind"] == "rmspair" else None
        ln1 = sb("ln1", [128, D]) if cfg["kind"] == "rope" else None
        rope = sb("rope", [128, 2, NT, 16]) if cfg["kind"] == "rope" else None
        psT = ctx.enter_context(nc.psum_tensor(f"{cfg['name']}_p_psT", [128, 3 * 512], F32))
        psQ = ctx.enter_context(nc.psum_tensor(f"{cfg['name']}_p_psQ", [128, 5 * 512], F32))
        qkv = psQ[:, :].rearrange("p (n w) -> p n w", w=256)[:, 0:NT, :]
        turned = [psT[:, :].bitcast(BF16)[0:QK, 0:NT * 128], psQ[:, 0:1024].bitcast(BF16)[0:QK, 0:NT * 128],
                  psQ[:, 1024:2048].bitcast(BF16)[0:QK, 0:NT * 128]]
        n_w = 0
        with nc.Block() as block:
            @block.sync
            def _(sp):
                n = 0
                sp.wait_ge(once["ones_set"], 3)
                loads = [(wT[0:KR, :], w["wT"])]
                if nw is not None:
                    loads += [(nw[:, 0:D].rearrange("p (h d) -> p h d", d=2),
                               w["qn"].partition_broadcast(128).unsqueeze(1).to_broadcast([128, 32, 2])),
                              (nw[:, D:QK].rearrange("p (h d) -> p h d", d=2),
                               w["kn"].partition_broadcast(128).unsqueeze(1).to_broadcast([128, 32, 2]))]
                if ln1 is not None:
                    loads += [(ln1[:], w["ln1"].partition_broadcast(128)), (rope[:], w["rope"])]
                for dst, src in loads:
                    sp.dma_start(dst, src).then_inc(once["w_in"], 16)
                    n += 16
                    sp.wait_ge(once["w_in"], n)

            @block.vector
            def _(dve):
                for uT in uT_:
                    nc.vector.memset(uT[:], 0.0).then_inc(once["ones_set"], 1)
                nc.vector.memset(wT[:], 0.0).then_inc(once["ones_set"], 1)
                dve.wait_ge(once["ones_set"], 3)
                for uT in uT_:
                    nc.vector.memset(uT[D:D + 1, :], 1.0).then_inc(once["ones_set"], 1)
                dve.wait_ge(once["ones_set"], 5)
        once.end_turn()
        with nc.Fori(0, B // 2) as b2:
            with nc.Block() as block:
                @block.sync
                def _(sp):
                    for i, sg in enumerate(sgs):
                        b = 2 * b2 + i
                        x = x_[i]
                        sp.dma_start(x[:], h_in[ds(b * S, NT * 128), :].rearrange("(n p) d -> p n d", p=128)) \
                            .then_inc(sg["x_in"], 16)
                    for i, sg in enumerate(sgs):
                        b = 2 * b2 + i
                        u, va, partT = u_[i], va_[i], partT_[i]
                        sp.wait_ge(sg["v_copied"], 1)
                        sp.dma_start(v_d[ds(b, 1)].rearrange("o p n v -> p (o n) v"), va[:]).then_inc(sg["store_done"], 16)
                        n = 16
                        if x_d is not None:
                            sp.wait_ge(sg["u_ready"], 1)
                            sp.dma_start(x_d[ds(b * NT * 128, NT * 128), :].rearrange("(n p) d -> p n d", p=128), u[:]) \
                                .then_inc(sg["store_done"], 16)
                            n += 16
                        for r in range(3):
                            sp.wait_ge(sg["part_copied"], r + 1)
                            sp.dma_start(parts_d[ds(b * 3 + r, 1)].rearrange("o r t -> (o r) t"), partT[:, r, 0:S]) \
                                .then_inc(sg["store_done"], 16)
                            n += 16

                    for sg in sgs:
                        sp.wait_ge(sg["store_done"], n)

                @block.vector
                def _(dve):
                    links = [Chain(dve, sg["dve_step"]) for sg in sgs]
                    for i, sg in enumerate(sgs):
                        link = links[i]
                        x, xc, sq, u, stat = x_[i], xc_[i], sq_[i], u_[i], stat_[i]
                        dve.wait_ge(sg["x_in"], 16)
                        dve_center(nc, link, x[:], xc[:], sq[:], stat, SH).then_inc(sg["var_ready"], 1)
                        dve.wait_ge(sg["std_ready"], 1)
                        ins = dve_scale_rows(nc, link, u[:], xc[:], stat, SH)
                        feed = u
                        if ln1 is not None:
                            ins.then_inc(sg["u_ready"], 1)
                            dve.wait_ge(sg["u_ready"], 1)
                            link(nc.vector.tensor_tensor(sq[:], u[:], u[:], ALU.mult))
                            nc.vector.tensor_reduce(stat[:, 1], sq[:], AX, ALU.add).then_inc(sg["var_ready"], 1)
                            dve.wait_ge(sg["std_ready"], 2)
                            link(dve_scale_rows(nc, link, xc[:], u[:], stat, SH))
                            ins = nc.vector.tensor_tensor(x[:], xc[:], ln1[:].unsqueeze(1).to_broadcast(SH), ALU.mult)
                            feed = x
                        ins.then_inc(sg["u_ready"], 1)
                    for i, sg in enumerate(sgs):
                        link = links[i]
                        va, qk, qk2, pstat, part, partT = va_[i], qk_[i], qk2_[i], pstat_[i], part_[i], partT_[i]
                        dve.wait_ge(sg["qkv_done"], 1)
                        nc.vector.tensor_copy(va[:], qkv[:, :, QK:W]).then_inc(sg["v_copied"], 1)
                        dve.wait_ge(sg["qk_ready"], 1)
                        src, oth = qk, qk2
                        if cfg["kind"] == "rmspair":
                            pairs = [128, NT * 64, 2]
                            v3 = lambda t: t[:].rearrange("p n (h d) -> p (n h) d", d=2)
                            link(nc.vector.tensor_tensor(oth[:], src[:], src[:], ALU.mult))
                            nc.vector.tensor_reduce(pstat[:, 1], v3(oth), AX, ALU.add).then_inc(sg["var_ready"], 1)
                            dve.wait_ge(sg["std_ready"], 2)
                            link(dve_scale_rows(nc, link, v3(oth), v3(src), pstat, pairs))
                            link(nc.vector.tensor_tensor(src[:], oth[:], nw[:].unsqueeze(1).to_broadcast([128, NT, QK]),
                                                         ALU.mult))
                        if cfg["kind"] == "rope":
                            H = QK // 16
                            for hh in range(H):
                                q_, o_ = src[:, :, 16 * hh:16 * hh + 16], oth[:, :, 16 * hh:16 * hh + 16]
                                nc.vector.tensor_tensor(o_[:, :, 0:8], q_[:, :, 8:16], rope[:, 1, :, 0:8], ALU.mult)
                                ins = nc.vector.tensor_tensor(o_[:, :, 8:16], q_[:, :, 0:8], rope[:, 1, :, 8:16], ALU.mult)
                            link(ins)
                            for hh in range(H):
                                q_ = src[:, :, 16 * hh:16 * hh + 16]
                                ins = nc.vector.tensor_tensor(q_, q_, rope[:, 0], ALU.mult)
                            link(ins)
                            link(nc.vector.tensor_tensor(src[:], src[:], oth[:], ALU.add))
                        link(nc.vector.tensor_scalar(src[:, :, 0:D], src[:, :, 0:D], float(hd) ** -0.5, None, ALU.mult))
                        nc.vector.tensor_copy(part[:, 0], src[:]).then_inc(sg["part_ready"], 1)
                        dve.wait_ge(sg["part_ready"], 1)
                        link(nc.vector.tensor_tensor(oth[:], src[:], part[:, 0], ALU.subtract))
                        nc.vector.tensor_copy(part[:, 1], oth[:]).then_inc(sg["part_ready"], 1)
                        dve.wait_ge(sg["part_ready"], 2)
                        link(nc.vector.tensor_tensor(src[:], oth[:], part[:, 1], ALU.subtract))
                        nc.vector.tensor_copy(part[:, 2], src[:]).then_inc(sg["part_ready"], 1)
                        for r in range(3):
                            dve.wait_ge(sg["part_turned"], r + 1)
                            nc.vector.tensor_copy(partT[:, r], turned[r]).then_inc(sg["part_copied"], 1)

                @block.scalar
                def _(act):
                    for i, sg in enumerate(sgs):
                        stat = stat_[i]
                        act.wait_ge(sg["var_ready"], 1)
                        act_std(nc, stat, k["eps5"][:]).then_inc(sg["std_ready"], 1)
                        if ln1 is not None:
                            act.wait_ge(sg["var_ready"], 2)
                            act_std(nc, stat, k["eps6"][:]).then_inc(sg["std_ready"], 1)
                    for i, sg in enumerate(sgs):
                        uT, qk, pstat = uT_[i], qk_[i], pstat_[i]
                        act.wait_ge(sg["uT_done"], 1)
                        nc.scalar.copy(uT[0:D, :], psT[0:D, 0:NT * 128]).then_inc(sg["uT_copied"], 1)
                        act.wait_ge(sg["v_copied"], 1)
                        nc.scalar.copy(qk[:], qkv[:, :, 0:QK]).then_inc(sg["qk_ready"], 1)
                        if cfg["kind"] == "rmspair":
                            act.wait_ge(sg["var_ready"], 2)
                            act_std(nc, pstat, k["eps6"][:], 2).then_inc(sg["std_ready"], 1)

                @block.tensor
                def _(pe):
                    for i, sg in enumerate(sgs):
                        x, u, uT, part = x_[i], u_[i], uT_[i], part_[i]
                        if i == 1:
                            pe.wait_ge(sgs[0]["part_copied"], 3)
                        feed = x if ln1 is not None else u
                        pe.wait_ge(sg["u_ready"], 2 if ln1 is not None else 1)
                        for n in range(NT):
                            ins = nc.tensor.transpose(psT[0:D, n * 128:n * 128 + 128], feed[:, n, :], k["ident"][:])
                        ins.then_inc(sg["uT_done"], 1)
                        pe.wait_ge(sg["uT_copied"], 1)
                        for n in range(NT):
                            ins = nc.tensor.matmul(qkv[:, n, 0:W], uT[:, n * 128:n * 128 + 128], wT[:, :],
                                                   start=True, stop=True)
                        ins.then_inc(sg["qkv_done"], 1)
                        pe.wait_ge(sg["v_copied"], 1)
                        pe.wait_ge(sg["qk_ready"], 1)
                        for r in range(3):
                            pe.wait_ge(sg["part_ready"], r + 1)
                            for n in range(NT):
                                ins = nc.tensor.transpose(turned[r][:, n * 128:n * 128 + 128], part[:, r, n, :],
                                                          k["identb"][:])
                            ins.then_inc(sg["part_turned"], 1)
            for sg in sgs:
                sg.end_turn()


def gather_bias(nc, ctx, sg, table, index, tiles):
    idx = [ctx.enter_context(nc.sbuf_tensor(f"bias_idx{i}", [WS2, WS2], I32)) for i in range(2)]
    gathered = nc.alloc_semaphore("bias_gathered")
    with nc.Block() as block:
        @block.sync
        def _(sp):
            sp.dma_start(idx[0][:], index[0]).then_inc(sg["loaded"], 16)
            sp.dma_start(idx[1][:], index[1]).then_inc(sg["loaded"], 16)

        @block.gpsimd
        def _(pool):
            pool.wait_ge(sg["loaded"], 32)
            n = 0
            for i in range(2):
                for c in range(WS2):
                    pool.indirect_dma_start(
                        out=tiles[i][:, c, :], out_offset=None, in_=table,
                        in_offset=bass.IndirectOffsetOnAxis(ap=idx[i][:, c:c + 1].bitcast(U32), axis=0)) \
                        .then_inc(gathered, 16)
                    n += 16
            pool.wait_ge(gathered, n)
    sg.end_turn()


def attention_core_bounded(nc, k, cfg, parts_d, v_d, o_d, w):
    hd, hk = cfg["hd"], cfg["hk"]
    IM = cfg["images_turn"]
    HG = IM * hk
    HS = cfg["stack"]
    R = hd * HS
    assert R * len(COMBOS) == 128
    RING = 2 * HS
    hpa, VR = heads_acc(cfg), v_cols(cfg)
    RW = hpa * (hd + 1)
    accs = [list(range(i + a, i + min(a + hpa, hk))) for i in range(0, HG, hk) for a in range(0, hk, hpa)]
    acc_of = {h: a for a, hs in enumerate(accs) for h in hs}
    last = S - 128 * (NT - 1)
    OC = 256 + last
    piece = lambda i: (128 * i, min(128 * i + 128, S), 32 * (i % 4), 128 * (i // 4))
    groups = [[(0, 0)]] + [[(j, 0), (NT - 1 - j, S - 128 * j)] for j in range(1, NT // 2)] + [[(NT // 2, 0)]]
    groups[1].append((NT - 1, 2 * S - 128 * (NT - 1)))
    NG = len(groups)
    width = lambda j: S - 128 * j
    PW = max(base + width(j) for g in groups for j, base in g)
    steps = [(h, g) for h in range(HG) for g in range(NG)]
    LAG = 2
    with ExitStack() as ctx:
        def sb(name, shape, dt=F32):
            return ctx.enter_context(nc.sbuf_tensor(f"{cfg['name']}_c_{name}", shape, dt))

        sg = Signals(nc, ctx, cfg["name"] + "_c", "own_in rows_set ones_set bound_in dve_step loaded0 loaded1 v_in0 v_in1 own_ready "
                              "v_ready scores_ready exp_done pv_done o_taken store_done")
        QA = sb("QA", [128, HG // HS, NT * 128], BF16)
        KA = sb("KA", [128, HG // HS, NT * 128], BF16)
        KM = sb("KM", [128, RING, NT * 128], BF16)
        own = sb("own", [128, HS])
        VX = sb("VX", [128, IM, NT, hk * hd])
        V = sb("V", [128, NT, HG, VR])
        P = sb("P", [128, LAG + 1, PW])
        O = sb("O", [128, len(accs), OC])
        wq = sb("wq", [128, hd])
        wk = sb("wk", [128, hd])
        bound = sb("bound", [128, 1])
        SC = ctx.enter_context(nc.psum_tensor(f"{cfg['name']}_c_SC", [128, 2, 3 * 512], F32))
        OP = ctx.enter_context(nc.psum_tensor(f"{cfg['name']}_c_OP", [128, 2, 512], F32))
        with nc.Block() as block:
            @block.sync
            def _(sp):
                sp.dma_start(own[:], w["own"]).then_inc(sg["own_in"], 16)
                sp.dma_start(wq[:], w["qn"].partition_broadcast(128)).then_inc(sg["bound_in"], 16)
                sp.dma_start(wk[:], w["kn"].partition_broadcast(128)).then_inc(sg["bound_in"], 16)
                sp.wait_ge(sg["own_in"], 16)

            @block.vector
            def _(dve):
                nc.vector.memset(QA[:], 0.0).then_inc(sg["rows_set"], 1)
                nc.vector.memset(KA[:], 0.0).then_inc(sg["rows_set"], 1)
                dve.wait_ge(sg["rows_set"], 2)
                nc.vector.memset(V[:], 0.0).then_inc(sg["ones_set"], 1)
                dve.wait_ge(sg["ones_set"], 1)
                for im in range(IM):
                    for i in range(hpa):
                        nc.vector.memset(V[:, :, im * hk + i:im * hk + hk:hpa, hpa * hd + i:hpa * hd + i + 1], 1.0) \
                            .then_inc(sg["ones_set"], 1)
                dve.wait_ge(sg["ones_set"], 1 + IM * hpa)
                link = Chain(dve, sg["dve_step"])
                dve.wait_ge(sg["bound_in"], 32)
                link(nc.vector.tensor_tensor(wq[:], wq[:], wk[:], ALU.mult))
                link(nc.vector.tensor_reduce(bound[:], wq[:], AX, ALU.max, apply_absolute_value=True))
                link(nc.vector.tensor_scalar(bound[:], bound[:], -(float(hd) ** 0.5), None, ALU.mult))
        sg.end_turn()

        with nc.Fori(0, B // IM) as b:
            with nc.Block() as block:
                @block.sync
                def _(sp):
                    for im in range(IM):
                        hs = slice(im * hk // HS, (im + 1) * hk // HS)
                        for c, (pq, pk) in enumerate(COMBOS):
                            q = parts_d[ds(b * (3 * IM) + 3 * im + pq, 1), 0:D, :]
                            kk = parts_d[ds(b * (3 * IM) + 3 * im + pk, 1), D:D + hk * hd, :]
                            sp.dma_start(QA[R * c:R * c + R, hs, 0:S], q.rearrange("o (h d) t -> d (o h) t", d=R)) \
                                .then_inc(sg[f"loaded{im}"], 16)
                            sp.dma_start(KA[R * c:R * c + R, hs, 0:S], kk.rearrange("o (h d) t -> d (o h) t", d=R)) \
                                .then_inc(sg[f"loaded{im}"], 16)
                        sp.dma_start(VX[:, im], v_d[ds(b * IM + im, 1)].rearrange("o p n v -> p (o n) v")) \
                            .then_inc(sg[f"v_in{im}"], 16)
                    for a in range(len(accs)):
                        sp.wait_ge(sg["o_taken"], a + 1)
                        dst = o_d[ds(b * len(accs) + a, 1)].rearrange("o r t -> (o r) t")
                        sp.dma_start(dst[0:RW, 1024:S], O[0:RW, a, 256:OC]).then_inc(sg["store_done"], 16)
                        tiles = dst[:, 0:1024].rearrange("r (m q c) -> r q m c", q=4, c=128)
                        for q in range(4):
                            sp.dma_start(tiles[0:RW, q], O[32 * q:32 * q + RW, a, 0:256]
                                         .rearrange("r (m c) -> r m c", c=128)).then_inc(sg["store_done"], 16)
                    sp.wait_ge(sg["store_done"], 16 * 5 * len(accs))

                @block.tensor
                def _(pe):
                    def scores(z):
                        h, g = steps[z]
                        if z >= 2:
                            pe.wait_ge(sg["exp_done"], z - 1)
                        if g == 0:
                            pe.wait_ge(sg["own_ready"], h + 1)
                        for j, base in groups[g]:
                            n, cols = min(128, width(j)), width(j)
                            keys = KM[:, h % RING, 128 * j:128 * j + 128]
                            edges = [0] + [e - base for e in range(512, 1536, 512) if base < e < base + cols] + [cols]
                            for c0, c1 in zip(edges, edges[1:]):
                                ins = nc.tensor.matmul(SC[:, z % 2, base + c0:base + c1], keys,
                                                       QA[:, h // HS, 128 * j + c0:128 * j + c1], start=True,
                                                       stop=(c0 >= n), skip_group_check=True)
                                m1 = min(n, c1)
                                if c0 < n:
                                    ins = nc.tensor.matmul(SC[:, z % 2, base + c0:base + m1], k["identb"][:],
                                                           k["mask_st"][:, c0:m1], start=False, stop=True,
                                                           skip_group_check=True)
                        ins.then_inc(sg["scores_ready"], 1)

                    def weigh(z):
                        h, g = steps[z]
                        pe.wait_ge(sg["exp_done"], z + 1)
                        if g == 0 and h % hk == 0:
                            pe.wait_ge(sg["v_ready"], h // hk + 1)
                        a = acc_of[h]
                        first = g == 0 and h == accs[a][0]
                        if first and a >= 2:
                            pe.wait_ge(sg["o_taken"], a - 1)
                        for j, base in groups[g]:
                            for i in range(j, NT):
                                t0, t1, p0, col = piece(i)
                                ins = nc.tensor.matmul(
                                    OP[p0:p0 + VR, a % 2, col:col + t1 - t0], V[0:min(128, width(j)), j, h, :],
                                    P[0:min(128, width(j)), z % (LAG + 1), base + t0 - 128 * j:base + t1 - 128 * j],
                                    start=(first and i < 4), stop=(h == accs[a][-1] and g == NG - 1),
                                    skip_group_check=True)
                        ins.then_inc(sg["pv_done"], 1)

                    for z in range(len(steps)):
                        scores(z)
                        if z >= LAG:
                            weigh(z - LAG)
                    for z in range(len(steps) - LAG, len(steps)):
                        weigh(z)

                @block.scalar
                def _(act):
                    for z, (h, g) in enumerate(steps):
                        j, base = groups[g][-1]
                        n = base + width(j)
                        act.wait_ge(sg["scores_ready"], z + 1)
                        if z >= LAG + 1:
                            act.wait_ge(sg["pv_done"], z - LAG)
                        nc.scalar.activation(P[:, z % (LAG + 1), 0:n], SC[:, z % 2, 0:n], ACT.Exp, bias=bound[:]) \
                            .then_inc(sg["exp_done"], 1)

                @block.vector
                def _(dve):
                    def spread_v(im):
                        dve.wait_ge(sg[f"v_in{im}"], 16)
                        vs = VX[:, im].rearrange("p n (h d) -> p n h d", d=hd)
                        vd = V[:, :, im * hk:im * hk + hk, :]
                        for i in range(hpa):
                            ins = nc.vector.tensor_copy(vd[:, :, i:hk:hpa, i * hd:i * hd + hd], vs[:, :, i:hk:hpa, :])
                        ins.then_inc(sg["v_ready"], 1)

                    def take_outputs(a):
                        dve.wait_ge(sg["pv_done"], (accs[a][-1] + 1) * NG)
                        nc.vector.tensor_copy(O[:, a, 0:256], OP[:, a % 2, 0:256])
                        nc.vector.tensor_copy(O[0:32, a, 256:OC], OP[0:32, a % 2, 256:OC]).then_inc(sg["o_taken"], 1)

                    taken = 0
                    for h in range(HG):
                        if h % hk == 0:
                            dve.wait_ge(sg[f"loaded{h // hk}"], 16 * 2 * len(COMBOS))
                        if h >= RING:
                            dve.wait_ge(sg["exp_done"], (h - RING + 1) * NG)
                        nc.vector.tensor_scalar(KM[:, h % RING, :], KA[:, h // HS, :], own[:, h % HS:h % HS + 1], None,
                                                ALU.mult).then_inc(sg["own_ready"], 1)
                        if h % hk == 1:
                            spread_v(h // hk)
                        if h == accs[taken][-1] + RING - 2:
                            take_outputs(taken)
                            taken += 1
                    for a in range(taken, len(accs)):
                        take_outputs(a)
            sg.end_turn()


def attention_core_max(nc, k, cfg, parts_d, v_d, nm_d, o_d, w):
    hd, hk, rep = cfg["hd"], cfg["hk"], cfg["hq"] // cfg["hk"]
    IM = cfg["images_turn"]
    HG, HK = IM * cfg["hq"], IM * hk
    causal, window = cfg["causal"], cfg["window"]
    HS = cfg["stack"]
    combos = COMBOS[0:6]
    per = min(len(combos), 128 // (hd * HS))
    NCH = len(combos) // per
    R0 = per * hd * HS
    RX = 3 * HS if NCH == 1 else 0
    UNITS = HG // HS
    hpa, VR = heads_acc(cfg), v_cols(cfg)
    RW = hpa * (hd + 1)
    accs = [list(range(i + a, i + min(a + hpa, cfg["hq"]))) for i in range(0, HG, cfg["hq"])
            for a in range(0, cfg["hq"], hpa)]
    acc_of = {h: a for a, hs in enumerate(accs) for h in hs}
    MAIN = 128 * (NT - 1)
    TAIL = S - MAIN
    if hd > 32:
        pieces = [(0, 512, 0, hd, 0, 0, 0), (512, MAIN, 0, hd, 64, 0, 0),
                  (0, 512, hd, VR, 64, 1, 0), (512, MAIN, hd, VR, 96, 1, 0)]
        tails = [(0, hd, 0, 1, 0), (hd, VR, 0, 1, 8)]
        evac = [(0, 128, 0, 0, 512), (64, 64, 1, 0, 512), (0, 64, 1, 0, TAIL), (0, 32, 1, 8, TAIL)]
        stores = [(0, hd, 0, 0, 0, 0, 512), (64, hd, 0, 0, 0, 512, 512), (0, hd, 1, 0, 0, MAIN, TAIL),
                  (64, 1, 1, 0, hd, 0, 512), (96, 1, 1, 0, hd, 512, 512), (0, 1, 1, 8, hd, MAIN, TAIL)]
    else:
        if causal:
            pieces = [(128 * i, 128 * i + 128, 0, VR, 32 * (i % 4), 0, 128 * (i // 4)) for i in range(NT - 1)]
            stores = []
        else:
            pieces = [(256 * i, 256 * i + 256, 0, VR, 32 * i, 0, 0) for i in range(4)]
            stores = [(32 * i, RW, 0, 0, 0, 256 * i, 256) for i in range(4)]
        tails = [(0, VR, 0, 0, 256)]
        evac = [(0, 128, 0, 0, 256), (0, 32, 0, 256, TAIL)]
        stores.append((0, RW, 0, 256, 0, MAIN, TAIL))
    n_stores = len(stores) + (4 if causal else 0)
    OB = 2 if hd > 32 else 1
    rows = lambda i: min(128, S - 128 * i)
    width = lambda j: max(0, MAIN - 128 * j) if causal else MAIN
    if causal:
        groups = [[(0, 0)]] + [[(j, 0), (NT - 1 - j, MAIN - 128 * j)] for j in range(1, NT // 2)] + [[(NT // 2, 0)]]
    else:
        groups = [[(j, 0)] for j in range(NT)]
    NG = len(groups)
    steps = [(h, g) for h in range(HG) for g in range(NG + 1)]
    mains = [z for z, (h, g) in enumerate(steps) if g < NG]
    LAG = 2
    limit = lambda i: min(MAIN, 128 * i + 128) if causal else MAIN
    chunks = [(i, c) for i in range(NT) for c in range(-(-limit(i) // 512))]
    maxima = [(h, n) for h in range(HG) for n in range(len(chunks) + 1)]
    per_unit = HS * (len(chunks) + 1)
    LEAD = 12 if UNITS > 1 else 0
    TURN = min(LEAD, 3)
    ratio = -(-(len(chunks) + 1) // (NG + 1))
    tiles_t = [NT - 1] if causal else list(range(NT))
    with ExitStack() as ctx:
        def sb(name, shape, dt=F32):
            return ctx.enter_context(nc.sbuf_tensor(f"{cfg['name']}_c_{name}", shape, dt))

        sg = Signals(nc, ctx, cfg["name"] + "_c", "loaded loaded0 loaded1 loaded2 loaded3 v_in0 v_in1 v_in2 v_in3 rows_set ones_set v_ready own_ready dve_step chunk_ready max_taken "
                              "tail_ready tail_read nm_ready nmT_done nmT_copied nm_stored negmax_in scores_ready exp_done "
                              "pv_done o_taken store_done")
        QA = sb("QA", [128, NCH, UNITS, NT * 128], BF16)
        KA = sb("KA", [128, NCH, HK // HS, NT * 128], BF16)
        if HS > 1:
            KM = sb("KM", [128, HG, NT * 128], BF16)
            own = sb("own", [128, HS])
            km = lambda c, h: KM[:, h, :]
        else:
            km = lambda c, h: KA[:, c, h // rep, :]
        if NCH > 1:
            QX = sb("QX", [128, UNITS, NT * 128], BF16)
            KX = sb("KX", [128, NT * 128], BF16)
        VX = sb("VX", [128, IM, NT, hk * hd])
        V = sb("V", [128, NT, HK, VR])
        P = sb("P", [128, LAG + 1, MAIN])
        O = sb("O", [128, len(accs) * OB, 512])
        NM = sb("NM", [128, HG, NT, 3])
        nmx = sb("nmx", [128, HS, NT])
        nmp = sb("nmp", [128, HS, 3, NT], BF16)
        nmT = sb("nmT", [HS * 3 * NT, 2, 128], BF16)
        SC = ctx.enter_context(nc.psum_tensor(f"{cfg['name']}_c_SC", [128, 2, MAIN], F32))
        CP = ctx.enter_context(nc.psum_tensor(f"{cfg['name']}_c_CP", [128, 2, 512], F32)) if UNITS > 1 else \
            SC[:, :, 0:512]
        TP = ctx.enter_context(nc.psum_tensor(f"{cfg['name']}_c_TP", [128, 512], F32))
        OP = ctx.enter_context(nc.psum_tensor(f"{cfg['name']}_c_OP", [128, OB, 512], F32))
        nmP = TP[0:HS * 3 * NT, 64:128].bitcast(BF16)
        blank = [QA, KA] + ([QX, KX] if NCH > 1 else [])

        if window:
            biases = [sb("biasT", [WS2, WS2, 8]), sb("biasA", [WS2, WS2, 8])]
            gather_bias(nc, ctx, sg, w["table"], w["index"], biases)
        with nc.Block() as block:
            @block.sync
            def _(sp):
                n = 0
                sp.wait_ge(sg["rows_set"], len(blank))
                if HS > 1:
                    sp.dma_start(own[:], w["own"]).then_inc(sg["loaded"], 16)
                    n += 16
                dst = KA[R0:R0 + RX, 0, :, 0:S] if NCH == 1 else KX[0:3, 0:S].unsqueeze(1)
                copies = HK // HS if NCH == 1 else 1
                sp.dma_start(dst, w["ones"][0:max(RX, 3), 0:copies * S].rearrange("r (h t) -> r h t", t=S)) \
                    .then_inc(sg["loaded"], 16)
                sp.wait_ge(sg["loaded"], n + 16)

            @block.vector
            def _(dve):
                for t in blank:
                    nc.vector.memset(t[:], 0.0).then_inc(sg["rows_set"], 1)
                nc.vector.memset(V[:], 0.0).then_inc(sg["ones_set"], 1)
                nc.vector.memset(NM[:], NEG).then_inc(sg["ones_set"], 1)
                dve.wait_ge(sg["ones_set"], 2)
                for im in range(IM):
                    for i in range(hpa):
                        nc.vector.memset(V[:, :, im * hk + i:im * hk + hk:hpa, hpa * hd + i:hpa * hd + i + 1], 1.0) \
                            .then_inc(sg["ones_set"], 1)
                dve.wait_ge(sg["ones_set"], 2 + IM * hpa)
        sg.end_turn()

        with nc.Fori(0, B // IM) as b:
            with nc.Block() as block:
                @block.sync
                def _(sp):
                    for im in range(IM):
                        us, ks = im * (UNITS // IM), im * (hk // HS)
                        for c, (pq, pk) in enumerate(combos):
                            ch, r0 = c // per, (c % per) * hd * HS
                            q = parts_d[ds(b * (3 * IM) + 3 * im + pq, 1), 0:D, :]
                            kk = parts_d[ds(b * (3 * IM) + 3 * im + pk, 1), D:D + hk * hd, :]
                            sp.dma_start(QA[r0:r0 + hd * HS, ch, us:us + UNITS // IM, 0:S],
                                         q.rearrange("o (h d) t -> d (o h) t", d=hd * HS)).then_inc(sg[f"loaded{im}"], 16)
                            sp.dma_start(KA[r0:r0 + hd * HS, ch, ks:ks + hk // HS, 0:S],
                                         kk.rearrange("o (h d) t -> d (o h) t", d=hd * HS)).then_inc(sg[f"loaded{im}"], 16)
                        sp.dma_start(VX[:, im], v_d[ds(b * IM + im, 1)].rearrange("o p n v -> p (o n) v")) \
                            .then_inc(sg[f"v_in{im}"], 16)
                    for u in range(UNITS):
                        sp.wait_ge(sg["nmT_copied"], u + 1)
                        sp.dma_start(nm_d[u], nmT[:, u % 2, :]).then_inc(sg["nm_stored"], 16)
                        sp.wait_ge(sg["nm_stored"], 16 * (u + 1))
                        for e in range(HS):
                            dst = QA[R0 + 3 * e:R0 + 3 * e + 3, 0, u, 0:S] if NCH == 1 else QX[0:3, u, 0:S]
                            src = nm_d[u, 3 * NT * e:3 * NT * e + 3 * NT, :].rearrange("(r i) p -> r (i p)", i=NT)
                            sp.dma_start(dst, src[:, 0:S]).then_inc(sg["negmax_in"], 16)
                        sp.wait_ge(sg["negmax_in"], 16 * HS * (u + 1))
                    sp.wait_ge(sg["store_done"], 16 * n_stores * len(accs))

                def products(out, base, c0, c1, lhs, rhs, adds):
                    edges = [c0] + [c0 + e - base for e in range(512, MAIN, 512) if base < e < base + c1 - c0] + [c1]
                    for e0, e1 in zip(edges, edges[1:]):
                        ops = [(e0, e1, 128, l, r[:, e0:e1]) for l, r in zip(lhs, rhs)]
                        ops += [(max(a0, e0), min(a1, e1), l.shape[1], l, r[:, max(a0, e0) - a0:min(a1, e1) - a0])
                                for a0, a1, l, r in adds if max(a0, e0) < min(a1, e1)]
                        for z, (x0, x1, m, l, r) in enumerate(ops):
                            m = min(m, l.shape[1])
                            ins = nc.tensor.matmul(out[0:m, base + x0 - c0:base + x1 - c0], l, r, start=(z == 0),
                                                   stop=(z == len(ops) - 1), skip_group_check=True)
                    return ins

                @block.tensor
                def _(pe):
                    reader = None

                    def chunk_logits(n):
                        nonlocal reader
                        h, c = maxima[n]
                        u = h // HS
                        if c == 0 and h % cfg["hq"] == 0:
                            pe.wait_ge(sg[f"loaded{h // cfg['hq']}"], 16 * 2 * len(combos))
                        if HS > 1 and c == 0:
                            pe.wait_ge(sg["own_ready"], h + 1)
                        q = lambda i, m: [QA[0:R0 if RX else 128, x, u, 128 * i:128 * i + m] for x in range(NCH)]
                        kk = [km(x, h)[0:R0 if RX else 128, :] for x in range(NCH)]
                        if c < len(chunks):
                            i, cc = chunks[c]
                            z = h * len(chunks) + c
                            if z >= 2:
                                pe.wait_ge(sg["max_taken"], z - 1)
                            m = rows(i)
                            adds = []
                            if causal and i < NT - 1:
                                adds.append((128 * i, 128 * i + 128, k["identb"][:], k["mask_ts"][:]))
                            if window and i >= NT - 2:
                                e0 = 128 * (i - NT + 2)
                                adds.append((S - WS2, S, k["shift"][:, e0:e0 + m], biases[1][:, :, h % cfg["hq"]]))
                            products(CP[:, z % 2, :], 0, 512 * cc, min(512 * cc + 512, limit(i)), q(i, m), kk, adds) \
                                .then_inc(sg["chunk_ready"], 1)
                            return
                        if reader:
                            pe.wait_ge(sg[reader[0]], reader[1])
                        reader = ("tail_read", h + 1)
                        for i in tiles_t:
                            adds = []
                            if causal:
                                adds.append((MAIN, S, k["identb"][:], k["mask_ts"][:, 0:TAIL]))
                            if window and i >= NT - 2:
                                e0 = 128 * (i - NT + 2)
                                adds.append((S - WS2, S, k["shift"][:, e0:e0 + rows(i)], biases[1][:, :, h % cfg["hq"]]))
                            ins = products(TP, TAIL * i, MAIN, S, q(i, 128), kk, adds)
                        ins.then_inc(sg["tail_ready"], 1)

                    def turn_maxima(u):
                        nonlocal reader
                        pe.wait_ge(sg["nm_ready"], u + 1)
                        pe.wait_ge(sg[reader[0]], reader[1])
                        reader = ("nmT_copied", u + 1)
                        nc.tensor.transpose(nmP, nmp[:].rearrange("p e r i -> p (e r i)"), k["identb"][:]) \
                            .then_inc(sg["nmT_done"], 1)

                    def scores(z):
                        nonlocal reader
                        h, g = steps[z]
                        if g == 0 and h % HS == 0:
                            pe.wait_ge(sg["negmax_in"], 16 * HS * (h // HS + 1))
                        lhs = lambda j, m: [km(x, h)[:, 128 * j:128 * j + m] for x in range(NCH)] + \
                            ([KX[:, 128 * j:128 * j + m]] if NCH > 1 else [])
                        rhs = [QA[:, x, h // HS, :] for x in range(NCH)] + ([QX[:, h, :]] if NCH > 1 else [])
                        if g < NG:
                            y = mains.index(z)
                            if y >= 2:
                                pe.wait_ge(sg["exp_done"], mains[y - 2] + 1)
                            for j, base in groups[g]:
                                adds = []
                                if causal:
                                    adds.append((128 * j, 128 * j + 128, k["identb"][:], k["mask_st"][:]))
                                if window and j >= NT - 2:
                                    e0 = 128 * (j - NT + 2)
                                    adds.append((S - WS2, S, k["shift"][:, e0:e0 + rows(j)], biases[0][:, :, h % cfg["hq"]]))
                                ins = products(SC[:, y % 2, :], base, 128 * j if causal else 0, MAIN, lhs(j, rows(j)),
                                               rhs, adds)
                        else:
                            pe.wait_ge(sg[reader[0]], reader[1])
                            reader = ("exp_done", z + 1)
                            for j in range(NT):
                                adds = []
                                if causal and j == NT - 1:
                                    adds.append((MAIN, S, k["identb"][:], k["mask_st"][:, 0:TAIL]))
                                if window and j >= NT - 2:
                                    e0 = 128 * (j - NT + 2)
                                    adds.append((S - WS2, S, k["shift"][:, e0:e0 + rows(j)], biases[0][:, :, h % cfg["hq"]]))
                                ins = products(TP, TAIL * j, MAIN, S, lhs(j, 128), rhs, adds)
                        ins.then_inc(sg["scores_ready"], 1)

                    def weigh(z):
                        h, g = steps[z]
                        a = acc_of[h]
                        pe.wait_ge(sg["exp_done"], z + 1)
                        if g == 0 and h % cfg["hq"] == 0:
                            pe.wait_ge(sg["v_ready"], h // cfg["hq"] + 1)
                        first = g == 0 and h == accs[a][0]
                        if first and a >= 1:
                            pe.wait_ge(sg["o_taken"], a)
                        last = h == accs[a][-1] and g == NG
                        begun = set()
                        for j, base in (groups[g] if g < NG else []):
                            m = rows(j)
                            t_first = 128 * j if causal else 0
                            for t0, t1, v0, v1, p0, bank, col in pieces:
                                if t0 < t_first:
                                    continue
                                start = first and (p0 // 32, bank) not in begun
                                begun |= {(q, bank) for q in range(p0 // 32, -(-(p0 + v1 - v0) // 32))}
                                ins = nc.tensor.matmul(OP[p0:p0 + v1 - v0, bank, col:col + t1 - t0],
                                                       V[0:m, j, h // rep, v0:v1],
                                                       P[0:m, z % (LAG + 1), base + t0 - t_first:base + t1 - t_first],
                                                       start=start, stop=False, skip_group_check=True)
                        if g == NG:
                            for j in range(NT):
                                m = rows(j)
                                for n, (v0, v1, p0, bank, col) in enumerate(tails):
                                    start = OB > 1 and j == 0 and n == 0
                                    ins = nc.tensor.matmul(OP[p0:p0 + v1 - v0, bank, col:col + TAIL],
                                                           V[0:m, j, h // rep, v0:v1],
                                                           P[0:m, z % (LAG + 1), TAIL * j:TAIL * j + TAIL], start=start,
                                                           stop=last and j == NT - 1, skip_group_check=True)
                        ins.then_inc(sg["pv_done"], 1)

                    done, turned, z_done = 0, 0, 0

                    def maxima_until(goal, z):
                        nonlocal done, turned, z_done
                        while done < min(goal, len(maxima)):
                            chunk_logits(done)
                            done += 1
                            z_done = z
                            if done == (turned + 1) * per_unit + TURN and turned < UNITS - 1:
                                turn_maxima(turned)
                                turned += 1

                    for z in range(len(steps)):
                        h, g = steps[z]
                        goal = (h // HS + 1) * per_unit + LEAD + ratio * (z - (h // HS) * HS * (NG + 1))
                        maxima_until(goal, z)
                        if turned == UNITS - 1 and done == len(maxima) and (h // HS == UNITS - 1 or z >= z_done + 2):
                            turn_maxima(turned)
                            turned += 1
                        scores(z)
                        maxima_until(goal + 1, z)
                        if z >= LAG:
                            weigh(z - LAG)
                    for z in range(len(steps) - LAG, len(steps)):
                        weigh(z)

                @block.scalar
                def _(act):
                    def take_outputs(a):
                        act.wait_ge(sg["pv_done"], (accs[a][-1] + 1) * (NG + 1))
                        for p0, nr, bank, col, n in evac:
                            ins = nc.scalar.copy(O[p0:p0 + nr, a * OB + bank, col:col + n], OP[p0:p0 + nr, bank, col:col + n])
                        ins.then_inc(sg["o_taken"], 1)
                        act.wait_ge(sg["o_taken"], a + 1)
                        dst = o_d[ds(b * len(accs) + a, 1)].rearrange("o r t -> (o r) t")
                        for p0, nr, bank, col, r0, t0, nt in stores:
                            act.dma_start(dst[r0:r0 + nr, t0:t0 + nt], O[p0:p0 + nr, a * OB + bank, col:col + nt]) \
                                .then_inc(sg["store_done"], 16)
                        if causal:
                            tiles = dst[:, 0:MAIN].rearrange("r (m q c) -> r q m c", q=4, c=128)
                            for q in range(4):
                                act.dma_start(tiles[0:RW, q], O[32 * q:32 * q + RW, a * OB, 0:256]
                                              .rearrange("r (m c) -> r m c", c=128)).then_inc(sg["store_done"], 16)

                    taken = 0
                    for z, (h, g) in enumerate(steps):
                        act.wait_ge(sg["scores_ready"], z + 1)
                        if z >= LAG + 1:
                            act.wait_ge(sg["pv_done"], z - LAG)
                        if g < NG:
                            j, base = groups[g][-1]
                            m, n = rows(j), base + width(j)
                            nc.scalar.activation(P[0:m, z % (LAG + 1), 0:n], SC[0:m, mains.index(z) % 2, 0:n], ACT.Exp,
                                                 bias=k["zero"][0:m, :]).then_inc(sg["exp_done"], 1)
                        else:
                            nc.scalar.activation(P[:, z % (LAG + 1), 0:TAIL * NT], TP[:, 0:TAIL * NT], ACT.Exp,
                                                 bias=k["zero"][:]).then_inc(sg["exp_done"], 1)
                        if taken < len(accs) and z == (accs[taken][-1] + 1) * (NG + 1) - 1 + LAG:
                            take_outputs(taken)
                            taken += 1
                    for a in range(taken, len(accs)):
                        take_outputs(a)

                @block.vector
                def _(dve):
                    link = Chain(dve, sg["dve_step"])

                    def own_keys(im):
                        dve.wait_ge(sg[f"loaded{im}"], 16 * 2 * len(combos))
                        for h in range(im * cfg["hq"], (im + 1) * cfg["hq"]):
                            nc.vector.tensor_scalar(KM[:, h, :], KA[:, 0, h // HS, :], own[:, h % HS:h % HS + 1], None,
                                                    ALU.mult).then_inc(sg["own_ready"], 1)

                    def spread_v(im):
                        dve.wait_ge(sg[f"v_in{im}"], 16)
                        vs = VX[:, im].rearrange("p n (h d) -> p n h d", d=hd)
                        vd = V[:, :, im * hk:im * hk + hk, :]
                        for i in range(hpa):
                            ins = nc.vector.tensor_copy(vd[:, :, i:hk:hpa, i * hd:i * hd + hd], vs[:, :, i:hk:hpa, :])
                        ins.then_inc(sg["v_ready"], 1)

                    if HS > 1:
                        own_keys(0)

                    def copy_turned(u):
                        if u >= 2:
                            dve.wait_ge(sg["nm_stored"], 16 * (u - 1))
                        dve.wait_ge(sg["nmT_done"], u + 1)
                        nc.vector.tensor_copy(nmT[:, u % 2, :], nmP).then_inc(sg["nmT_copied"], 1)

                    for n, (h, c) in enumerate(maxima):
                        if c < len(chunks):
                            i, cc = chunks[c]
                            z = h * len(chunks) + c
                            m, cols = rows(i), min(512, limit(i) - 512 * cc)
                            dve.wait_ge(sg["chunk_ready"], z + 1)
                            nc.vector.tensor_reduce(NM[0:m, h, i, cc:cc + 1], CP[0:m, z % 2, 0:cols], AX, ALU.max) \
                                .then_inc(sg["max_taken"], 1)
                        else:
                            i0 = tiles_t[0]
                            dve.wait_ge(sg["tail_ready"], h + 1)
                            nc.vector.tensor_reduce(NM[:, h, i0:NT, 2],
                                                    TP[:, TAIL * i0:TAIL * NT].rearrange("p (i t) -> p i t", t=TAIL),
                                                    AX, ALU.max).then_inc(sg["tail_read"], 1)
                        if n == len(chunks):
                            spread_v(0)
                            for im in range(1, IM):
                                if HS > 1:
                                    own_keys(im)
                                spread_v(im)
                        u = n // per_unit
                        if u >= 1 and n == u * per_unit + TURN:
                            copy_turned(u - 1)
                        if n % per_unit < per_unit - 1:
                            continue
                        dve.wait_ge(sg["max_taken"], (h + 1) * len(chunks))
                        dve.wait_ge(sg["tail_read"], h + 1)
                        link(nc.vector.tensor_reduce(nmx[:], NM[:, u * HS:u * HS + HS], AX, ALU.max, negate=True))
                        for r in range(3):
                            ins = nc.vector.tensor_copy(nmp[:, :, r, :], nmx[:])
                            if r < 2:
                                link(ins)
                                link(nc.vector.tensor_tensor(nmx[:], nmx[:], nmp[:, :, r, :], ALU.subtract))
                        ins.then_inc(sg["nm_ready"], 1)
                    copy_turned(UNITS - 1)
            sg.end_turn()


def attention_output(nc, k, cfg, h_in, h_out, o_d, x_d, x1_d, w):
    SH = [128, NT, D]
    hd, hq = cfg["hd"], cfg["hq"]
    hpa = heads_acc(cfg)
    n_acc = -(-cfg["heads_turn"] // hpa) * (hq // cfg["heads_turn"])
    RO = D + hq
    BT = 512 // RO
    last = S % 128
    proj = w is not None
    with ExitStack() as ctx:
        def sb(name, shape, dt=F32):
            return ctx.enter_context(nc.sbuf_tensor(f"{cfg['name']}_o_{name}", shape, dt))

        once = Signals(nc, ctx, cfg["name"] + "_o", "w_in ones_set")
        sgs = [Signals(nc, ctx, f"{cfg['name']}_o{i}", "in_done x_in turned dve_step o_ready oT_done oT_copied y_done "
                                                  "out_ready store_done") for i in range(2)]
        pair = lambda name, shape: [sb(f"{name}{i}", shape) for i in range(2)]
        OD_ = pair("OD", [RO, S])
        O_, x_, y_ = (pair(n, SH) for n in ("O", "x", "y"))
        rden_ = pair("rden", [128, NT, hq])
        oT_ = pair("oT", [D + 1, NT * 128])
        wT = sb("wT", [D + 1, D])
        psN = ctx.enter_context(nc.psum_tensor(f"{cfg['name']}_o_psN", [128, 3, 512], F32))
        psT = ctx.enter_context(nc.psum_tensor(f"{cfg['name']}_o_psT", [128, 3 * 512], F32))
        psY = ctx.enter_context(nc.psum_tensor(f"{cfg['name']}_o_psY", [128, 2 * 512], F32))
        KR = D + 1 if cfg["out_bias"] else D
        with nc.Block() as block:
            @block.sync
            def _(sp):
                if proj:
                    sp.dma_start(wT[0:KR, :], w).then_inc(once["w_in"], 16)
                    sp.wait_ge(once["w_in"], 16)

            @block.vector
            def _(dve):
                for i in range(2):
                    nc.vector.memset(oT_[i][:], 1.0).then_inc(once["ones_set"], 1)
                    nc.vector.memset(O_[i][:], 0.0).then_inc(once["ones_set"], 1)
                dve.wait_ge(once["ones_set"], 4)
        once.end_turn()
        with nc.Fori(0, B // 2) as b2:
            with nc.Block() as block:
                @block.sync
                def _(sp):
                    for i, sg in enumerate(sgs):
                        b = 2 * b2 + i
                        OD, x = OD_[i], x_[i]
                        src = o_d[ds(b * n_acc, n_acc)]
                        for a in range(n_acc):
                            n = min(hpa, hq - a * hpa)
                            h0 = a * hpa
                            sp.dma_start(OD[h0 * hd:(h0 + n) * hd, :], src[a, 0:n * hd, 0:S]).then_inc(sg["in_done"], 16)
                            sp.dma_start(OD[D + h0:D + h0 + n, :], src[a, hpa * hd:hpa * hd + n, 0:S]) \
                                .then_inc(sg["in_done"], 16)
                        if x_d is None:
                            src = h_in[ds(b * S, NT * 128), :]
                        else:
                            src = x_d[ds(b * NT * 128, NT * 128), :]
                        sp.dma_start(x[:], src.rearrange("(n p) d -> p n d", p=128)).then_inc(sg["x_in"], 16)
                    for i, sg in enumerate(sgs):
                        b = 2 * b2 + i
                        y = y_[i]
                        sp.wait_ge(sg["out_ready"], 1)
                        out = h_out if x1_d is None else x1_d
                        sp.dma_start(out[ds(b * S, S - last), :].rearrange("(n p) d -> p n d", p=128), y[:, 0:NT - 1]) \
                            .then_inc(sg["store_done"], 16)
                        sp.dma_start(out[ds(b * S + S - last, last), :], y[0:last, NT - 1]).then_inc(sg["store_done"], 16)
                    for sg in sgs:
                        sp.wait_ge(sg["store_done"], 32)

                @block.tensor
                def _(pe):
                    for i, sg in enumerate(sgs):
                        OD, O, oT = OD_[i], O_[i], oT_[i]
                        if i == 1:
                            pe.wait_ge(sgs[0]["o_ready"], 1)
                        pe.wait_ge(sg["in_done"], 32 * n_acc)
                        for n in range(NT):
                            m = min(128, S - 128 * n)
                            c = RO * (n % BT)
                            ins = nc.tensor.transpose(psN[0:m, n // BT, c:c + RO], OD[:, 128 * n:128 * n + m],
                                                      k["ident"][0:RO, 0:RO])
                        ins.then_inc(sg["turned"], 1)
                        if proj:
                            pe.wait_ge(sg["o_ready"], 1)
                            for n in range(NT):
                                ins = nc.tensor.transpose(psT[0:D, n * 128:n * 128 + 128], O[:, n, :], k["ident"][:])
                            ins.then_inc(sg["oT_done"], 1)
                            pe.wait_ge(sg["oT_copied"], 1)
                            if i == 1:
                                pe.wait_ge(sgs[0]["out_ready"], 1)
                            for n in range(NT):
                                ins = nc.tensor.matmul(psY[:, n * D:n * D + D], oT[0:KR, n * 128:n * 128 + 128], wT[0:KR, :],
                                                       start=True, stop=True)
                            ins.then_inc(sg["y_done"], 1)

                @block.scalar
                def _(act):
                    for i, sg in enumerate(sgs):
                        oT = oT_[i]
                        if proj:
                            act.wait_ge(sg["oT_done"], 1)
                            nc.scalar.copy(oT[0:D, :], psT[0:D, 0:NT * 128]).then_inc(sg["oT_copied"], 1)

                @block.vector
                def _(dve):
                    for i, sg in enumerate(sgs):
                        O, x, y, rden = O_[i], x_[i], y_[i], rden_[i]
                        link = Chain(dve, sg["dve_step"])
                        dve.wait_ge(sg["turned"], 1)
                        parts = [(128, n, min(n + BT, NT - 1)) for n in range(0, NT - 1, BT)] + [(last, NT - 1, NT)]
                        for m, n0, n1 in parts:
                            c = RO * (n0 % BT)
                            t = psN[0:m, n0 // BT, c:c + RO * (n1 - n0)].rearrange("p (n r) -> p n r", r=RO)
                            link(nc.vector.reciprocal(rden[0:m, n0:n1, :], t[:, :, D:RO]))
                            for n in range(n0, n1):
                                ins = nc.vector.tensor_tensor(
                                    O[0:m, n, :].rearrange("p (h d) -> p h d", d=hd),
                                    t[:, n - n0, 0:D].rearrange("p (h d) -> p h d", d=hd),
                                    per_row(rden[0:m, n, :], [m, hq, hd]), ALU.mult)
                        ins.then_inc(sg["o_ready"], 1)
                        dve.wait_ge(sg["x_in"], 16)
                        if proj:
                            dve.wait_ge(sg["y_done"], 1)
                            a = psY[:, 0:NT * D].rearrange("p (n d) -> p n d", d=D)
                        else:
                            dve.wait_ge(sg["o_ready"], 1)
                            a = O[:]
                        nc.vector.tensor_tensor(y[:], a, x[:], ALU.add).then_inc(sg["out_ready"], 1)
            for sg in sgs:
                sg.end_turn()


def attention_stage(nc, k, cfg, h_in, h_out, w, x1_d=None):
    name = cfg["name"]
    hd, hk = cfg["hd"], cfg["hk"]
    parts_d = nc.dram_tensor(name + "_parts", [B * 3, D + hk * hd, S], BF16).ap()
    v_d = nc.dram_tensor(name + "_v", [B, 128, NT, hk * hd], F32).ap()
    hpa = heads_acc(cfg)
    n_acc = -(-cfg["heads_turn"] // hpa) * (cfg["hq"] // cfg["heads_turn"])
    o_d = nc.dram_tensor(name + "_o", [B * n_acc, hpa * (hd + 1), NT * 128], F32).ap()
    x_d = nc.dram_tensor(name + "_x", [B * NT * 128, D], F32).ap() if x1_d is not None else None
    attention_project(nc, k, cfg, h_in, w, parts_d, v_d, x_d)
    if cfg["rowmax"]:
        nm_d = nc.dram_tensor(name + "_nm", [cfg["images_turn"] * cfg["hq"] // cfg["stack"], cfg["stack"] * 3 * NT, 128], BF16).ap()
        attention_core_max(nc, k, cfg, parts_d, v_d, nm_d, o_d, w)
    else:
        attention_core_bounded(nc, k, cfg, parts_d, v_d, o_d, w)
    attention_output(nc, k, cfg, h_in, h_out, o_d, x_d, x1_d, w.get("wo"))


ATT = {
    "L0": dict(name="att0", images_turn=2, stack=8, hd=2, hq=32, hk=32, heads_turn=32, causal=True, window=False, rowmax=False, bias=False, kind="rmspair",
               out_bias=False),
    "L1": dict(name="att1", images_turn=1, stack=1, hd=64, hq=1, hk=1, heads_turn=1, causal=False, window=False, rowmax=True, bias=True, kind="plain",
               out_bias=False),
    "L2": dict(name="att2", images_turn=2, stack=2, hd=8, hq=8, hk=8, heads_turn=8, causal=False, window=True, rowmax=True, bias=False, kind="plain",
               out_bias=True),
    "L2f": dict(name="att2f", images_turn=4, stack=1, hd=16, hq=4, hk=2, heads_turn=4, causal=True, window=False, rowmax=True, bias=False, kind="rope",
                out_bias=False),
}


def own_rows(hd, stack, extra):
    import numpy as np
    head = np.concatenate([np.tile(np.repeat(np.arange(stack), hd), 6 if extra else 8), np.repeat(np.arange(stack), extra)])
    head = np.concatenate([head, np.full(128 - len(head), stack)])
    return (head[:, None] == np.arange(stack)[None, :]).astype(np.float32)


def constants():
    import numpy as np
    from concourse import mybir as mb
    bf = mb.dt.np(mb.dt.bfloat16)
    r = np.arange(128)
    inv = 1.0 / 10000.0 ** (np.arange(0, 16, 2, dtype=np.float32) / 16)
    emb = np.outer(np.arange(NT * 128, dtype=np.float32), inv)
    emb = np.concatenate([emb, emb], -1)
    sin = np.sin(emb)
    sin[:, :8] *= -1
    rope = np.stack([np.cos(emb), sin]).reshape(2, NT, 128, 16).transpose(2, 0, 1, 3)
    return {
        "ident": np.eye(128, dtype=np.float32),
        "identb": np.eye(128, dtype=np.float32).astype(bf),
        "mask_st": np.where(r[:, None] > r[None, :], NEG, 0.0).astype(np.float32).astype(bf),
        "mask_ts": np.where(r[None, :] > r[:, None], NEG, 0.0).astype(np.float32).astype(bf),
        "shift": (np.arange(WS2)[:, None] == np.arange(132)[None, :] - (S - WS2) % 128).astype(np.float32),
        "iota": np.tile(np.arange(16, dtype=np.float32), (128, 1)),
        "rope": np.ascontiguousarray(rope.astype(np.float32)),
        "ones3": np.ones((6, 8 * S), np.float32).astype(bf),
        "own0": own_rows(2, 8, 0),
        "own2": own_rows(8, 2, 3),
    }



def gated_ffn_stage(nc, k, cfg, h_in, h_out, w, x1_d):
    E, F, chunks = cfg["E"], cfg["F"], cfg["chunks"]
    EP = max(8, E)
    UNITS = E * chunks
    SH = [128, FT, D]
    parts = [(n, min(5, FT - n)) for n in range(0, FT, 5)]
    half = lambda p: 64 * parts[p][1]
    with ExitStack() as ctx:
        def sb(name, shape, dt=F32):
            return ctx.enter_context(nc.sbuf_tensor(f"{cfg['name']}_{name}", shape, dt))

        sg = Signals(nc, ctx, cfg["name"], "w_in x_in x1_in preset dve_step var_ready std_ready u_ready uT_done uT_copied "
                              "logits_done shifted_ready exp_ready c_ready hid_done hid_used gate_used unit_done y_used out_ready store_done")
        x, xc, sq, u, y = (sb(n, SH) for n in ("x", "xc", "sq", "u", "y"))
        x1 = sb("x1", SH)
        stat = sb("stat", [128, 4, FT])
        uT = sb("uT", [128, FTOK])
        w1 = sb("w1", [128, UNITS, 128])
        w3 = sb("w3", [128, UNITS, 128])
        w2 = sb("w2", [128, UNITS, D])
        rw = sb("rw", [128, E])
        lnw = sb("lnw", [128, D])
        hT = sb("hT", [128, 2, 640])
        gT = sb("gT", [128, 2, 640])
        lg = sb("lg", [128, FT, EP])
        top = sb("top", [128, FT, 8])
        idx = sb("idx", [128, FT, 8], U32)
        idxf = sb("idxf", [128, FT, 8])
        rst = sb("rst", [128, 4, FT])
        wt = sb("wt", [128, FT, 2])
        c = sb("c", [128, FT, E])
        c2 = sb("c2", [128, FT, E])
        acc = sb("acc", SH)
        HP = ctx.enter_context(nc.psum_tensor(f"{cfg['name']}_HP", [128, 4, 512], F32))
        YP = ctx.enter_context(nc.psum_tensor(f"{cfg['name']}_YP", [128, 2, 512], F32))
        MP = ctx.enter_context(nc.psum_tensor(f"{cfg['name']}_MP", [128, 2 * 512], F32))
        lgP = MP[:, 768:768 + FT * 16].rearrange("p (n e) -> p n e", e=16)
        blank = [uT, w1, w2, w3, rw]
        n_preset = len(blank) + 1
        with nc.Block() as block:
            @block.sync
            def _(sp):
                sp.wait_ge(sg["preset"], n_preset)
                loads = [(w1[0:D, :, 0:F], w["w1"]), (w3[0:D, :, 0:F], w["w3"]), (w2[0:F], w["w2"]),
                         (rw[0:D, :], w["rw"]), (lnw[:], w["ln"].partition_broadcast(128))]
                for n, (dst, src) in enumerate(loads):
                    sp.dma_start(dst, src).then_inc(sg["w_in"], 16)
                    sp.wait_ge(sg["w_in"], 16 * (n + 1))

            @block.vector
            def _(dve):
                for t in blank:
                    nc.vector.memset(t[:], 0.0).then_inc(sg["preset"], 1)
                nc.vector.memset(lg[:], NEG).then_inc(sg["preset"], 1)
                dve.wait_ge(sg["preset"], n_preset)
        sg.end_turn()
        units = [(p, un) for p in range(len(parts)) for un in range(UNITS)]
        items = [(gu, hf) for gu in range(len(units)) for hf in range(2)]
        with nc.Fori(0, F_TURNS) as it:
            with nc.Block() as block:
                @block.sync
                def _(sp):
                    tok = lambda t: t[ds(it * FTOK, FTOK), :].rearrange("(p n) d -> p n d", n=FT)
                    sp.dma_start(x1[:], tok(x1_d)).then_inc(sg["x1_in"], 16)
                    sp.dma_start(x[:], tok(h_in)).then_inc(sg["x_in"], 16)
                    sp.wait_ge(sg["out_ready"], 1)
                    sp.dma_start(tok(h_out), y[:]).then_inc(sg["store_done"], 16)
                    sp.wait_ge(sg["store_done"], 16)

                @block.tensor
                def _(pe):
                    pe.wait_ge(sg["u_ready"], 1)
                    for p, (n0, nn) in enumerate(parts):
                        if p >= 1:
                            pe.wait_ge(sg["uT_copied"], p)
                        for n in range(nn):
                            ins = nc.tensor.transpose(MP[0:D, 128 * n:128 * n + 128], u[:, n0 + n, :], k["ident"][:])
                        ins.then_inc(sg["uT_done"], 1)
                    pe.wait_ge(sg["uT_copied"], len(parts))
                    for n in range(FT):
                        ins = nc.tensor.matmul(lgP[:, n, 0:E], uT[:, 128 * n:128 * n + 128], rw[:], start=True,
                                               stop=True)
                    ins.then_inc(sg["logits_done"], 1)

                    def hidden(gu):
                        p, un = units[gu]
                        cn = half(p)
                        for hf in range(2):
                            z = 2 * gu + hf
                            c0 = 128 * parts[p][0] + cn * hf
                            if z >= 2:
                                pe.wait_ge(sg["hid_used"], z - 1)
                            nc.tensor.matmul(HP[:, 2 * (z % 2), 0:cn], w1[:, un, :], uT[:, c0:c0 + cn],
                                             start=True, stop=True)
                            nc.tensor.matmul(HP[:, 2 * (z % 2) + 1, 0:cn], w3[:, un, :], uT[:, c0:c0 + cn],
                                             start=True, stop=True).then_inc(sg["hid_done"], 1)

                    def outputs(gu):
                        p, un = units[gu]
                        e, ch = un // chunks, un % chunks
                        pe.wait_ge(sg["hid_used"], 2 * gu + 2)
                        if ch == 0 and p * E + e >= 2:
                            pe.wait_ge(sg["y_used"], p * E + e - 1)
                        for n in range(parts[p][1]):
                            ins = nc.tensor.matmul(YP[:, e % 2, D * n:D * n + D], hT[:, gu % 2, 128 * n:128 * n + 128],
                                                   w2[:, un, :], start=(ch == 0 and n == 0), stop=(ch == chunks - 1),
                                                   skip_group_check=True)
                        ins.then_inc(sg["unit_done"], 1)

                    for gu, (p, un) in enumerate(units):
                        hidden(gu)
                        if gu >= 1:
                            outputs(gu - 1)
                    outputs(len(units) - 1)

                @block.scalar
                def _(act):
                    act.wait_ge(sg["var_ready"], 1)
                    act_std(nc, stat, k["eps6"][:]).then_inc(sg["std_ready"], 1)
                    for p, (n0, nn) in enumerate(parts):
                        act.wait_ge(sg["uT_done"], p + 1)
                        nc.scalar.copy(uT[0:D, 128 * n0:128 * n0 + 128 * nn], MP[0:D, 0:128 * nn]) \
                            .then_inc(sg["uT_copied"], 1)
                    act.wait_ge(sg["shifted_ready"], 1)
                    nc.scalar.activation(lg[:, :, 0:E], lg[:, :, 0:E], ACT.Exp).then_inc(sg["exp_ready"], 1)
                    for z, (gu, hf) in enumerate(items):
                        cn = half(units[gu][0])
                        cols = slice(cn * hf, cn * hf + cn)
                        act.wait_ge(sg["hid_done"], z + 1)
                        if z >= 4:
                            act.wait_ge(sg["hid_used"], z - 3)
                        nc.scalar.activation(gT[:, gu % 2, cols], HP[:, 2 * (z % 2), 0:cn], ACT.Silu) \
                            .then_inc(sg["gate_used"], 1)

                @block.vector
                def _(dve):
                    link = Chain(dve, sg["dve_step"])
                    dve.wait_ge(sg["x1_in"], 16)
                    link(nc.vector.tensor_tensor(sq[:], x1[:], x1[:], ALU.mult))
                    nc.vector.tensor_reduce(stat[:, 1], sq[:], AX, ALU.add).then_inc(sg["var_ready"], 1)
                    dve.wait_ge(sg["std_ready"], 1)
                    link(dve_scale_rows(nc, link, xc[:], x1[:], stat, SH))
                    nc.vector.tensor_tensor(u[:], xc[:], lnw[:].unsqueeze(1).to_broadcast(SH), ALU.mult) \
                        .then_inc(sg["u_ready"], 1)
                    dve.wait_ge(sg["logits_done"], 1)
                    link(nc.vector.tensor_reduce(rst[:, 0], lgP[:, :, 0:E], AX, ALU.max))
                    nc.vector.tensor_tensor(lg[:, :, 0:E], lgP[:, :, 0:E], per_row(rst[:, 0], [128, FT, E]),
                                            ALU.subtract).then_inc(sg["shifted_ready"], 1)
                    dve.wait_ge(sg["exp_ready"], 1)
                    link(nc.vector.tensor_reduce(rst[:, 0], lg[:, :, 0:E], AX, ALU.add))
                    link(nc.vector.reciprocal(rst[:, 1], rst[:, 0]))
                    link(nc.vector.tensor_tensor(lg[:, :, 0:E], lg[:, :, 0:E], per_row(rst[:, 1], [128, FT, E]),
                                                 ALU.mult))
                    for n in range(FT):
                        ins = nc.vector.max(top[:, n, :], lg[:, n, :])
                    link(ins)
                    for n in range(FT):
                        ins = nc.vector.max_index(idx[:, n, :], top[:, n, :], lg[:, n, :])
                    link(ins)
                    link(nc.vector.tensor_copy(idxf[:], idx[:]))
                    link(nc.vector.tensor_tensor(rst[:, 0], top[:, :, 0], top[:, :, 1], ALU.add))
                    link(nc.vector.tensor_scalar(rst[:, 0], rst[:, 0], cfg["guard"], None, ALU.add))
                    link(nc.vector.reciprocal(rst[:, 1], rst[:, 0]))
                    link(nc.vector.tensor_tensor(wt[:], top[:, :, 0:2], per_row(rst[:, 1], [128, FT, 2]), ALU.mult))
                    for n in range(FT):
                        nc.vector.tensor_scalar(c[:, n, :], k["iota"][:, 0:E], idxf[:, n, 0:1], wt[:, n, 0:1],
                                                ALU.is_equal, ALU.mult)
                        ins = nc.vector.tensor_scalar(c2[:, n, :], k["iota"][:, 0:E], idxf[:, n, 1:2], wt[:, n, 1:2],
                                                      ALU.is_equal, ALU.mult)
                    link(ins)
                    nc.vector.tensor_tensor(c[:], c[:], c2[:], ALU.add).then_inc(sg["c_ready"], 1)
                    dve.wait_ge(sg["c_ready"], 1)

                    def add_outputs(gu):
                        p, un = units[gu]
                        n0, nn = parts[p]
                        e = un // chunks
                        dve.wait_ge(sg["unit_done"], gu + 1)
                        if e >= 1:
                            dve.wait_ge(sg["y_used"], p * E + e)
                        for n in range(n0, n0 + nn):
                            ye = YP[:, e % 2, D * (n - n0):D * (n - n0) + D]
                            if e == 0:
                                ins = nc.vector.tensor_scalar(acc[:, n, :], ye, c[:, n, e:e + 1], None, ALU.mult)
                            else:
                                ins = nc.vector.scalar_tensor_tensor(acc[:, n, :], ye, c[:, n, e:e + 1], acc[:, n, :],
                                                                     ALU.mult, ALU.add)
                        ins.then_inc(sg["y_used"], 1)

                    for z, (gu, hf) in enumerate(items):
                        cn = half(units[gu][0])
                        cols = slice(cn * hf, cn * hf + cn)
                        dve.wait_ge(sg["gate_used"], z + 1)
                        if gu >= 2:
                            dve.wait_ge(sg["unit_done"], gu - 1)
                        nc.vector.tensor_tensor(hT[:, gu % 2, cols], gT[:, gu % 2, cols],
                                                HP[:, 2 * (z % 2) + 1, 0:cn], ALU.mult).then_inc(sg["hid_used"], 1)
                        if hf == 1 and gu >= 1 and (gu - 1) % chunks == chunks - 1:
                            add_outputs(gu - 1)
                    add_outputs(len(units) - 1)
                    dve.wait_ge(sg["y_used"], len(parts) * E)
                    dve.wait_ge(sg["x_in"], 16)
                    link(nc.vector.tensor_tensor(acc[:], acc[:], x1[:], ALU.add))
                    nc.vector.tensor_tensor(y[:], acc[:], x[:], ALU.add).then_inc(sg["out_ready"], 1)
            sg.end_turn()



def ffn_stage(nc, k, cfg, h_in, h_out, w):
    E, F, mode = cfg["E"], cfg["F"], cfg["mode"]
    EP = max(8, E)
    pair, deep = cfg["pair"], cfg["deep"]
    UNITS = E // 2 if pair else E
    M = 128
    layers = 2 if deep else 1
    KR = D + 1
    SH = [128, FT, D]
    n_parts = -(-FT // 8)
    bounds = [-(-FT * i // n_parts) for i in range(n_parts + 1)]
    parts = [(n0, n1 - n0) for n0, n1 in zip(bounds, bounds[1:])]
    halves = [((n0, nn - nn // 2), (n0 + nn - nn // 2, nn // 2)) for n0, nn in parts]
    HC = 128 * max(nn for p in halves for n0, nn in p)
    FUNC = {"gelu": ACT.Gelu, "relu": ACT.Relu, "silu": ACT.Silu}[cfg["act"]]
    RH = 32
    with ExitStack() as ctx:
        def sb(name, shape, dt=F32):
            return ctx.enter_context(nc.sbuf_tensor(f"{cfg['name']}_{name}", shape, dt))

        sg = Signals(nc, ctx, cfg["name"], "w_in x_in preset dve_step var_ready std_ready u_ready uT_done uT_copied rh_done "
                              "rh_copied logits_done shifted_ready exp_ready gap_ready gap_exp c_ready cT_done cT_copied "
                              "hid_ready first_ready mid_ready a_ready cb_ready weighed out_done y_done y_copied half_turned y_turned y_taken c_parts out_ready store_done")
        x, xc, sq, u, y = (sb(n, SH) for n in ("x", "xc", "sq", "u", "y"))
        stat = sb("stat", [128, 4, FT])
        uT = sb("uT", [128, FTOK])
        w1 = sb("w1", [128, UNITS, M])
        wm = sb("wm", [128, UNITS, 128]) if deep else None
        bm = sb("bm", [128, UNITS]) if deep else None
        w2 = sb("w2", [128, UNITS, D])
        b2 = sb("b2", [3 * E, 2, D])
        b2p = sb("b2p", [128, 3, D], BF16)
        sel = sb("sel", [128, UNITS, 128], BF16)
        rw = sb("rw", [128, E])
        rw1 = sb("rw1", [128, RH]) if deep else None
        rhT = sb("rhT", [128, FTOK]) if deep else None
        gb = sb("gb", [128, 2, D]) if cfg["post"] else None
        gT = sb("gT", [128, 4, HC]) if deep else None
        aT = sb("aT", [128, 4, HC])
        hT = sb("hT", [128, 4, HC])
        yT = sb("yT", [128, HC])
        lg = sb("lg", [128, FT, EP])
        top = sb("top", [128, FT, 8])
        idx = sb("idx", [128, FT, 8], U32)
        idxf = sb("idxf", [128, FT, 8])
        rst = sb("rst", [128, 4, FT])
        wt = sb("wt", [128, FT, 2])
        c = sb("c", [128, FT, E])
        c2 = sb("c2", [128, FT, E])
        cp = sb("cp", [128, FT, 3, E], BF16)
        cT = sb("cT", [128, FTOK], BF16)
        acc = sb("acc", SH)
        HP = ctx.enter_context(nc.psum_tensor(f"{cfg['name']}_HP", [128, 4, 512], F32))
        YP = ctx.enter_context(nc.psum_tensor(f"{cfg['name']}_YP", [128, 2, 512], F32))
        CB = ctx.enter_context(nc.psum_tensor(f"{cfg['name']}_CB", [128, 2, 512], F32))
        MP = CB[:].rearrange("p a b -> p (a b)")
        cTP = MP.bitcast(BF16)[0:3 * E, 0:FTOK]
        lgP = MP[:, 768:768 + FT * 16].rearrange("p (n e) -> p n e", e=16)
        blank = [uT, w1, w2, rw, c, c2, cT] + [b2p] + ([rw1, rhT, wm] if deep else [])
        n_preset = len(blank) + (3 if deep else 2)
        n_loads = 7 + (4 if deep else 0) + (2 if cfg["post"] else 0)
        REXT = D + 1 if cfg["router_bias"] else D
        with nc.Block() as block:
            @block.sync
            def _(sp):
                sp.wait_ge(sg["preset"], n_preset)
                FU = M if pair else F
                loads = [(w1[0:KR, :, 0:FU], w["w1"]), (rw[0:(RH + 1 if deep else REXT), :], w["rw"])]
                loads.append((w2[:], w["w2"]))
                loads.append((sel[:], w["sel"]))
                loads += [(b2[E * r:E * r + E, 0, :], w["b2"]) for r in range(3)]
                if deep:
                    loads += [(rw1[0:KR], w["rw1"]), (bm[:], w["bm"]),
                              (wm[0:64, :, 0:64], w["wm"][0]), (wm[64:128, :, 64:128], w["wm"][1])]
                if cfg["post"]:
                    loads += [(gb[:, 0, :], w["gamma"].partition_broadcast(128)),
                              (gb[:, 1, :], w["beta"].partition_broadcast(128))]
                assert len(loads) == n_loads
                for n, (dst, src) in enumerate(loads):
                    sp.dma_start(dst, src).then_inc(sg["w_in"], 16)
                    sp.wait_ge(sg["w_in"], 16 * (n + 1))

            @block.vector
            def _(dve):
                for t in blank:
                    nc.vector.memset(t[:], 0.0).then_inc(sg["preset"], 1)
                nc.vector.memset(lg[:], NEG).then_inc(sg["preset"], 1)
                dve.wait_ge(sg["preset"], len(blank) + 1)
                nc.vector.memset(uT[D:D + 1, :], 1.0).then_inc(sg["preset"], 1)
                if deep:
                    nc.vector.memset(rhT[RH:RH + 1, :], 1.0).then_inc(sg["preset"], 1)
                dve.wait_ge(sg["preset"], n_preset)
                link = Chain(dve, sg["dve_step"])
                dve.wait_ge(sg["w_in"], 16 * n_loads)
                for r in range(3):
                    link(nc.vector.tensor_copy(b2p[0:3 * E, r, :], b2[:, r % 2, :]))
                    if r < 2:
                        link(nc.vector.tensor_tensor(b2[:, 1 - r % 2, :], b2[:, r % 2, :], b2p[0:3 * E, r, :],
                                                     ALU.subtract))
        sg.end_turn()
        columns = lambda p, hf: (128 * halves[p][hf][0], 128 * halves[p][hf][1])
        work = [(p, un, hf) for p in range(len(parts)) for un in range(UNITS) for hf in range(2)]
        last_of = [max(n for n, x in enumerate(work) if x[0] == p) for p in range(len(parts))]
        SPREAD = 2 if deep else 1
        OUT = SPREAD + 2
        with nc.Fori(0, F_TURNS) as it:
            with nc.Block() as block:
                @block.sync
                def _(sp):
                    tok = lambda t: t[ds(it * FTOK, FTOK), :].rearrange("(p n) d -> p n d", n=FT)
                    sp.dma_start(x[:], tok(h_in)).then_inc(sg["x_in"], 16)
                    sp.wait_ge(sg["out_ready"], 1)
                    sp.dma_start(tok(h_out), y[:]).then_inc(sg["store_done"], 16)
                    sp.wait_ge(sg["store_done"], 16)

                @block.tensor
                def _(pe):
                    pe.wait_ge(sg["u_ready"], 1)
                    for p, (n0, nn) in enumerate(parts):
                        if p >= 1:
                            pe.wait_ge(sg["uT_copied"], p)
                        for n in range(nn):
                            ins = nc.tensor.transpose(MP[0:D, 128 * n:128 * n + 128], u[:, n0 + n, :], k["ident"][:])
                        ins.then_inc(sg["uT_done"], 1)
                    pe.wait_ge(sg["uT_copied"], len(parts))
                    if deep:
                        for p, (n0, nn) in enumerate(parts):
                            if p >= 1:
                                pe.wait_ge(sg["rh_copied"], 2 * p)
                            for hf in range(2):
                                c0, cn = columns(p, hf)
                                ins = nc.tensor.matmul(MP[0:RH, 512 * hf:512 * hf + cn], rw1[:],
                                                       uT[:, c0:c0 + cn], start=True, stop=True)
                            ins.then_inc(sg["rh_done"], 1)
                        pe.wait_ge(sg["rh_copied"], 2 * len(parts))
                    for n in range(FT):
                        src = (rhT if deep else uT)[:, 128 * n:128 * n + 128]
                        ins = nc.tensor.matmul(lgP[:, n, 0:E], src, rw[:],
                                               start=True, stop=True)
                    ins.then_inc(sg["logits_done"], 1)

                    def first_layer(n):
                        p, un, hf = work[n]
                        c0, cn = columns(p, hf)
                        ring = 2 if deep else 4
                        if n >= ring:
                            pe.wait_ge(sg["first_ready" if deep else "a_ready"], n - ring + 1)
                        ins = nc.tensor.matmul(HP[:, n % ring, 0:cn], w1[:, un, :], uT[:, c0:c0 + cn],
                                               start=True, stop=True)
                        ins.then_inc(sg["hid_ready"], 1)

                    def middle_layer(n):
                        p, un, hf = work[n]
                        pe.wait_ge(sg["first_ready"], n + 1)
                        if n >= 2:
                            pe.wait_ge(sg["a_ready"], n - 1)
                        c0, cn = columns(p, hf)
                        nc.tensor.matmul(HP[:, 2 + n % 2, 0:cn], wm[:, un, :], gT[:, n % 4, 0:cn],
                                         start=True, stop=True).then_inc(sg["mid_ready"], 1)

                    def spread_weights(n):
                        p, un, hf = work[n]
                        c0, cn = columns(p, hf)
                        if n == 0:
                            pe.wait_ge(sg["cT_copied"], 1)
                        if n >= 2:
                            pe.wait_ge(sg["weighed"], n - 1)
                        nc.tensor.matmul(CB[:, n % 2, 0:cn], sel[:, un, :], cT[:, c0:c0 + cn], start=True, stop=True) \
                            .then_inc(sg["cb_ready"], 1)

                    def outputs(n):
                        p, un, hf = work[n]
                        c0, cn = columns(p, hf)
                        o = YP[D * hf:D * hf + D, 0, 0:cn]
                        if un == 0 and p >= 1:
                            pe.wait_ge(sg["y_taken"], p)
                        if un == 0:
                            for r in range(3):
                                nc.tensor.matmul(o, b2p[:, r, :], cT[:, c0:c0 + cn], start=(r == 0), stop=False,
                                                 skip_group_check=True)
                        pe.wait_ge(sg["weighed"], n + 1)
                        nc.tensor.matmul(o, w2[:, un, :], hT[:, n % 4, 0:cn], start=False,
                                         stop=(un == UNITS - 1), skip_group_check=True).then_inc(sg["out_done"], 1)

                    def turn_outputs(p):
                        pe.wait_ge(sg["y_copied"], p + 1)
                        for hf in range(2):
                            n0, nn = halves[p][hf]
                            r = slice(D * hf, D * hf + D)
                            if hf == 1:
                                ins.then_inc(sg["half_turned"], 1)
                                pe.wait_ge(sg["half_turned"], p + 1)
                            for n in range(nn):
                                col = D * (n0 + n - parts[p][0])
                                ins = nc.tensor.transpose(YP[:, 1, col:col + D], yT[r, 128 * n:128 * n + 128],
                                                          k["ident"][r, r])
                        ins.then_inc(sg["y_turned"], 1)

                    N = len(work)
                    for n in range(N + OUT):
                        if n < N:
                            first_layer(n)
                        if n == 1:
                            pe.wait_ge(sg["c_parts"], 1)
                            for t in range(FT):
                                ins = nc.tensor.transpose(cTP[:, 128 * t:128 * t + 128],
                                                          cp[:, t].rearrange("p r e -> p (r e)"), k["identb"][:])
                            ins.then_inc(sg["cT_done"], 1)
                        if deep and 1 <= n <= N:
                            middle_layer(n - 1)
                        if SPREAD <= n < N + SPREAD:
                            spread_weights(n - SPREAD)
                        for p in range(len(parts) - 1):
                            if n - OUT == last_of[p] + 1:
                                turn_outputs(p)
                        if n >= OUT and (n - OUT) % 2 == 1:
                            outputs(n - OUT - 1)
                            outputs(n - OUT)
                    turn_outputs(len(parts) - 1)

                @block.scalar
                def _(act):
                    act.wait_ge(sg["var_ready"], 1)
                    act_std(nc, stat, k["eps5"][:]).then_inc(sg["std_ready"], 1)
                    for p, (n0, nn) in enumerate(parts):
                        act.wait_ge(sg["uT_done"], p + 1)
                        nc.scalar.copy(uT[0:D, 128 * n0:128 * n0 + 128 * nn], MP[0:D, 0:128 * nn]) \
                            .then_inc(sg["uT_copied"], 1)
                    if deep:
                        for p, (n0, nn) in enumerate(parts):
                            act.wait_ge(sg["rh_done"], p + 1)
                            for hf in range(2):
                                c0, cn = columns(p, hf)
                                nc.scalar.activation(rhT[0:RH, c0:c0 + cn], MP[0:RH, 512 * hf:512 * hf + cn],
                                                     ACT.Relu).then_inc(sg["rh_copied"], 1)
                    if mode != "logits":
                        act.wait_ge(sg["shifted_ready"], 1)
                        nc.scalar.activation(lg[:, :, 0:E], lg[:, :, 0:E], ACT.Exp).then_inc(sg["exp_ready"], 1)

                    def copy_outputs(p):
                        act.wait_ge(sg["out_done"], last_of[p] + 1)
                        if p >= 1:
                            act.wait_ge(sg["y_turned"], p)
                        for hf in range(2):
                            c0, cn = columns(p, hf)
                            ins = nc.scalar.copy(yT[D * hf:D * hf + D, 0:cn], YP[D * hf:D * hf + D, 0, 0:cn])
                        ins.then_inc(sg["y_copied"], 1)

                    N = len(work)
                    for n in range(N + OUT + 1):
                        if n < N:
                            p, un, hf = work[n]
                            c0, cn = columns(p, hf)
                            act.wait_ge(sg["hid_ready"], n + 1)
                            if deep:
                                if n >= 4:
                                    act.wait_ge(sg["mid_ready"], n - 3)
                                nc.scalar.activation(gT[:, n % 4, 0:cn], HP[:, n % 2, 0:cn], FUNC) \
                                    .then_inc(sg["first_ready"], 1)
                            else:
                                if n >= 4:
                                    act.wait_ge(sg["weighed"], n - 3)
                                nc.scalar.activation(aT[:, n % 4, 0:cn], HP[:, n % 4, 0:cn], FUNC) \
                                    .then_inc(sg["a_ready"], 1)
                        if deep and 1 <= n <= N:
                            p, un, hf = work[n - 1]
                            c0, cn = columns(p, hf)
                            act.wait_ge(sg["mid_ready"], n)
                            if n - 1 >= 4:
                                act.wait_ge(sg["weighed"], n - 4)
                            nc.scalar.activation(aT[:, (n - 1) % 4, 0:cn], HP[:, 2 + (n - 1) % 2, 0:cn], FUNC,
                                                 bias=bm[:, un:un + 1]).then_inc(sg["a_ready"], 1)
                        if n == 0:
                            if mode != "probs":
                                act.wait_ge(sg["gap_ready"], 1)
                                nc.scalar.activation(rst[:, 3], rst[:, 2], ACT.Exp).then_inc(sg["gap_exp"], 1)
                        if n == 1:
                            act.wait_ge(sg["cT_done"], 1)
                            nc.scalar.copy(cT[0:3 * E, :], cTP).then_inc(sg["cT_copied"], 1)
                        for p in range(len(parts)):
                            if n - OUT == last_of[p]:
                                copy_outputs(p)
                    if cfg["post"]:
                        act.wait_ge(sg["var_ready"], 2)
                        act_std(nc, stat, k["eps5"][:]).then_inc(sg["std_ready"], 1)

                @block.vector
                def _(dve):
                    link = Chain(dve, sg["dve_step"])
                    dve.wait_ge(sg["x_in"], 16)
                    dve_center(nc, link, x[:], xc[:], sq[:], stat, SH).then_inc(sg["var_ready"], 1)
                    dve.wait_ge(sg["std_ready"], 1)
                    dve_scale_rows(nc, link, u[:], xc[:], stat, SH).then_inc(sg["u_ready"], 1)
                    dve.wait_ge(sg["logits_done"], 1)
                    if mode == "logits":
                        link(nc.vector.tensor_copy(lg[:, :, 0:E], lgP[:, :, 0:E]))
                    else:
                        link(nc.vector.tensor_reduce(rst[:, 0], lgP[:, :, 0:E], AX, ALU.max))
                        nc.vector.tensor_tensor(lg[:, :, 0:E], lgP[:, :, 0:E], per_row(rst[:, 0], [128, FT, E]),
                                                ALU.subtract).then_inc(sg["shifted_ready"], 1)
                        dve.wait_ge(sg["exp_ready"], 1)
                        link(nc.vector.tensor_reduce(rst[:, 0], lg[:, :, 0:E], AX, ALU.add))
                        link(nc.vector.reciprocal(rst[:, 1], rst[:, 0]))
                        link(nc.vector.tensor_tensor(lg[:, :, 0:E], lg[:, :, 0:E], per_row(rst[:, 1], [128, FT, E]),
                                                     ALU.mult))
                    for n in range(FT):
                        ins = nc.vector.max(top[:, n, :], lg[:, n, :])
                    link(ins)
                    for n in range(FT):
                        ins = nc.vector.max_index(idx[:, n, :], top[:, n, :], lg[:, n, :])
                    link(ins)
                    link(nc.vector.tensor_copy(idxf[:], idx[:]))
                    if mode == "probs":
                        link(nc.vector.tensor_tensor(rst[:, 0], top[:, :, 0], top[:, :, 1], ALU.add))
                        link(nc.vector.tensor_scalar(rst[:, 0], rst[:, 0], cfg["guard"], None,
                                                     ALU.max if cfg["guard"] < 1e-10 else ALU.add))
                        link(nc.vector.reciprocal(rst[:, 1], rst[:, 0]))
                        link(nc.vector.tensor_tensor(wt[:], top[:, :, 0:2], per_row(rst[:, 1], [128, FT, 2]), ALU.mult))
                    else:
                        nc.vector.tensor_tensor(rst[:, 2], top[:, :, 1], top[:, :, 0], ALU.subtract) \
                            .then_inc(sg["gap_ready"], 1)
                        dve.wait_ge(sg["gap_exp"], 1)
                        link(nc.vector.tensor_scalar(rst[:, 0], rst[:, 3], 1.0, None, ALU.add))
                        link(nc.vector.reciprocal(wt[:, :, 0], rst[:, 0]))
                        link(nc.vector.tensor_tensor(wt[:, :, 1], rst[:, 3], wt[:, :, 0], ALU.mult))
                    for n in range(FT):
                        nc.vector.tensor_scalar(c[:, n, :], k["iota"][:, 0:E], idxf[:, n, 0:1], wt[:, n, 0:1],
                                                ALU.is_equal, ALU.mult)
                        ins = nc.vector.tensor_scalar(c2[:, n, :], k["iota"][:, 0:E], idxf[:, n, 1:2], wt[:, n, 1:2],
                                                      ALU.is_equal, ALU.mult)
                    link(ins)
                    link(nc.vector.tensor_tensor(c[:], c[:], c2[:], ALU.add))
                    for r in range(3):
                        ins = nc.vector.tensor_copy(cp[:, :, r, :], c[:])
                        if r < 2:
                            link(ins)
                            link(nc.vector.tensor_tensor(c[:], c[:], cp[:, :, r, :], ALU.subtract))
                    ins.then_inc(sg["c_parts"], 1)

                    def take_outputs(p):
                        n0, nn = parts[p]
                        dve.wait_ge(sg["y_turned"], p + 1)
                        nc.vector.tensor_copy(acc[:, n0:n0 + nn, :],
                                              YP[:, 1, 0:D * nn].rearrange("p (n d) -> p n d", d=D)) \
                            .then_inc(sg["y_taken"], 1)

                    for n, (p, un, hf) in enumerate(work):
                        c0, cn = columns(p, hf)
                        dve.wait_ge(sg["a_ready"], n + 1)
                        if n >= 4:
                            dve.wait_ge(sg["out_done"], n - 3)
                        a = aT[:, n % 4, 0:cn]
                        dve.wait_ge(sg["cb_ready"], n + 1)
                        nc.vector.tensor_tensor(hT[:, n % 4, 0:cn], a, CB[:, n % 2, 0:cn], ALU.mult) \
                            .then_inc(sg["weighed"], 1)
                        for q in range(len(parts) - 1):
                            if n == last_of[q] + 1 + OUT - SPREAD:
                                take_outputs(q)
                    take_outputs(len(parts) - 1)
                    dve.wait_ge(sg["y_taken"], len(parts))
                    dve.wait_ge(sg["x_in"], 16)
                    if cfg["inner"]:
                        link(nc.vector.tensor_tensor(acc[:], acc[:], u[:], ALU.add))
                    if cfg["post"]:
                        dve_center(nc, link, acc[:], xc[:], sq[:], stat, SH).then_inc(sg["var_ready"], 1)
                        dve.wait_ge(sg["std_ready"], 2)
                        link(dve_scale_rows(nc, link, acc[:], xc[:], stat, SH))
                        link(nc.vector.tensor_tensor(acc[:], acc[:], gb[:, 0:1, :].to_broadcast(SH), ALU.mult))
                        link(nc.vector.tensor_tensor(acc[:], acc[:], gb[:, 1:2, :].to_broadcast(SH), ALU.add))
                    nc.vector.tensor_tensor(y[:], acc[:], x[:], ALU.add).then_inc(sg["out_ready"], 1)
            sg.end_turn()


FFN = {
    "L0": dict(name="ffn0", E=8, F=64, mode="probs", guard=1e-12, pair=True, glu=False, deep=False, chunks=1,
               act="gelu", router_bias=False, post=False, inner=True),
    "L1": dict(name="ffn1", E=16, F=128, mode="logits", guard=0.0, pair=False, glu=False, deep=False, chunks=1,
               act="relu", router_bias=True, post=True, inner=True),
    "L2": dict(name="ffn2", E=8, F=85, mode="probs", guard=1e-9, pair=False, glu=True, deep=False, chunks=2,
               act="silu", router_bias=False, post=False, inner=True),
    "L3": dict(name="ffn3", E=6, F=64, mode="both", guard=0.0, pair=True, glu=False, deep=True, chunks=1,
               act="relu", router_bias=True, post=False, inner=False),
}


def unit_rows(cfg):
    import numpy as np
    from concourse import mybir as mb
    units = cfg["E"] // 2 if cfg["pair"] else cfg["E"]
    un, row = np.arange(units)[:, None], np.arange(128)[None, :]
    expert = 2 * un + row // 64 if cfg["pair"] else un + 0 * row
    r = np.arange(128)[:, None, None]
    hit = (r % cfg["E"] == expert[None]) & (r < 3 * cfg["E"])
    return hit.astype(np.float32).astype(mb.dt.np(mb.dt.bfloat16))


def ffn_weights(I, L):
    return dict(expert_weights(I, L), **({} if FFN[L]["glu"] else {"sel": unit_rows(FFN[L])}))


def expert_weights(I, L):
    import numpy as np
    p = L + "_ffn_"
    cat = np.concatenate
    if L == "L0":
        w1 = cat([I[p + "w1"], I[p + "b1"][:, None]], 1).transpose(1, 0, 2)
        w2 = I[p + "w2"].reshape(4, 128, 64).transpose(1, 0, 2)
        return dict(w1=w1.reshape(65, 4, 128), w2=w2, b2=I[p + "b2"], rw=I[p + "router_w"].T)
    if L == "L1":
        w1 = cat([I[p + "w1"], I[p + "b1"][:, None]], 1).transpose(1, 0, 2)
        return dict(w1=w1, w2=I[p + "w2"].transpose(1, 0, 2), b2=I[p + "b2"],
                    rw=cat([I[p + "gate_w"], I[p + "gate_b"][None]]), gamma=I[p + "gamma"], beta=I[p + "beta"])
    if L == "L2":
        f = lambda n: I[p + n].transpose(2, 0, 1).reshape(64, 16, 85)
        w2 = I[p + "w2"].transpose(0, 2, 1).reshape(16, 85, 64).transpose(1, 0, 2)
        return dict(w1=f("w1"), w3=f("w3"), w2=w2, rw=I[p + "router_w"].T, ln=I[p + "ln2_w"])
    w1 = cat([I[p + "expert_w1"], I[p + "expert_b1"][:, None]], 1).transpose(1, 0, 2)
    return dict(w1=w1.reshape(65, 3, 128), w2=I[p + "expert_w3"].reshape(3, 128, 64).transpose(1, 0, 2),
                b2=I[p + "expert_b3"], rw1=cat([I[p + "router_w1"], I[p + "router_b1"][None]]),
                rw=cat([I[p + "router_w2"], I[p + "router_b2"][None]]),
                wm=I[p + "expert_w2"].reshape(3, 2, 64, 64).transpose(1, 2, 0, 3),
                bm=I[p + "expert_b2"].reshape(3, 128).T)



def linear_attention_stage(nc, k, h_in, h_out, w):
    SH = [128, NT, D]
    HEADS, HD = 8, 8
    GR = [128, NT * HEADS, HD]
    last = S % 128
    with ExitStack() as ctx:
        def sb(name, shape, dt=F32):
            return ctx.enter_context(nc.sbuf_tensor("l_" + name, shape, dt))

        sg = Signals(nc, ctx, "lin", "w_in x_in dve_step var_ready std_ready u_ready uT_done uT_copied kv_ready kv_done kvm_ready "
                              "y_done out_ready store_done")
        x, xc, sq, u, kk, vv, y = (sb(n, SH) for n in ("x", "xc", "sq", "u", "kk", "vv", "y"))
        stat, gst = sb("stat", [128, 4, NT]), sb("gst", [128, 4, NT * HEADS])
        uT = sb("uT", [D, NT * 128])
        kvm = sb("kvm", [D, D])
        blk = sb("blk", [D, D])
        wts = sb("wts", [128, 4, D])
        psT = ctx.enter_context(nc.psum_tensor("l_psT", [128, 3 * 512], F32))
        psY = ctx.enter_context(nc.psum_tensor("l_psY", [128, 2 * 512], F32))
        psK = ctx.enter_context(nc.psum_tensor("l_psK", [128, 512], F32))
        with nc.Block() as block:
            @block.sync
            def _(sp):
                for n, name in enumerate(("kw", "kb", "vw", "vb")):
                    sp.dma_start(wts[:, n, :], w[name].partition_broadcast(128)).then_inc(sg["w_in"], 16)
                sp.dma_start(blk[:], w["blk"]).then_inc(sg["w_in"], 16)
                sp.wait_ge(sg["w_in"], 80)
        sg.end_turn()
        with nc.Fori(0, B) as b:
            with nc.Block() as block:
                @block.sync
                def _(sp):
                    sp.dma_start(x[:], h_in[ds(b * S, NT * 128), :].rearrange("(n p) d -> p n d", p=128)) \
                        .then_inc(sg["x_in"], 16)
                    sp.wait_ge(sg["out_ready"], 1)
                    sp.dma_start(h_out[ds(b * S, S - last), :].rearrange("(n p) d -> p n d", p=128), y[:, 0:NT - 1]) \
                        .then_inc(sg["store_done"], 16)
                    sp.dma_start(h_out[ds(b * S + S - last, last), :], y[0:last, NT - 1]).then_inc(sg["store_done"], 16)
                    sp.wait_ge(sg["store_done"], 32)

                @block.vector
                def _(dve):
                    link = Chain(dve, sg["dve_step"])
                    g3 = lambda t: t[:].rearrange("p n (h d) -> p (n h) d", d=HD)
                    dve.wait_ge(sg["x_in"], 16)
                    dve_center(nc, link, x[:], xc[:], sq[:], stat, SH).then_inc(sg["var_ready"], 1)
                    dve.wait_ge(sg["std_ready"], 1)
                    dve_scale_rows(nc, link, u[:], xc[:], stat, SH).then_inc(sg["u_ready"], 1)
                    dve.wait_ge(sg["u_ready"], 1)
                    link(nc.vector.tensor_reduce(gst[:, 0], g3(u), AX, ALU.add))
                    link(nc.vector.tensor_scalar(gst[:, 0], gst[:, 0], -1.0 / HD, None, ALU.mult))
                    link(nc.vector.tensor_tensor(g3(xc), g3(u), per_row(gst[:, 0], GR), ALU.add))
                    link(nc.vector.tensor_tensor(sq[:], xc[:], xc[:], ALU.mult))
                    nc.vector.tensor_reduce(gst[:, 1], g3(sq), AX, ALU.add).then_inc(sg["var_ready"], 1)
                    dve.wait_ge(sg["std_ready"], 2)
                    link(nc.vector.tensor_scalar(gst[:, 2], gst[:, 2], LN_EPS, None, ALU.add))
                    link(dve_scale_rows(nc, link, g3(sq), g3(xc), gst, GR))
                    for out, i in ((kk, 0), (vv, 2)):
                        link(nc.vector.tensor_tensor(out[:], sq[:], wts[:, i:i + 1, :].to_broadcast(SH), ALU.mult))
                        nc.vector.tensor_tensor(out[:], out[:], wts[:, i + 1:i + 2, :].to_broadcast(SH), ALU.add) \
                            .then_inc(sg["kv_ready"], 1)
                    dve.wait_ge(sg["kv_done"], 1)
                    nc.vector.tensor_tensor(kvm[:], psK[0:D, 0:D], blk[:], ALU.mult).then_inc(sg["kvm_ready"], 1)
                    link(nc.vector.tensor_tensor(xc[:], u[:], x[:], ALU.add))
                    dve.wait_ge(sg["y_done"], 1)
                    nc.vector.tensor_tensor(y[:], psY[:, 0:NT * D].rearrange("p (n d) -> p n d", d=D), xc[:], ALU.add) \
                        .then_inc(sg["out_ready"], 1)

                @block.scalar
                def _(act):
                    act.wait_ge(sg["var_ready"], 1)
                    act_std(nc, stat, k["eps5"][:]).then_inc(sg["std_ready"], 1)
                    act.wait_ge(sg["uT_done"], 1)
                    nc.scalar.copy(uT[:], psT[0:D, 0:NT * 128]).then_inc(sg["uT_copied"], 1)
                    act.wait_ge(sg["var_ready"], 2)
                    nc.scalar.activation(gst[:, 2], gst[:, 1], ACT.Sqrt, bias=k["zero"][:], scale=1.0 / (HD - 1)) \
                        .then_inc(sg["std_ready"], 1)

                @block.tensor
                def _(pe):
                    pe.wait_ge(sg["u_ready"], 1)
                    for n in range(NT):
                        ins = nc.tensor.transpose(psT[0:D, 128 * n:128 * n + 128], u[:, n, :], k["ident"][:])
                    ins.then_inc(sg["uT_done"], 1)
                    pe.wait_ge(sg["kv_ready"], 2)
                    for n in range(NT):
                        m = min(128, S - 128 * n)
                        ins = nc.tensor.matmul(psK[0:D, 0:D], kk[0:m, n, :], vv[0:m, n, :], start=(n == 0),
                                               stop=(n == NT - 1))
                    ins.then_inc(sg["kv_done"], 1)
                    pe.wait_ge(sg["uT_copied"], 1)
                    pe.wait_ge(sg["kvm_ready"], 1)
                    for n in range(NT):
                        ins = nc.tensor.matmul(psY[:, D * n:D * n + D], uT[:, 128 * n:128 * n + 128], kvm[:],
                                               start=True, stop=True)
                    ins.then_inc(sg["y_done"], 1)
            sg.end_turn()



def text_stage(nc, k, h_out, w):
    EW = 75
    with ExitStack() as ctx:
        def sb(name, shape, dt=F32):
            return ctx.enter_context(nc.sbuf_tensor("t_" + name, shape, dt))

        sg = Signals(nc, ctx, "txt", "w_in tok_in preset dve_step eT_done eT_copied p_done p_copied shifted exp_ready out_ready "
                              "store_done")
        rows_in = nc.alloc_semaphore("embeddings_gathered")
        tok = sb("tok", [128, B], I32)
        e = sb("e", [128, 2, B, EW])
        eT = sb("eT", [EW + 1, 2, B * 128])
        wt = sb("wt", [EW + 1, 2, D])
        wa = sb("wa", [128, D])
        ba = sb("ba", [128, 1])
        p, q = sb("p", [128, 2 * B, D]), sb("q", [128, 2 * B, D])
        lg = sb("lg", [128, 4, 2 * B])
        psE = ctx.enter_context(nc.psum_tensor("t_psE", [128, 2, 1024], F32))
        psP = ctx.enter_context(nc.psum_tensor("t_psP", [128, 1024], F32))
        with nc.Block() as block:
            @block.sync
            def _(sp):
                sp.dma_start(tok[:], w["tokens"]).then_inc(sg["tok_in"], 16)
                sp.dma_start(wt[:], w["wt"]).then_inc(sg["w_in"], 16)
                sp.dma_start(wa[:], w["wa"].partition_broadcast(128)).then_inc(sg["w_in"], 16)
                sp.dma_start(ba[:], w["ba"].partition_broadcast(128)).then_inc(sg["w_in"], 16)
                sp.wait_ge(sg["out_ready"], 1)
                for b in range(B):
                    sp.dma_start(h_out[b * S + VIS:(b + 1) * S, :], p[:, b, :]).then_inc(sg["store_done"], 16)
                sp.wait_ge(sg["store_done"], 16 * B)

            @block.gpsimd
            def _(pool):
                pool.wait_ge(sg["tok_in"], 16)
                for i, table in enumerate((w["E0"], w["E1"])):
                    for b in range(B):
                        pool.indirect_dma_start(
                            out=e[:, i, b, :], out_offset=None, in_=table,
                            in_offset=bass.IndirectOffsetOnAxis(ap=tok[:, b:b + 1].bitcast(U32), axis=0)) \
                            .then_inc(rows_in, 16)
                pool.wait_ge(rows_in, 32 * B)

            @block.tensor
            def _(pe):
                pe.wait_ge(rows_in, 32 * B)
                for i in range(2):
                    for b in range(B):
                        ins = nc.tensor.transpose(psE[0:EW, i, 128 * b:128 * b + 128], e[:, i, b, :], k["ident"][:])
                    ins.then_inc(sg["eT_done"], 1)
                pe.wait_ge(sg["w_in"], 48)
                for i in range(2):
                    pe.wait_ge(sg["eT_copied"], i + 1)
                    for b in range(B):
                        c = D * (B * i + b)
                        ins = nc.tensor.matmul(psP[:, c:c + D], eT[:, i, 128 * b:128 * b + 128], wt[:, i, :],
                                               start=True, stop=True)
                ins.then_inc(sg["p_done"], 1)

            @block.scalar
            def _(act):
                act.wait_ge(sg["preset"], 1)
                for i in range(2):
                    act.wait_ge(sg["eT_done"], i + 1)
                    nc.scalar.copy(eT[0:EW, i, :], psE[0:EW, i, :]).then_inc(sg["eT_copied"], 1)
                act.wait_ge(sg["shifted"], 1)
                nc.scalar.activation(lg[:, 2], lg[:, 1], ACT.Exp).then_inc(sg["exp_ready"], 1)

            @block.vector
            def _(dve):
                link = Chain(dve, sg["dve_step"])
                nc.vector.memset(eT[:], 1.0).then_inc(sg["preset"], 1)
                dve.wait_ge(sg["p_done"], 1)
                dve.wait_ge(sg["w_in"], 48)
                SH = [128, 2 * B, D]
                link(nc.vector.tensor_copy(p[:], psP[:, :].rearrange("p (n d) -> p n d", d=D)))
                link(nc.vector.tensor_tensor(q[:], p[:], wa[:].unsqueeze(1).to_broadcast(SH), ALU.mult))
                link(nc.vector.tensor_reduce(lg[:, 0], q[:], AX, ALU.add))
                link(nc.vector.tensor_scalar(lg[:, 0], lg[:, 0], ba[:, 0:1], None, ALU.add))
                link(nc.vector.tensor_tensor(lg[:, 3, 0:B], lg[:, 0, 0:B], lg[:, 0, B:2 * B], ALU.max))
                nc.vector.tensor_tensor(lg[:, 1, 0:B], lg[:, 0, 0:B], lg[:, 3, 0:B], ALU.subtract)
                nc.vector.tensor_tensor(lg[:, 1, B:2 * B], lg[:, 0, B:2 * B], lg[:, 3, 0:B], ALU.subtract) \
                    .then_inc(sg["shifted"], 1)
                dve.wait_ge(sg["exp_ready"], 1)
                link(nc.vector.tensor_tensor(lg[:, 0, 0:B], lg[:, 2, 0:B], lg[:, 2, B:2 * B], ALU.add))
                link(nc.vector.reciprocal(lg[:, 0, B:2 * B], lg[:, 0, 0:B]))
                nc.vector.tensor_tensor(lg[:, 3, 0:B], lg[:, 2, 0:B], lg[:, 0, B:2 * B], ALU.mult)
                link(nc.vector.tensor_tensor(lg[:, 3, B:2 * B], lg[:, 2, B:2 * B], lg[:, 0, B:2 * B], ALU.mult))
                link(nc.vector.tensor_tensor(q[:], p[:], per_row(lg[:, 3], SH), ALU.mult))
                nc.vector.tensor_tensor(p[:, 0:B], q[:, 0:B], q[:, B:2 * B], ALU.add).then_inc(sg["out_ready"], 1)
        sg.end_turn()



HW = 96
PX = HW * HW
HALF_PX = PX // 2
CH = 9
VC = 128
KS, STRIDE = 8, 3
GI = 4
PT = GI * GRID
TILES = (B // GI) * GRID
BAND = STRIDE * HW
GRP = 4


def similarity_maps(nc, k, ctx, wn, x_d, sim_d, best_d, w):
    def sb(name, shape, dt=F32):
        return ctx.enter_context(nc.sbuf_tensor("s_" + name, shape, dt))

    sg = Signals(nc, ctx, "sim", "w_in x_in wsq_ready wn_done wstd_ready dve_step wn_ready sq_ready norm_done std_ready inv_ready spread_done xn_ready "
                          "map_done map_copied map_stored px_done px_taken best_ready")
    ROUNDS = -(-CH // 4)
    x = sb("x", [128, HALF_PX])
    sq = sb("sq", [128, HALF_PX])
    xn = sb("xn", [128, HALF_PX])
    wz = sb("wz", [128, 2, VC])
    maps = sb("maps", [128, 2, HALF_PX])
    best = sb("best", [128, 2, 36])
    halves = sb("halves", [128, 128])
    half_sums = sb("half_sums", [128, 32])
    half_rows = sb("half_rows", [128, 4, 128])
    std = sb("std", [128, ROUNDS, 512])
    cw = sb("cw", [128, VC])
    cq = sb("cq", [128, VC])
    PN = ctx.enter_context(nc.psum_tensor("s_PN", [128, 2, 512], F32))
    PM = ctx.enter_context(nc.psum_tensor("s_PM", [128, 3, 512], F32))
    PB = ctx.enter_context(nc.psum_tensor("s_PB", [128, 3, 512], F32))
    with nc.Block() as block:
        @block.sync
        def _(sp):
            sp.dma_start(cw[0:64, :], w["conv_wT"]).then_inc(sg["w_in"], 16)
            sp.dma_start(cw[64:128, :], w["conv_wT"]).then_inc(sg["w_in"], 16)
            sp.dma_start(halves[:], w["halves"]).then_inc(sg["w_in"], 16)
            sp.dma_start(half_sums[:], w["half_sums"]).then_inc(sg["w_in"], 16)
            sp.dma_start(half_rows[:], w["half_rows"]).then_inc(sg["w_in"], 16)

        @block.vector
        def _(dve):
            link = Chain(dve, sg["dve_step"])
            dve.wait_ge(sg["w_in"], 80)
            nc.vector.tensor_tensor(cq[:], cw[:], cw[:], ALU.mult).then_inc(sg["wsq_ready"], 1)
            dve.wait_ge(sg["wstd_ready"], 1)
            link(nc.vector.reciprocal(cq[:], cq[:]))
            link(nc.vector.tensor_tensor(wn[:], cw[:], cq[:], ALU.mult))
            link(nc.vector.memset(wz[:], 0.0))
            for hf in range(2):
                r = slice(64 * hf, 64 * hf + 64)
                link(nc.vector.tensor_copy(wz[r, hf, :], wn[r, :]))

        @block.tensor
        def _(pe):
            pe.wait_ge(sg["w_in"], 80)
            pe.wait_ge(sg["wsq_ready"], 1)
            nc.tensor.matmul(PN[:, 0, 0:VC], halves[:], cq[:], start=True, stop=True).then_inc(sg["wn_done"], 1)

        @block.scalar
        def _(act):
            act.wait_ge(sg["wn_done"], 1)
            nc.scalar.activation(cq[:], PN[:, 0, 0:VC], ACT.Sqrt).then_inc(sg["wstd_ready"], 1)
    sg.end_turn()
    cols = lambda c: slice(512 * c, 512 * c + 512)
    with nc.Fori(0, B) as b:
        with nc.Block() as block:
            @block.sync
            def _(sp):
                for hf in range(2):
                    sp.dma_start(x[64 * hf:64 * hf + 64, :], x_d[ds(b, 1), :, HALF_PX * hf:HALF_PX * hf + HALF_PX]
                                 .rearrange("o c t -> (o c) t")).then_inc(sg["x_in"], 16)
                for hf in range(2):
                    for z, (c0, c1) in enumerate(((0, 3), (3, 6), (6, 9))):
                        sp.wait_ge(sg["map_copied"], CH * hf + c1)
                        sp.dma_start(sim_d[ds(b, 1), :, HALF_PX * hf + 512 * c0:HALF_PX * hf + 512 * c1]
                                     .rearrange("o v t -> (o v) t"), maps[:, hf, 512 * c0:512 * c1]) \
                            .then_inc(sg["map_stored"], 16)
                sp.wait_ge(sg["best_ready"], 1)
                sp.dma_start(best_d[ds(b, 1), :].rearrange("o (h p t) -> p (o h) t", h=2, p=128), best[:]) \
                    .then_inc(sg["map_stored"], 16)
                sp.wait_ge(sg["map_stored"], 7 * 16)

            @block.scalar
            def _(act):
                act.wait_ge(sg["x_in"], 32)
                for c in range(CH):
                    nc.scalar.activation(sq[:, cols(c)], x[:, cols(c)], ACT.Square).then_inc(sg["sq_ready"], 1)
                for r in range(ROUNDS):
                    act.wait_ge(sg["norm_done"], r + 1)
                    nc.scalar.activation(std[:, r, :], PN[:, r % 2, :], ACT.Sqrt).then_inc(sg["std_ready"], 1)
                for z in range(2 * CH):
                    act.wait_ge(sg["map_done"], z + 1)
                    nc.scalar.copy(maps[:, z // CH, cols(z % CH)], PM[:, z % 3, :]).then_inc(sg["map_copied"], 1)

            @block.tensor
            def _(pe):
                for r in range(ROUNDS):
                    if r >= 2:
                        pe.wait_ge(sg["std_ready"], r - 1)
                    for c in range(4 * r, min(4 * r + 4, CH)):
                        pe.wait_ge(sg["sq_ready"], c + 1)
                        q = 32 * (c % 4)
                        ins = nc.tensor.matmul(PN[q:q + 32, r % 2, :], half_sums[:], sq[:, cols(c)], start=True, stop=True)
                    ins.then_inc(sg["norm_done"], 1)
                for c in range(CH):
                    pe.wait_ge(sg["inv_ready"], c // 4 + 1)
                    if c >= 3:
                        pe.wait_ge(sg["xn_ready"], c - 2)
                    nc.tensor.matmul(PB[:, c % 3, :], half_rows[:, c % 4, :], std[:, c // 4, :], start=True, stop=True) \
                        .then_inc(sg["spread_done"], 1)
                for hf in range(2):
                    for c in range(CH):
                        z = CH * hf + c
                        pe.wait_ge(sg["xn_ready"], c + 1)
                        if z >= 3:
                            pe.wait_ge(sg["map_copied"], z - 2)
                        nc.tensor.matmul(PM[:, z % 3, :], wz[:, hf, :], xn[:, cols(c)], start=True, stop=True) \
                            .then_inc(sg["map_done"], 1)
                pe.wait_ge(sg["xn_ready"], CH)
                xs = xn[:].rearrange("c (p t) -> c p t", t=36)
                for z in range(18):
                    if z >= 3:
                        pe.wait_ge(sg["px_taken"], z - 2)
                    for j in range(2):
                        ins = nc.tensor.matmul(PB[:, z % 3, 256 * j:256 * j + 256], xs[:, :, 2 * z + j],
                                               wz[:].rearrange("c h v -> c (h v)"), start=True, stop=True)
                    ins.then_inc(sg["px_done"], 1)

            @block.vector
            def _(dve):
                for r in range(ROUNDS):
                    dve.wait_ge(sg["std_ready"], r + 1)
                    nc.vector.reciprocal(std[:, r, :], std[:, r, :]).then_inc(sg["inv_ready"], 1)
                for c in range(CH):
                    dve.wait_ge(sg["spread_done"], c + 1)
                    nc.vector.tensor_tensor(xn[:, cols(c)], x[:, cols(c)], PB[:, c % 3, :], ALU.mult) \
                        .then_inc(sg["xn_ready"], 1)
                for z in range(18):
                    dve.wait_ge(sg["px_done"], z + 1)
                    nc.vector.tensor_reduce(best[:, :, 2 * z:2 * z + 2].rearrange("p h j -> p j h"),
                                            PB[:, z % 3, :].rearrange("p (j h v) -> p j h v", h=2, v=128), AX, ALU.max) \
                        .then_inc(sg["px_taken"], 1)
                dve.wait_ge(sg["px_taken"], 18)
                nc.vector.tensor_copy(best[0:1, 0, 0:1], best[0:1, 0, 0:1]).then_inc(sg["best_ready"], 1)
        sg.end_turn()


def visual_stage(nc, k, h_out, w):
    sim_d = nc.dram_tensor("similarities", [B, VC, PX], F32).ap()
    best_d = nc.dram_tensor("best_of_pixel", [B, PX], F32).ap()
    with ExitStack() as ctx:
        def sb(c, name, shape, dt=F32):
            return c.enter_context(nc.sbuf_tensor("v_" + name, shape, dt))

        wn = sb(ctx, "wn", [128, VC])
        with ExitStack() as c2:
            similarity_maps(nc, k, c2, wn, w["x"], sim_d, best_d, w)
        pix_in = nc.alloc_semaphore("pixels_gathered")
        con_in = nc.alloc_semaphore("concepts_gathered")
        RING = 8
        band_in = [nc.alloc_semaphore(f"bands_gathered_{i}") for i in range(RING)]
        sg = Signals(nc, ctx, "vis", "w_in bands_in dve_step win_ready top_ready pix_ready sq_ready std_ready n_ready nT_done "
                              "nT_copied sv_done sv_copied concept_ready band_used mix_ready sims_ready inT_done inT_copied "
                              "h_done h_biased h_ready o_done o_ready store_done")
        xs = sb(ctx, "xs", [PT, TILES, D])
        ms = sb(ctx, "ms", [PT, TILES])
        vrow = sb(ctx, "vrow", [PT, TILES], U32)
        srow = sb(ctx, "srow", [PT, 3, TILES], U32)
        base = sb(ctx, "base", [PT, 2, TILES])
        with ExitStack() as c2:
            band = sb(c2, "band", [PT, 2, 3 * BAND])
            win = sb(c2, "win", [PT, TILES, KS * KS])
            m8 = sb(c2, "m8", [PT, TILES, 8])
            i8 = sb(c2, "i8", [PT, TILES, 8], U32)
            pos = sb(c2, "pos", [PT, 3, TILES], U32)
            posf = sb(c2, "posf", [PT, 2, TILES])
            window = lambda t: band[:, t // GRID, :].rearrange("p (r c) -> p r c", c=HW)[
                :, 0:KS, STRIDE * (t % GRID):STRIDE * (t % GRID) + KS]
            with nc.Block() as block:
                @block.sync
                def _(sp):
                    sp.dma_start(base[:], w["patch_base"]).then_inc(sg["w_in"], 16)
                    src = best_d.rearrange("b (q t) -> b q t", t=BAND)
                    for b in range(B):
                        p0 = GRID * (b % GI)
                        for z in range(3):
                            sp.dma_start(band[p0:p0 + GRID, b // GI, BAND * z:BAND * z + BAND], src[b, z:z + GRID, :]) \
                                .then_inc(sg["bands_in"], 16)

                @block.scalar
                def _(act):
                    act.wait_ge(sg["bands_in"], 16 * 24)
                    for t in range(TILES):
                        nc.scalar.copy(win[:, t, :].rearrange("p (r c) -> p r c", c=KS), window(t)) \
                            .then_inc(sg["win_ready"], 1)

                @block.vector
                def _(dve):
                    link = Chain(dve, sg["dve_step"])
                    dve.wait_ge(sg["w_in"], 16)
                    dve.wait_ge(sg["win_ready"], TILES)
                    for t in range(TILES):
                        ins = nc.vector.max(m8[:, t, :], win[:, t, :])
                    link(ins)
                    for t in range(TILES):
                        ins = nc.vector.max_index(i8[:, t, :], m8[:, t, :], win[:, t, :])
                    link(ins)
                    link(nc.vector.tensor_copy(pos[:, 2, :], i8[:, :, 0]))
                    nc.vector.tensor_scalar(pos[:, 0, :], pos[:, 2, :], 3, None, ALU.logical_shift_right)
                    link(nc.vector.tensor_scalar(pos[:, 1, :], pos[:, 2, :], 7, None, ALU.bitwise_and))
                    link(nc.vector.tensor_copy(posf[:], pos[:, 0:2, :]))
                    link(nc.vector.scalar_tensor_tensor(posf[:, 0, :], posf[:, 0, :], float(HW), posf[:, 1, :],
                                                        ALU.mult, ALU.add))
                    nc.vector.tensor_tensor(pos[:, 0, :], posf[:, 0, :], base[:, 0, :], ALU.add) \
                        .then_inc(sg["pix_ready"], 1)

                @block.gpsimd
                def _(pool):
                    pool.wait_ge(sg["pix_ready"], 1)
                    for t in range(TILES):
                        pool.indirect_dma_start(out=xs[:, t, :], out_offset=None, in_=w["x_px"],
                                                in_offset=bass.IndirectOffsetOnAxis(ap=pos[:, 0, t:t + 1], axis=0)) \
                            .then_inc(pix_in, 16)
                    pool.wait_ge(pix_in, 16 * TILES)
            sg.end_turn()
        groups = range(TILES // GRP)
        with ExitStack() as c2:
            sq = sb(c2, "sq", [PT, TILES, D])
            st = sb(c2, "st", [PT, 4, TILES])
            nT = sb(c2, "nT", [D, 2, GRP * 128])
            sv = sb(c2, "sv", [PT, 2, GRP, VC])
            m8 = sb(c2, "n8", [PT, TILES, 8])
            i8 = sb(c2, "j8", [PT, TILES, 8], U32)
            vf = sb(c2, "vf", [PT, 2, TILES])
            PT_ = c2.enter_context(nc.psum_tensor("v_PT", [128, 2, 512], F32))
            PV = c2.enter_context(nc.psum_tensor("v_PV", [128, 2, 512], F32))
            with nc.Block() as block:
                @block.vector
                def _(dve):
                    link = Chain(dve, sg["dve_step"])
                    SH = [PT, TILES, D]
                    link(nc.vector.tensor_tensor(sq[:], xs[:], xs[:], ALU.mult))
                    nc.vector.tensor_reduce(st[:, 1], sq[:], AX, ALU.add).then_inc(sg["sq_ready"], 1)
                    dve.wait_ge(sg["std_ready"], 1)
                    dve_scale_rows(nc, link, sq[:], xs[:], st, SH).then_inc(sg["n_ready"], 1)
                    for g in groups:
                        dve.wait_ge(sg["sv_copied"], g + 1)
                        for j in range(GRP):
                            ins = nc.vector.max(m8[:, GRP * g + j, :], sv[:, g % 2, j, :])
                        link(ins)
                        for j in range(GRP):
                            ins = nc.vector.max_index(i8[:, GRP * g + j, :], m8[:, GRP * g + j, :], sv[:, g % 2, j, :])
                        ins.then_inc(sg["top_ready"], 1)
                    dve.wait_ge(sg["top_ready"], len(groups))
                    nc.vector.tensor_copy(vrow[:], i8[:, :, 0]).then_inc(sg["concept_ready"], 1)
                    link(nc.vector.tensor_copy(ms[:], m8[:, :, 0]))
                    link(nc.vector.tensor_copy(vf[:, 0], i8[:, :, 0]))
                    link(nc.vector.scalar_tensor_tensor(vf[:, 1], vf[:, 0], float(PX // BAND), base[:, 1, :],
                                                        ALU.mult, ALU.add))
                    for z in range(3):
                        ins = nc.vector.tensor_scalar(srow[:, z, :], vf[:, 1], float(z), None, ALU.add)
                    link(ins)

                @block.scalar
                def _(act):
                    act.wait_ge(sg["sq_ready"], 1)
                    nc.scalar.activation(st[:, 2], st[:, 1], ACT.Sqrt).then_inc(sg["std_ready"], 1)
                    for g in groups:
                        act.wait_ge(sg["nT_done"], g + 1)
                        nc.scalar.copy(nT[:, g % 2, 0:GRP * PT], PT_[0:D, g % 2, 0:GRP * PT]).then_inc(sg["nT_copied"], 1)
                        act.wait_ge(sg["sv_done"], g + 1)
                        if g >= 2:
                            act.wait_ge(sg["top_ready"], g - 1)
                        nc.scalar.copy(sv[:, g % 2].rearrange("p j v -> p (j v)"), PV[0:PT, g % 2, :]) \
                            .then_inc(sg["sv_copied"], 1)

                @block.tensor
                def _(pe):
                    pe.wait_ge(sg["n_ready"], 1)
                    for g in groups:
                        if g >= 2:
                            pe.wait_ge(sg["nT_copied"], g - 1)
                            pe.wait_ge(sg["sv_copied"], g - 1)
                        for j in range(GRP):
                            ins = nc.tensor.transpose(PT_[0:D, g % 2, PT * j:PT * j + PT], sq[:, GRP * g + j, :],
                                                      k["ident"][0:PT, 0:PT])
                        ins.then_inc(sg["nT_done"], 1)
                        pe.wait_ge(sg["nT_copied"], g + 1)
                        for j in range(GRP):
                            ins = nc.tensor.matmul(PV[0:PT, g % 2, VC * j:VC * j + VC], nT[:, g % 2, PT * j:PT * j + PT],
                                                   wn[0:D, :], start=True, stop=True)
                        ins.then_inc(sg["sv_done"], 1)
            sg.end_turn()
        with ExitStack() as c2:
            ws = sb(c2, "ws", [PT, TILES, D])
            inp = sb(c2, "inp", [PT, TILES, 2 * D])
            bands = sb(c2, "bands", [PT, RING, 3 * BAND])
            om = sb(c2, "om", [PT, TILES])
            inT = sb(c2, "inT", [2 * D, 2, GRP * PT])
            hb = sb(c2, "hb", [96, 2, 2, GRP * PT])
            ha = sb(c2, "ha", [96, 2, 2, GRP * PT])
            w1 = sb(c2, "w1", [2 * D, 192])
            b1 = sb(c2, "b1", [96, 2])
            w2 = sb(c2, "w2", [96, 2, D])
            b2 = sb(c2, "b2", [1, D])
            one = sb(c2, "one", [1, PT])
            PI = c2.enter_context(nc.psum_tensor("v_PI", [128, 2, 512], F32))
            PH = c2.enter_context(nc.psum_tensor("v_PH", [128, 4, 512], F32))
            PO = c2.enter_context(nc.psum_tensor("v_PO", [128, 2, 512], F32))
            with nc.Block() as block:
                @block.sync
                def _(sp):
                    for dst, src in ((w1, "tW1"), (b1, "tb1"), (w2, "tW2"), (b2, "tb2"), (one, "one")):
                        sp.dma_start(dst[:], w[src]).then_inc(sg["w_in"], 16)
                    sp.wait_ge(sg["o_ready"], len(groups))
                    for b in range(B):
                        p0, t0 = GRID * (b % GI), GRID * (b // GI)
                        sp.dma_start(h_out[b * S:b * S + VIS, :].rearrange("(q t) d -> q t d", t=GRID),
                                     xs[p0:p0 + GRID, t0:t0 + GRID, :]).then_inc(sg["store_done"], 16)
                    sp.wait_ge(sg["store_done"], 16 * B)

                @block.gpsimd
                def _(pool):
                    for t in range(TILES):
                        pool.indirect_dma_start(out=ws[:, t, :], out_offset=None, in_=w["conv_w"],
                                                in_offset=bass.IndirectOffsetOnAxis(ap=vrow[:, t:t + 1], axis=0)) \
                            .then_inc(con_in, 16)
                    for t in range(TILES):
                        if t >= RING:
                            pool.wait_ge(sg["band_used"], t - RING + 1)
                        for z in range(3):
                            pool.indirect_dma_start(
                                out=bands[:, t % RING, BAND * z:BAND * z + BAND], out_offset=None, in_=sim_d.rearrange("b v (q t) -> (b v q) t", t=BAND),
                                in_offset=bass.IndirectOffsetOnAxis(ap=srow[:, z, t:t + 1], axis=0)) \
                                .then_inc(band_in[t % RING], 16)
                    for i in range(RING):
                        pool.wait_ge(band_in[i], 48 * len(range(i, TILES, RING)))

                def leaky(dve, g):
                    dve.wait_ge(sg["h_biased"], 2 * g + 2)
                    if g >= 2:
                        dve.wait_ge(sg["o_done"], g - 1)
                    nc.vector.scalar_tensor_tensor(ha[:, g % 2], hb[:, g % 2], 0.2, hb[:, g % 2], ALU.mult, ALU.max) \
                        .then_inc(sg["h_ready"], 1)

                @block.vector
                def _(dve):
                    link = Chain(dve, sg["dve_step"])
                    SH = [PT, TILES, D]
                    link(nc.vector.tensor_scalar(om[:], ms[:], -1.0, 1.0, ALU.mult, ALU.add))
                    link(nc.vector.tensor_tensor(inp[:, :, 0:D], xs[:], per_row(ms[:], SH), ALU.mult))
                    dve.wait_ge(con_in, 16 * TILES)
                    link(nc.vector.tensor_tensor(ws[:], ws[:], per_row(om[:], SH), ALU.mult))
                    nc.vector.tensor_tensor(inp[:, :, 0:D], inp[:, :, 0:D], ws[:], ALU.add).then_inc(sg["mix_ready"], 1)
                    for t in range(TILES):
                        dve.wait_ge(band_in[t % RING], 48 * (t // RING + 1))
                        nc.vector.tensor_copy(
                            inp[:, t, D:2 * D].rearrange("p (r c) -> p r c", c=KS),
                            bands[:, t % RING, :].rearrange("p (r c) -> p r c", c=HW)[
                                :, 0:KS, STRIDE * (t % GRID):STRIDE * (t % GRID) + KS]).then_inc(sg["band_used"], 1)
                        g = t // GRP
                        if t % GRP == GRP - 1 and g >= 1:
                            leaky(dve, g - 1)
                    leaky(dve, len(groups) - 1)

                def tanh(act, g):
                    act.wait_ge(sg["o_done"], g + 1)
                    act.wait_ge(sg["mix_ready"], 1)
                    nc.scalar.activation(xs[:, GRP * g:GRP * g + GRP, :].rearrange("p j d -> p (j d)"),
                                         PO[0:PT, g % 2, 0:GRP * D], ACT.Tanh).then_inc(sg["o_ready"], 1)

                @block.scalar
                def _(act):
                    act.wait_ge(sg["w_in"], 80)
                    for g in groups:
                        act.wait_ge(sg["inT_done"], g + 1)
                        if g >= 2:
                            act.wait_ge(sg["h_done"], 2 * g - 2)
                        nc.scalar.copy(inT[:, g % 2, :], PI[:, g % 2, 0:GRP * PT]).then_inc(sg["inT_copied"], 1)
                        for z in range(2):
                            act.wait_ge(sg["h_done"], 2 * g + z + 1)
                            if g >= 2:
                                act.wait_ge(sg["h_ready"], g - 1)
                            nc.scalar.activation(hb[:, g % 2, z], PH[0:96, 2 * (g % 2) + z, 0:GRP * PT], ACT.Identity,
                                                 bias=b1[:, z:z + 1]).then_inc(sg["h_biased"], 1)
                        if g >= 1:
                            tanh(act, g - 1)
                    tanh(act, len(groups) - 1)

                @block.tensor
                def _(pe):
                    pe.wait_ge(sg["w_in"], 80)
                    pe.wait_ge(sg["mix_ready"], 1)

                    def second(g):
                        pe.wait_ge(sg["h_ready"], g + 1)
                        if g >= 2:
                            pe.wait_ge(sg["o_ready"], g - 1)
                        for j in range(GRP):
                            o = PO[0:PT, g % 2, D * j:D * j + D]
                            for z in range(2):
                                nc.tensor.matmul(o, ha[:, g % 2, z, PT * j:PT * j + PT], w2[:, z, :], start=(z == 0),
                                                 stop=False)
                            ins = nc.tensor.matmul(o, one[:], b2[:], start=False, stop=True)
                        ins.then_inc(sg["o_done"], 1)

                    for g in groups:
                        pe.wait_ge(sg["band_used"], GRP * g + GRP)
                        if g >= 2:
                            pe.wait_ge(sg["inT_copied"], g - 1)
                        for j in range(GRP):
                            ins = nc.tensor.transpose(PI[:, g % 2, PT * j:PT * j + PT], inp[:, GRP * g + j, :],
                                                      k["ident"][0:PT, 0:PT])
                        ins.then_inc(sg["inT_done"], 1)
                        pe.wait_ge(sg["inT_copied"], g + 1)
                        if g >= 2:
                            pe.wait_ge(sg["h_biased"], 2 * g - 2)
                        for z in range(2):
                            nc.tensor.matmul(PH[0:96, 2 * (g % 2) + z, 0:GRP * PT], w1[:, 96 * z:96 * z + 96],
                                             inT[:, g % 2, :], start=True, stop=True).then_inc(sg["h_done"], 1)
                        if g >= 1:
                            second(g - 1)
                    second(len(groups) - 1)
            sg.end_turn()


def token_constants():
    import numpy as np
    p, t = np.arange(PT)[:, None], np.arange(TILES)[None, :]
    img = t // GRID * GI + p // GRID
    row, col = p % GRID, t % GRID
    first = img * PX + STRIDE * row * HW + STRIDE * col
    bandrow = img * VC * (PX // BAND) + row + 0 * col
    half = np.arange(128) // 64
    blk = np.arange(D) // 8
    return {
        "patch_base": np.ascontiguousarray(np.stack([first, bandrow], 1).astype(np.float32)),
        "halves": (half[:, None] == half[None, :]).astype(np.float32),
        "half_sums": (half[:, None] == np.arange(32)[None, :] % 2).astype(np.float32),
        "half_rows": (np.arange(128)[:, None, None] == 32 * np.arange(4)[None, :, None] + half[None, None, :])
        .astype(np.float32),
        "one": np.ones((1, PT), np.float32),
        "blk": np.where(blk[:, None] == blk[None, :], np.float32(1.0 / S), np.float32(0)).astype(np.float32),
    }



def program(nc, a, out):
    buf = [nc.dram_tensor(f"tokens_{i}", [PAD_ROWS, D], F32).ap() for i in range(2)]
    mid = nc.dram_tensor("tokens_inner", [PAD_ROWS, D], F32).ap()
    sub = lambda pre: {n[len(pre):]: v for n, v in a.items() if n.startswith(pre)}
    with ExitStack() as ctx:
        k = load_constants(nc, ctx, dict(sub("c_"), pads=buf + [mid]))
        visual_stage(nc, k, buf[0], dict(sub("c_"), **sub("tok_")))
        text_stage(nc, k, buf[0], sub("txt_"))
        attention_stage(nc, k, ATT["L0"], buf[0], buf[1], dict(sub("a0_"), own=a["c_own0"]))
        ffn_stage(nc, k, FFN["L0"], buf[1], buf[0], sub("f0_"))
        ones = {"ones": a["c_ones3"]}
        attention_stage(nc, k, ATT["L1"], buf[0], buf[1], dict(sub("a1_"), **ones))
        ffn_stage(nc, k, FFN["L1"], buf[1], buf[0], sub("f1_"))
        attention_stage(nc, k, ATT["L2"], buf[0], buf[1], dict(sub("a2_"), own=a["c_own2"], **ones))
        attention_stage(nc, k, ATT["L2f"], buf[1], None, dict(sub("a3_"), rope=a["c_rope"], **ones), x1_d=mid)
        gated_ffn_stage(nc, k, FFN["L2"], buf[1], buf[0], sub("f2_"), x1_d=mid)
        linear_attention_stage(nc, k, buf[0], buf[1], dict(sub("a4_"), blk=a["c_blk"]))
        ffn_stage(nc, k, FFN["L3"], buf[1], out, sub("f3_"))


def lay_out(I):
    import numpy as np
    cat, st = np.concatenate, np.stack
    x = I["x"]
    a = {"c_" + n: v for n, v in {**constants(), **token_constants()}.items()}
    a.update(
        tok_x=x.reshape(B, D, PX), tok_x_px=x.transpose(0, 2, 3, 1).reshape(-1, D),
        tok_conv_wT=I["L0_tok_conv_w"].T, tok_conv_w=I["L0_tok_conv_w"], tok_tW1=I["L0_tok_W1"].T,
        tok_tb1=I["L0_tok_b1"].reshape(2, 96).T, tok_tW2=I["L0_tok_W2"].T.reshape(2, 96, D).transpose(1, 0, 2),
        tok_tb2=I["L0_tok_b2"][None],
        txt_tokens=I["x_txt"].T, txt_E0=I["L0_txt_E0"], txt_E1=I["L0_txt_E1"],
        txt_wt=st([cat([I[f"L0_txt_W{i}"], I[f"L0_txt_b{i}"][None]]) for i in (0, 1)], 1),
        txt_wa=I["L0_txt_Wa"].reshape(-1), txt_ba=I["L0_txt_ba"],
        a0_wT=I["L0_attn_w_qkv"].T, a0_wo=I["L0_attn_w_proj"].T, a0_qn=I["L0_attn_qn_w"], a0_kn=I["L0_attn_kn_w"],
        a1_wT=cat([cat([I["L1_attn_W" + n] for n in "qkv"], 1), cat([I["L1_attn_b" + n] for n in "qkv"])[None]]),
        a2_wT=I["L2_attn_w_qkv"].T, a2_wo=cat([I["L2_attn_w_proj"].T, I["L2_attn_b_proj"][None]]),
        a2_table=I["L2_attn_rel_table"],
        a2_index=st([I["L2_attn_rel_index"].reshape(WS2, WS2).T, I["L2_attn_rel_index"].reshape(WS2, WS2)]),
        a3_wT=cat([I["L2_ffn_w" + n] for n in "qkv"]).T, a3_wo=I["L2_ffn_wo"].T, a3_ln1=I["L2_ffn_ln1_w"],
        a4_kw=I["L3_attn_kln_weight"].reshape(-1), a4_kb=I["L3_attn_kln_bias"].reshape(-1),
        a4_vw=I["L3_attn_vln_weight"].reshape(-1), a4_vb=I["L3_attn_vln_bias"].reshape(-1))
    for n in range(4):
        a.update({f"f{n}_{m}": v for m, v in ffn_weights(I, f"L{n}").items()})
    return a


def kernel(**inputs):
    import numpy as np
    import concourse.bacc as bacc
    from concourse.bass_utils import run_bass_kernel_spmd

    arrays = {n: np.ascontiguousarray(v) for n, v in lay_out({n: np.asarray(v) for n, v in inputs.items()}).items()}
    nc = bacc.Bacc("TRN2", target_bir_lowering=False, num_devices=1)
    a = {n: nc.dram_tensor("in_" + n, v.shape, mybir.dt.from_np(v.dtype), kind="ExternalInput").ap()
         for n, v in arrays.items()}
    out = nc.dram_tensor("out_tokens", (F_TURNS * FTOK, D), F32, kind="ExternalOutput").ap()
    program(nc, a, out)
    r = run_bass_kernel_spmd(nc, [{"in_" + n: v for n, v in arrays.items()}], core_ids=[0])
    return r.results[0]["out_tokens"][:N_TOK].reshape(B, S, D)
```
